# Optimizing a Trainium2 kernel written in Bass

```python
import numpy as np
import jax
import jax.numpy as jnp

def _softmax(x, axis=-1):
    return jax.nn.softmax(x, axis=axis)

def _gelu(x):
    return jax.nn.gelu(x, approximate=True)

def _silu(x):
    return jax.nn.silu(x)

def _sigmoid(x):
    return jax.nn.sigmoid(x)

def _layernorm(x, axis=-1, eps=1e-05):
    m = jnp.mean(x, axis=axis, keepdims=True)
    v = jnp.var(x, axis=axis, keepdims=True)
    return (x - m) / jnp.sqrt(v + eps)

def _scatter_add(tgt, idx, src, axis=0):
    return tgt.at[idx].add(src)

def _segment_sum(src, seg, n):
    return jax.ops.segment_sum(src, seg, n)
kernel_name = 'mk_decoder_postln_d4_seqx_r8_cb5e9e'

def setup_inputs(seed: int=0):
    np.random.seed(seed)
    _w = jnp.asarray

    def _rec_inputs():
        import jax
        import jax.numpy as jnp
        _rk = jax.random.key(seed)
        x = -0.000125 + 0.9999 * jax.random.normal(jax.random.fold_in(_rk, 1), (32, 128, 128), jnp.float32)
        _lenS = 128 - jax.random.randint(jax.random.fold_in(_rk, 7), (32,), 0, max(1, 128 // 4) + 1, jnp.int32)
        _lenS2 = 77 - jax.random.randint(jax.random.fold_in(_rk, 8), (32,), 0, max(1, 77 // 4) + 1, jnp.int32)
        _ctx_768P = jax.random.normal(jax.random.fold_in(_rk, 11), (32, 16, 96), jnp.float32)
        _ctx_768c = jax.random.dirichlet(jax.random.fold_in(_rk, 511), 0.3 * jnp.ones((16,), jnp.float32), (32, 77))
        _ctx_768t = jnp.einsum('bsk,bkd->bsd', _ctx_768c, _ctx_768P)
        _ctx_768t = _ctx_768t * jax.lax.rsqrt(jnp.mean(jnp.square(_ctx_768t)) + 1e-12) * 0.953939
        ctx_768 = 0.00272024 + 0.999456 * (_ctx_768t + 0.3 * jax.random.normal(jax.random.fold_in(_rk, 611), (32, 77, 96), jnp.float32))
        _validS = jnp.arange(128)[None, :] < _lenS[:, None]
        _validS2 = jnp.arange(77)[None, :] < _lenS2[:, None]
        _causal = jnp.tril(jnp.ones((128, 128), dtype=bool))
        mask_BxS_bf1 = jnp.ones((32, 128), dtype=bool)
        mask_BxS2_bf1 = jnp.ones((32, 77), dtype=bool)
        return (x, ctx_768, mask_BxS_bf1, mask_BxS2_bf1)
    x, ctx_768, mask_BxS_bf1, mask_BxS2_bf1 = _rec_inputs()

    def _L0_attn_setup():
        import jax, jax.numpy as jnp
        import numpy as np
        D_MODEL = 128
        N_QK = 32
        D_QK = 32
        N_OV = 256
        D_OV = 1
        SEQ = 128
        BATCH = 2
        VKV = 16
        ROT_DIM = 32
        ROT_BASE = 10000.0
        SCALE = D_QK ** 0.5

        def _kaiming(k, shape, fan_in):
            return jax.random.normal(k, shape, jnp.float32) * np.sqrt(2.0 / fan_in)

        def _rotary_sin_cos(n_ctx, rd, base):
            pos = jnp.arange(n_ctx, dtype=jnp.float32)
            dim = jnp.arange(rd // 2, dtype=jnp.float32)
            freq = base ** (dim / (rd / 2))
            freq = jnp.concatenate([freq, freq])
            angles = pos[:, None] / freq[None, :]
            return (jnp.sin(angles), jnp.cos(angles))

        def _apply_rotary(x, sin, cos, rd):
            s = x.shape[1]
            x_rot, x_pass = (x[..., :rd], x[..., rd:])
            flip = jnp.concatenate([-x_rot[..., rd // 2:], x_rot[..., :rd // 2]], axis=-1)
            rot = x_rot * cos[None, :s, None, :] + flip * sin[None, :s, None, :]
            return jnp.concatenate([rot, x_pass], axis=-1)
        key = jax.random.key(seed)
        ks = jax.random.split(key, 7)
        return {'resid': jax.random.normal(ks[0], (BATCH, SEQ, D_MODEL), jnp.float32), 'W_Q': _kaiming(ks[1], (N_QK, D_MODEL, D_QK), D_MODEL * D_QK), 'W_K': _kaiming(ks[2], (N_QK, D_MODEL, D_QK), D_MODEL * D_QK), 'W_V': _kaiming(ks[3], (N_OV, D_MODEL, D_OV), D_MODEL * D_OV), 'W_O': _kaiming(ks[4], (N_OV, D_OV, D_MODEL), D_OV * D_MODEL), 'b_Q': jnp.zeros((N_QK, D_QK), jnp.float32), 'b_K': jnp.zeros((N_QK, D_QK), jnp.float32), 'b_V': jnp.zeros((N_OV, D_OV), jnp.float32), 'virtual_k': _kaiming(ks[5], (VKV, N_QK, D_QK), N_QK * D_QK), 'virtual_v': jnp.zeros((VKV, N_OV, D_OV), jnp.float32)}
    _L0_attn_all = _L0_attn_setup()
    _L0_attn_in = {k: v for k, v in _L0_attn_all.items() if k in ('W_Q', 'W_K', 'W_V', 'W_O', 'b_Q', 'b_K', 'b_V', 'virtual_k', 'virtual_v')}
    del _L0_attn_all

    def _L0_xattn_setup():
        import jax, jax.numpy as jnp
        import numpy as np
        QUERY_DIM = 128
        CONTEXT_DIM = 96
        HEADS = 8
        DIM_HEAD = 64
        INNER = HEADS * DIM_HEAD
        key = jax.random.key(seed)
        ks = jax.random.split(key, 7)
        B, S, L = (8, 512, 77)
        x = jax.random.normal(ks[0], (B, S, QUERY_DIM), dtype=jnp.float32)
        context = jax.random.normal(ks[1], (B, L, CONTEXT_DIM), dtype=jnp.float32)
        Wq = jax.random.normal(ks[2], (QUERY_DIM, INNER), dtype=jnp.float32) * QUERY_DIM ** (-0.5)
        Wk = jax.random.normal(ks[3], (CONTEXT_DIM, INNER), dtype=jnp.float32) * CONTEXT_DIM ** (-0.5)
        Wv = jax.random.normal(ks[4], (CONTEXT_DIM, INNER), dtype=jnp.float32) * CONTEXT_DIM ** (-0.5)
        Wo = jax.random.normal(ks[5], (INNER, QUERY_DIM), dtype=jnp.float32) * INNER ** (-0.5)
        bo = jax.random.normal(ks[6], (QUERY_DIM,), dtype=jnp.float32) * 0.01
        return {'x': x, 'context': context, 'Wq': Wq, 'Wk': Wk, 'Wv': Wv, 'Wo': Wo, 'bo': bo}
    _L0_xattn_all = _L0_xattn_setup()
    _L0_xattn_in = {k: v for k, v in _L0_xattn_all.items() if k in ('Wq', 'Wk', 'Wv', 'Wo', 'bo')}
    del _L0_xattn_all

    def _L0_ffn_setup():
        import jax, jax.numpy as jnp
        import numpy as np
        B, S, D = (1, 256, 128)
        I = 256
        E = 8
        K = 2
        LIMIT = 7.0
        ALPHA = 1.702
        EPS = 1e-05

        def _swiglu(h):
            x_glu = jnp.minimum(h[..., ::2], LIMIT)
            x_lin = jnp.clip(h[..., 1::2], -LIMIT, LIMIT)
            return x_glu * jax.nn.sigmoid(ALPHA * x_glu) * (x_lin + 1.0)

        def _moe(t, gate_w, gate_b, mlp1_w, mlp1_b, mlp2_w, mlp2_b):
            T = t.shape[0]
            logits = t @ gate_w + gate_b
            top_v, top_i = jax.lax.top_k(logits, K)
            probs = jax.nn.softmax(top_v, axis=-1)
            w = jnp.zeros((T, E), t.dtype).at[jnp.arange(T)[:, None], top_i].set(probs)

            def body(acc, ew):
                w1, b1, w2, b2, we = ew
                h = _swiglu(t @ w1 + b1)
                y = h @ w2 + b2
                return (acc + we[:, None] * y, None)
            acc0 = jnp.zeros((T, t.shape[1]), t.dtype)
            acc, _ = jax.lax.scan(body, acc0, (mlp1_w, mlp1_b, mlp2_w, mlp2_b, w.T))
            return acc
        key = jax.random.key(seed)
        ks = jax.random.split(key, 4)
        s = 0.02
        return {'x': jax.random.normal(ks[0], (B, S, D), jnp.float32), 'norm_scale': jnp.ones((D,), jnp.float32), 'gate_w': jax.random.normal(ks[1], (D, E), jnp.float32) * s, 'gate_b': jnp.zeros((E,), jnp.float32), 'mlp1_w': jax.random.normal(ks[2], (E, D, 2 * I), jnp.float32) * s, 'mlp1_b': jnp.zeros((E, 2 * I), jnp.float32), 'mlp2_w': jax.random.normal(ks[3], (E, I, D), jnp.float32) * s, 'mlp2_b': jnp.zeros((E, D), jnp.float32)}
    _L0_ffn_all = _L0_ffn_setup()
    _L0_ffn_in = {k: v for k, v in _L0_ffn_all.items() if k in ('norm_scale', 'gate_w', 'gate_b', 'mlp1_w', 'mlp1_b', 'mlp2_w', 'mlp2_b')}
    del _L0_ffn_all

    def _L1_attn_setup():
        import jax, jax.numpy as jnp
        import numpy as np
        B, T, D = (4, 512, 128)
        H = 16
        DK = D // H
        EPS = 1e-06

        def _phi(x):
            return jax.nn.elu(x) + 1.0
        key = jax.random.key(seed)
        ks = jax.random.split(key, 9)
        s = 1.0 / np.sqrt(D)
        return {'x': jax.random.normal(ks[0], (B, T, D), dtype=jnp.float32), 'Wq': jax.random.uniform(ks[1], (D, D), jnp.float32, -s, s), 'bq': jax.random.uniform(ks[2], (D,), jnp.float32, -s, s), 'Wk': jax.random.uniform(ks[3], (D, D), jnp.float32, -s, s), 'bk': jax.random.uniform(ks[4], (D,), jnp.float32, -s, s), 'Wv': jax.random.uniform(ks[5], (D, D), jnp.float32, -s, s), 'bv': jax.random.uniform(ks[6], (D,), jnp.float32, -s, s), 'Wo': jax.random.uniform(ks[7], (D, D), jnp.float32, -s, s), 'bo': jax.random.uniform(ks[8], (D,), jnp.float32, -s, s)}
    _L1_attn_all = _L1_attn_setup()
    _L1_attn_in = {k: v for k, v in _L1_attn_all.items() if k in ('Wq', 'bq', 'Wk', 'bk', 'Wv', 'bv', 'Wo', 'bo')}
    del _L1_attn_all

    def _L1_xattn_setup():
        import jax, jax.numpy as jnp
        import numpy as np
        N_HEADS = 16
        DIMS = 128
        D_CTX = 96
        HEAD = DIMS // N_HEADS
        key = jax.random.key(seed)
        ks = jax.random.split(key, 10)
        s_q = 1.0 / np.sqrt(DIMS)
        s_c = 1.0 / np.sqrt(D_CTX)
        return {'x': jax.random.normal(ks[0], (2, 256, DIMS), jnp.float32), 'context': jax.random.normal(ks[1], (2, 256, D_CTX), jnp.float32), 'w_q': jax.random.normal(ks[2], (DIMS, DIMS), jnp.float32) * s_q, 'b_q': jax.random.normal(ks[3], (DIMS,), jnp.float32) * 0.01, 'w_k': jax.random.normal(ks[4], (D_CTX, DIMS), jnp.float32) * s_c, 'b_k': jax.random.normal(ks[5], (DIMS,), jnp.float32) * 0.01, 'w_v': jax.random.normal(ks[6], (D_CTX, DIMS), jnp.float32) * s_c, 'b_v': jax.random.normal(ks[7], (DIMS,), jnp.float32) * 0.01, 'w_o': jax.random.normal(ks[8], (DIMS, DIMS), jnp.float32) * s_q, 'b_o': jax.random.normal(ks[9], (DIMS,), jnp.float32) * 0.01}
    _L1_xattn_all = _L1_xattn_setup()
    _L1_xattn_in = {k: v for k, v in _L1_xattn_all.items() if k in ('w_q', 'b_q', 'w_k', 'b_k', 'w_v', 'b_v', 'w_o', 'b_o')}
    del _L1_xattn_all

    def _L1_ffn_setup():
        import jax, jax.numpy as jnp
        import numpy as np
        D = 128
        F = 128
        E = 8
        K = 2
        B, T = (2, 256)

        def _moe_forward(x, router_w, w1, w2, shared_gate_up, shared_down, shared_gate_w):
            b, t, d = x.shape
            xf = x.reshape(-1, d)
            n = xf.shape[0]
            logits = xf @ router_w
            probs = jax.nn.softmax(logits, axis=-1)
            topw, topi = jax.lax.top_k(probs, K)
            combine = jnp.zeros((n, E), dtype=probs.dtype).at[jnp.arange(n)[:, None], topi].add(topw)
            h = jax.nn.silu(jnp.einsum('nd,edf->nef', xf, w1))
            ye = jnp.einsum('nef,efd->ned', h, w2)
            routed = jnp.einsum('ne,ned->nd', combine, ye)
            gu = xf @ shared_gate_up
            gate, up = (gu[:, :F], gu[:, F:])
            shared = jax.nn.silu(gate) * up @ shared_down
            shared = jax.nn.sigmoid(xf @ shared_gate_w) * shared
            return (routed + shared).reshape(b, t, d)
        key = jax.random.key(seed)
        ks = jax.random.split(key, 7)
        std = 0.02
        x = jax.random.normal(ks[0], (B, T, D), dtype=jnp.float32)
        router_w = jax.random.normal(ks[1], (D, E), dtype=jnp.float32) * std
        w1 = jax.random.normal(ks[2], (E, D, F), dtype=jnp.float32) * std
        w2 = jax.random.normal(ks[3], (E, F, D), dtype=jnp.float32) * std
        shared_gate_up = jax.random.normal(ks[4], (D, 2 * F), dtype=jnp.float32) * std
        shared_down = jax.random.normal(ks[5], (F, D), dtype=jnp.float32) * std
        shared_gate_w = jax.random.normal(ks[6], (D, 1), dtype=jnp.float32) * std
        return {'x': x, 'router_w': router_w, 'w1': w1, 'w2': w2, 'shared_gate_up': shared_gate_up, 'shared_down': shared_down, 'shared_gate_w': shared_gate_w}
    _L1_ffn_all = _L1_ffn_setup()
    _L1_ffn_in = {k: v for k, v in _L1_ffn_all.items() if k in ('router_w', 'w1', 'w2', 'shared_gate_up', 'shared_down', 'shared_gate_w')}
    del _L1_ffn_all

    def _L2_attn_setup():
        import jax, jax.numpy as jnp
        import numpy as np
        D_MODEL = 128
        H = 16
        DH = 64
        FFN = 512
        CHUNK = 64
        LN_EPS = 1e-05

        def layer_norm(x, w, b):
            mu = x.mean(-1, keepdims=True)
            var = x.var(-1, keepdims=True)
            return (x - mu) * jax.lax.rsqrt(var + LN_EPS) * w + b

        def l2_normalize(x):
            n = jnp.sqrt(jnp.sum(x * x, axis=-1, keepdims=True))
            return x / jnp.maximum(n, 1e-12)

        def chunk_gla(q, k, v, alpha, C=CHUNK):
            B, Hh, N, D = q.shape
            nc = N // C
            q = q.reshape(B, Hh, nc, C, D)
            k = k.reshape(B, Hh, nc, C, D)
            v = v.reshape(B, Hh, nc, C, D)
            alpha = alpha.reshape(B, Hh, nc, C, D)
            log_a = jnp.log(jnp.maximum(alpha, 1e-06))
            la_cum = jnp.cumsum(log_a, axis=3)
            la_mean = la_cum.mean(-1)
            tril = jnp.tril(jnp.ones((C, C), dtype=q.dtype))
            decay = jnp.exp(la_mean[..., :, None] - la_mean[..., None, :]) * tril
            attn_intra = jnp.einsum('bhncd,bhnmd->bhncm', q, k) * decay
            o_intra = jnp.einsum('bhncm,bhnmd->bhncd', attn_intra, v)
            decay_to_end = jnp.exp(la_cum[:, :, :, -1:, :] - la_cum)
            kv_chunk = jnp.einsum('bhncf,bhnce->bhnfe', k * decay_to_end, v)
            chunk_decay = jnp.exp(log_a.sum(3))
            q_dec = q * jnp.exp(la_cum)

            def step(S, inp):
                qd, kv, cd = inp
                o = jnp.einsum('bhcd,bhde->bhce', qd, S)
                S_new = S * cd[:, :, :, None] + kv
                return (S_new, o)
            S0 = jnp.zeros((B, Hh, D, D), dtype=q.dtype)
            _, o_inter = jax.lax.scan(step, S0, (jnp.moveaxis(q_dec, 2, 0), jnp.moveaxis(kv_chunk, 2, 0), jnp.moveaxis(chunk_decay, 2, 0)))
            o_inter = jnp.moveaxis(o_inter, 0, 2)
            return (o_intra + o_inter).reshape(B, Hh, N, D)
        key = jax.random.key(seed)
        ks = jax.random.split(key, 16)
        s = 0.02
        td = H * DH
        return {'x': jax.random.normal(ks[0], (2, 512, D_MODEL), dtype=jnp.float32), 'Wq': jax.random.normal(ks[1], (D_MODEL, td), dtype=jnp.float32) * s, 'Wk': jax.random.normal(ks[2], (D_MODEL, td), dtype=jnp.float32) * s, 'Wv': jax.random.normal(ks[3], (D_MODEL, td), dtype=jnp.float32) * s, 'Wg': jax.random.normal(ks[4], (D_MODEL, td), dtype=jnp.float32) * s, 'bg': jnp.full((td,), -0.5, dtype=jnp.float32), 'Wo': jax.random.normal(ks[5], (td, D_MODEL), dtype=jnp.float32) * s, 'ln1_w': jnp.ones((D_MODEL,), jnp.float32), 'ln1_b': jnp.zeros((D_MODEL,), jnp.float32), 'ln2_w': jnp.ones((D_MODEL,), jnp.float32), 'ln2_b': jnp.zeros((D_MODEL,), jnp.float32), 'W1': jax.random.normal(ks[6], (D_MODEL, FFN), dtype=jnp.float32) * s, 'b1': jnp.zeros((FFN,), jnp.float32), 'W2': jax.random.normal(ks[7], (FFN, D_MODEL), dtype=jnp.float32) * s, 'b2': jnp.zeros((D_MODEL,), jnp.float32)}
    _L2_attn_all = _L2_attn_setup()
    _L2_attn_in = {k: v for k, v in _L2_attn_all.items() if k in ('Wq', 'Wk', 'Wv', 'Wg', 'bg', 'Wo', 'ln1_w', 'ln1_b', 'ln2_w', 'ln2_b', 'W1', 'b1', 'W2', 'b2')}
    del _L2_attn_all

    def _L2_xattn_setup():
        import jax, jax.numpy as jnp
        import numpy as np
        B, T, DT, G, DV = (16, 64, 128, 72, 96)
        H, DH = (4, 32)
        INNER = H * DH
        HID = 4 * DT
        N_STATE = 64
        K_TOP = 32

        def layernorm(x, g, b, eps=1e-05):
            m = x.mean(-1, keepdims=True)
            v = x.var(-1, keepdims=True)
            return (x - m) * jax.lax.rsqrt(v + eps) * g + b

        def s4d(x, log_dt, A_re, A_im, C_re, C_im, D_skip):
            Bb, L, D = x.shape
            dt = jnp.exp(log_dt)
            A = A_re + 1j * A_im
            C = C_re + 1j * C_im
            dtA = dt[:, None] * A
            dC = C * (jnp.exp(dtA) - 1.0) / A
            powers = jnp.exp(dtA[:, :, None] * jnp.arange(L))
            K = 2.0 * jnp.einsum('dn,dnl->dl', dC, powers).real
            n = 2 * L
            Kf = jnp.fft.rfft(K, n=n, axis=-1)
            xf = jnp.fft.rfft(x, n=n, axis=1)
            y = jnp.fft.irfft(xf * Kf.T[None], n=n, axis=1)[:, :L]
            return y + x * D_skip
        key = jax.random.key(seed)
        ks = jax.random.split(key, 16)
        s = 0.02
        inp = {'x_text': jax.random.normal(ks[0], (B, T, DT), jnp.float32), 'x_vision': jax.random.normal(ks[1], (B, G, DV), jnp.float32), 'text_mask': jnp.ones((B, T), bool), 'vision_mask': jnp.ones((B, G), bool), 'Wq': jax.random.normal(ks[2], (DT, INNER), jnp.float32) * s, 'Wk': jax.random.normal(ks[3], (DV, INNER), jnp.float32) * s, 'Wv': jax.random.normal(ks[4], (DV, DT), jnp.float32) * s, 'W_film_in': jax.random.normal(ks[5], (DT, 2 * DT), jnp.float32) * s, 'b_film_in': jnp.zeros((2 * DT,), jnp.float32), 'W_film_out': jax.random.normal(ks[6], (DT, 2 * DT), jnp.float32) * s, 'b_film_out': jnp.zeros((2 * DT,), jnp.float32), 'g_norm_in': jnp.ones((DT,), jnp.float32), 'b_norm_in': jnp.zeros((DT,), jnp.float32), 'g_norm_out': jnp.ones((DT,), jnp.float32), 'b_norm_out': jnp.zeros((DT,), jnp.float32), 'g_ffn': jnp.ones((DT,), jnp.float32), 'b_ffn': jnp.zeros((DT,), jnp.float32), 'W1': jax.random.normal(ks[7], (DT, HID), jnp.float32) * s, 'b1': jnp.zeros((HID,), jnp.float32), 'W2': jax.random.normal(ks[8], (HID, DT), jnp.float32) * s, 'b2': jnp.zeros((DT,), jnp.float32), 'log_dt': jnp.log(0.001) + jax.random.uniform(ks[9], (DT,), jnp.float32) * (jnp.log(0.1) - jnp.log(0.001)), 'A_re': -0.5 * jnp.ones((DT, N_STATE), jnp.float32), 'A_im': jnp.tile(jnp.pi * jnp.arange(N_STATE, dtype=jnp.float32), (DT, 1)), 'C_re': jax.random.normal(ks[10], (DT, N_STATE), jnp.float32) * 0.5 ** 0.5, 'C_im': jax.random.normal(ks[11], (DT, N_STATE), jnp.float32) * 0.5 ** 0.5, 'D_skip': jax.random.normal(ks[12], (DT,), jnp.float32), 'mod_gate': jnp.array(0.5, jnp.float32)}
        return inp
    _L2_xattn_all = _L2_xattn_setup()
    _L2_xattn_in = {k: v for k, v in _L2_xattn_all.items() if k in ('Wq', 'Wk', 'Wv', 'W_film_in', 'b_film_in', 'W_film_out', 'b_film_out', 'g_norm_in', 'b_norm_in', 'g_norm_out', 'b_norm_out', 'g_ffn', 'b_ffn', 'W1', 'b1', 'W2', 'b2', 'log_dt', 'A_re', 'A_im', 'C_re', 'C_im', 'D_skip', 'mod_gate')}
    del _L2_xattn_all

    def _L2_ffn_setup():
        import jax, jax.numpy as jnp
        import numpy as np
        TOP_K = 2
        key = jax.random.key(seed)
        ks = jax.random.split(key, 6)
        B, S, D, E, H = (4, 256, 128, 8, 512)
        x = jax.random.normal(ks[0], (B, S, D), dtype=jnp.float32)
        Wg = jax.random.normal(ks[1], (D, E), dtype=jnp.float32) * 0.02
        W1 = jax.random.normal(ks[2], (E, D, H), dtype=jnp.float32) * 0.02
        b1 = jnp.zeros((E, H), dtype=jnp.float32)
        W2 = jax.random.normal(ks[3], (E, H, D), dtype=jnp.float32) * 0.02
        b2 = jnp.zeros((E, D), dtype=jnp.float32)
        return {'x': x, 'Wg': Wg, 'W1': W1, 'b1': b1, 'W2': W2, 'b2': b2}
    _L2_ffn_all = _L2_ffn_setup()
    _L2_ffn_in = {k: v for k, v in _L2_ffn_all.items() if k in ('Wg', 'W1', 'b1', 'W2', 'b2')}
    del _L2_ffn_all

    def _L3_attn_setup():
        import jax, jax.numpy as jnp
        import numpy as np
        import math
        DIM_EMB = 128
        KSQRT = math.sqrt(DIM_EMB)
        key = jax.random.key(seed)
        ks = jax.random.split(key, 7)
        b, t, e, d = (4, 512, DIM_EMB, 128)
        s = 1.0 / math.sqrt(e)
        return {'x': jax.random.normal(ks[0], (b, t, e), dtype=jnp.float32), 'Wq': jax.random.normal(ks[1], (d, e), dtype=jnp.float32) * s, 'bq': jax.random.normal(ks[2], (d,), dtype=jnp.float32) * s, 'Wk': jax.random.normal(ks[3], (d, e), dtype=jnp.float32) * s, 'bk': jax.random.normal(ks[4], (d,), dtype=jnp.float32) * s, 'Wv': jax.random.normal(ks[5], (d, e), dtype=jnp.float32) * s, 'bv': jax.random.normal(ks[6], (d,), dtype=jnp.float32) * s}
    _L3_attn_all = _L3_attn_setup()
    _L3_attn_in = {k: v for k, v in _L3_attn_all.items() if k in ('Wq', 'bq', 'Wk', 'bk', 'Wv', 'bv')}
    del _L3_attn_all

    def _L3_xattn_setup():
        import jax, jax.numpy as jnp
        import numpy as np
        IN_DIM = 128
        CTX_DIM = 96
        NUM_HEADS = 16
        HEAD_DIM = IN_DIM // NUM_HEADS
        SCALE = 1.0 / float(np.sqrt(HEAD_DIM))
        key = jax.random.key(seed)
        ks = jax.random.split(key, 10)
        B, NQ, NKV = (8, 128, 64)
        s_in = 1.0 / float(np.sqrt(IN_DIM))
        s_ctx = 1.0 / float(np.sqrt(CTX_DIM))
        return {'x': jax.random.normal(ks[0], (B, NQ, IN_DIM), dtype=jnp.float32), 'context': jax.random.normal(ks[1], (B, NKV, CTX_DIM), dtype=jnp.float32), 'Wq': jax.random.normal(ks[2], (IN_DIM, IN_DIM), dtype=jnp.float32) * s_in, 'bq': jax.random.normal(ks[3], (IN_DIM,), dtype=jnp.float32) * 0.01, 'Wk': jax.random.normal(ks[4], (IN_DIM, CTX_DIM), dtype=jnp.float32) * s_ctx, 'bk': jax.random.normal(ks[5], (IN_DIM,), dtype=jnp.float32) * 0.01, 'Wv': jax.random.normal(ks[6], (IN_DIM, CTX_DIM), dtype=jnp.float32) * s_ctx, 'bv': jax.random.normal(ks[7], (IN_DIM,), dtype=jnp.float32) * 0.01, 'Wo': jax.random.normal(ks[8], (IN_DIM, IN_DIM), dtype=jnp.float32) * s_in, 'bo': jax.random.normal(ks[9], (IN_DIM,), dtype=jnp.float32) * 0.01}
    _L3_xattn_all = _L3_xattn_setup()
    _L3_xattn_in = {k: v for k, v in _L3_xattn_all.items() if k in ('Wq', 'bq', 'Wk', 'bk', 'Wv', 'bv', 'Wo', 'bo')}
    del _L3_xattn_all

    def _L3_ffn_setup():
        import jax, jax.numpy as jnp
        import numpy as np
        EPS = 1e-06
        N_EXPERTS = 8

        def _rms_norm(x, scale, eps=EPS):
            mean_sq = jnp.mean(x.astype(jnp.float32) ** 2, axis=-1, keepdims=True)
            s = scale.astype(jnp.float32) * jax.lax.rsqrt(mean_sq + eps)
            return x * s.astype(x.dtype)

        def _dist2(x, y):
            nx = jnp.sum(x ** 2, axis=-1)[..., :, None]
            ny = jnp.sum(y ** 2, axis=-1)[..., None, :]
            return nx + ny - 2.0 * (x @ y.T)
        key = jax.random.key(seed)
        ks = jax.random.split(key, 5)
        dim, hidden, E = (128, 256, N_EXPERTS)
        x = jax.random.normal(ks[0], (4, 256, dim), dtype=jnp.float32)
        scale = jnp.ones((dim,), dtype=jnp.float32)
        centroids = jax.random.normal(ks[1], (E, dim), dtype=jnp.float32)
        up_w = jax.random.normal(ks[2], (E, dim, hidden * 2), dtype=jnp.float32) * dim ** (-0.5)
        down_w = jax.random.normal(ks[3], (E, hidden, dim), dtype=jnp.float32) * hidden ** (-0.5)
        return {'x': x, 'scale': scale, 'centroids': centroids, 'up_w': up_w, 'down_w': down_w}
    _L3_ffn_all = _L3_ffn_setup()
    _L3_ffn_in = {k: v for k, v in _L3_ffn_all.items() if k in ('scale', 'centroids', 'up_w', 'down_w')}
    del _L3_ffn_all
    return {'x': x, 'ctx_768': ctx_768, 'mask_BxS_bf1': mask_BxS_bf1, 'mask_BxS2_bf1': mask_BxS2_bf1, 'L0_attn_W_Q': _L0_attn_in['W_Q'], 'L0_attn_W_K': _L0_attn_in['W_K'], 'L0_attn_W_V': _L0_attn_in['W_V'], 'L0_attn_W_O': _L0_attn_in['W_O'], 'L0_attn_b_Q': _L0_attn_in['b_Q'], 'L0_attn_b_K': _L0_attn_in['b_K'], 'L0_attn_b_V': _L0_attn_in['b_V'], 'L0_attn_virtual_k': _L0_attn_in['virtual_k'], 'L0_attn_virtual_v': _L0_attn_in['virtual_v'], 'L0_xattn_Wq': _L0_xattn_in['Wq'], 'L0_xattn_Wk': _L0_xattn_in['Wk'], 'L0_xattn_Wv': _L0_xattn_in['Wv'], 'L0_xattn_Wo': _L0_xattn_in['Wo'], 'L0_xattn_bo': _L0_xattn_in['bo'], 'L0_ffn_norm_scale': _L0_ffn_in['norm_scale'], 'L0_ffn_gate_w': _L0_ffn_in['gate_w'], 'L0_ffn_gate_b': _L0_ffn_in['gate_b'], 'L0_ffn_mlp1_w': _L0_ffn_in['mlp1_w'], 'L0_ffn_mlp1_b': _L0_ffn_in['mlp1_b'], 'L0_ffn_mlp2_w': _L0_ffn_in['mlp2_w'], 'L0_ffn_mlp2_b': _L0_ffn_in['mlp2_b'], 'L1_attn_Wq': _L1_attn_in['Wq'], 'L1_attn_bq': _L1_attn_in['bq'], 'L1_attn_Wk': _L1_attn_in['Wk'], 'L1_attn_bk': _L1_attn_in['bk'], 'L1_attn_Wv': _L1_attn_in['Wv'], 'L1_attn_bv': _L1_attn_in['bv'], 'L1_attn_Wo': _L1_attn_in['Wo'], 'L1_attn_bo': _L1_attn_in['bo'], 'L1_xattn_w_q': _L1_xattn_in['w_q'], 'L1_xattn_b_q': _L1_xattn_in['b_q'], 'L1_xattn_w_k': _L1_xattn_in['w_k'], 'L1_xattn_b_k': _L1_xattn_in['b_k'], 'L1_xattn_w_v': _L1_xattn_in['w_v'], 'L1_xattn_b_v': _L1_xattn_in['b_v'], 'L1_xattn_w_o': _L1_xattn_in['w_o'], 'L1_xattn_b_o': _L1_xattn_in['b_o'], 'L1_ffn_router_w': _L1_ffn_in['router_w'], 'L1_ffn_w1': _L1_ffn_in['w1'], 'L1_ffn_w2': _L1_ffn_in['w2'], 'L1_ffn_shared_gate_up': _L1_ffn_in['shared_gate_up'], 'L1_ffn_shared_down': _L1_ffn_in['shared_down'], 'L1_ffn_shared_gate_w': _L1_ffn_in['shared_gate_w'], 'L2_attn_Wq': _L2_attn_in['Wq'], 'L2_attn_Wk': _L2_attn_in['Wk'], 'L2_attn_Wv': _L2_attn_in['Wv'], 'L2_attn_Wg': _L2_attn_in['Wg'], 'L2_attn_bg': _L2_attn_in['bg'], 'L2_attn_Wo': _L2_attn_in['Wo'], 'L2_attn_ln1_w': _L2_attn_in['ln1_w'], 'L2_attn_ln1_b': _L2_attn_in['ln1_b'], 'L2_attn_ln2_w': _L2_attn_in['ln2_w'], 'L2_attn_ln2_b': _L2_attn_in['ln2_b'], 'L2_attn_W1': _L2_attn_in['W1'], 'L2_attn_b1': _L2_attn_in['b1'], 'L2_attn_W2': _L2_attn_in['W2'], 'L2_attn_b2': _L2_attn_in['b2'], 'L2_xattn_Wq': _L2_xattn_in['Wq'], 'L2_xattn_Wk': _L2_xattn_in['Wk'], 'L2_xattn_Wv': _L2_xattn_in['Wv'], 'L2_xattn_W_film_in': _L2_xattn_in['W_film_in'], 'L2_xattn_b_film_in': _L2_xattn_in['b_film_in'], 'L2_xattn_W_film_out': _L2_xattn_in['W_film_out'], 'L2_xattn_b_film_out': _L2_xattn_in['b_film_out'], 'L2_xattn_g_norm_in': _L2_xattn_in['g_norm_in'], 'L2_xattn_b_norm_in': _L2_xattn_in['b_norm_in'], 'L2_xattn_g_norm_out': _L2_xattn_in['g_norm_out'], 'L2_xattn_b_norm_out': _L2_xattn_in['b_norm_out'], 'L2_xattn_g_ffn': _L2_xattn_in['g_ffn'], 'L2_xattn_b_ffn': _L2_xattn_in['b_ffn'], 'L2_xattn_W1': _L2_xattn_in['W1'], 'L2_xattn_b1': _L2_xattn_in['b1'], 'L2_xattn_W2': _L2_xattn_in['W2'], 'L2_xattn_b2': _L2_xattn_in['b2'], 'L2_xattn_log_dt': _L2_xattn_in['log_dt'], 'L2_xattn_A_re': _L2_xattn_in['A_re'], 'L2_xattn_A_im': _L2_xattn_in['A_im'], 'L2_xattn_C_re': _L2_xattn_in['C_re'], 'L2_xattn_C_im': _L2_xattn_in['C_im'], 'L2_xattn_D_skip': _L2_xattn_in['D_skip'], 'L2_xattn_mod_gate': _L2_xattn_in['mod_gate'], 'L2_ffn_Wg': _L2_ffn_in['Wg'], 'L2_ffn_W1': _L2_ffn_in['W1'], 'L2_ffn_b1': _L2_ffn_in['b1'], 'L2_ffn_W2': _L2_ffn_in['W2'], 'L2_ffn_b2': _L2_ffn_in['b2'], 'L3_attn_Wq': _L3_attn_in['Wq'], 'L3_attn_bq': _L3_attn_in['bq'], 'L3_attn_Wk': _L3_attn_in['Wk'], 'L3_attn_bk': _L3_attn_in['bk'], 'L3_attn_Wv': _L3_attn_in['Wv'], 'L3_attn_bv': _L3_attn_in['bv'], 'L3_xattn_Wq': _L3_xattn_in['Wq'], 'L3_xattn_bq': _L3_xattn_in['bq'], 'L3_xattn_Wk': _L3_xattn_in['Wk'], 'L3_xattn_bk': _L3_xattn_in['bk'], 'L3_xattn_Wv': _L3_xattn_in['Wv'], 'L3_xattn_bv': _L3_xattn_in['bv'], 'L3_xattn_Wo': _L3_xattn_in['Wo'], 'L3_xattn_bo': _L3_xattn_in['bo'], 'L3_ffn_scale': _L3_ffn_in['scale'], 'L3_ffn_centroids': _L3_ffn_in['centroids'], 'L3_ffn_up_w': _L3_ffn_in['up_w'], 'L3_ffn_down_w': _L3_ffn_in['down_w']}

def reference(x, ctx_768, mask_BxS_bf1, mask_BxS2_bf1, L0_attn_W_Q, L0_attn_W_K, L0_attn_W_V, L0_attn_W_O, L0_attn_b_Q, L0_attn_b_K, L0_attn_b_V, L0_attn_virtual_k, L0_attn_virtual_v, L0_xattn_Wq, L0_xattn_Wk, L0_xattn_Wv, L0_xattn_Wo, L0_xattn_bo, L0_ffn_norm_scale, L0_ffn_gate_w, L0_ffn_gate_b, L0_ffn_mlp1_w, L0_ffn_mlp1_b, L0_ffn_mlp2_w, L0_ffn_mlp2_b, L1_attn_Wq, L1_attn_bq, L1_attn_Wk, L1_attn_bk, L1_attn_Wv, L1_attn_bv, L1_attn_Wo, L1_attn_bo, L1_xattn_w_q, L1_xattn_b_q, L1_xattn_w_k, L1_xattn_b_k, L1_xattn_w_v, L1_xattn_b_v, L1_xattn_w_o, L1_xattn_b_o, L1_ffn_router_w, L1_ffn_w1, L1_ffn_w2, L1_ffn_shared_gate_up, L1_ffn_shared_down, L1_ffn_shared_gate_w, L2_attn_Wq, L2_attn_Wk, L2_attn_Wv, L2_attn_Wg, L2_attn_bg, L2_attn_Wo, L2_attn_ln1_w, L2_attn_ln1_b, L2_attn_ln2_w, L2_attn_ln2_b, L2_attn_W1, L2_attn_b1, L2_attn_W2, L2_attn_b2, L2_xattn_Wq, L2_xattn_Wk, L2_xattn_Wv, L2_xattn_W_film_in, L2_xattn_b_film_in, L2_xattn_W_film_out, L2_xattn_b_film_out, L2_xattn_g_norm_in, L2_xattn_b_norm_in, L2_xattn_g_norm_out, L2_xattn_b_norm_out, L2_xattn_g_ffn, L2_xattn_b_ffn, L2_xattn_W1, L2_xattn_b1, L2_xattn_W2, L2_xattn_b2, L2_xattn_log_dt, L2_xattn_A_re, L2_xattn_A_im, L2_xattn_C_re, L2_xattn_C_im, L2_xattn_D_skip, L2_xattn_mod_gate, L2_ffn_Wg, L2_ffn_W1, L2_ffn_b1, L2_ffn_W2, L2_ffn_b2, L3_attn_Wq, L3_attn_bq, L3_attn_Wk, L3_attn_bk, L3_attn_Wv, L3_attn_bv, L3_xattn_Wq, L3_xattn_bq, L3_xattn_Wk, L3_xattn_bk, L3_xattn_Wv, L3_xattn_bv, L3_xattn_Wo, L3_xattn_bo, L3_ffn_scale, L3_ffn_centroids, L3_ffn_up_w, L3_ffn_down_w):
    import jax
    import jax.numpy as jnp

    def _L0_attn_ref(resid, W_Q, W_K, W_V, W_O, b_Q, b_K, b_V, virtual_k, virtual_v):
        import jax, jax.numpy as jnp
        import numpy as np
        D_MODEL = 128
        N_QK = 32
        D_QK = 32
        N_OV = 256
        D_OV = 1
        SEQ = 128
        BATCH = 2
        VKV = 16
        ROT_DIM = 32
        ROT_BASE = 10000.0
        SCALE = D_QK ** 0.5

        def _kaiming(k, shape, fan_in):
            return jax.random.normal(k, shape, jnp.float32) * np.sqrt(2.0 / fan_in)

        def _rotary_sin_cos(n_ctx, rd, base):
            pos = jnp.arange(n_ctx, dtype=jnp.float32)
            dim = jnp.arange(rd // 2, dtype=jnp.float32)
            freq = base ** (dim / (rd / 2))
            freq = jnp.concatenate([freq, freq])
            angles = pos[:, None] / freq[None, :]
            return (jnp.sin(angles), jnp.cos(angles))

        def _apply_rotary(x, sin, cos, rd):
            s = x.shape[1]
            x_rot, x_pass = (x[..., :rd], x[..., rd:])
            flip = jnp.concatenate([-x_rot[..., rd // 2:], x_rot[..., :rd // 2]], axis=-1)
            rot = x_rot * cos[None, :s, None, :] + flip * sin[None, :s, None, :]
            return jnp.concatenate([rot, x_pass], axis=-1)
        b, s, _ = resid.shape
        q = jnp.einsum('bsm,hmd->bshd', resid, W_Q) + b_Q
        k = jnp.einsum('bsm,hmd->bshd', resid, W_K) + b_K
        v = jnp.einsum('bsm,hmd->bshd', resid, W_V) + b_V
        sin, cos = _rotary_sin_cos(s, ROT_DIM, ROT_BASE)
        q = _apply_rotary(q, sin, cos, ROT_DIM)
        k = _apply_rotary(k, sin, cos, ROT_DIM)
        k = jnp.concatenate([k, jnp.broadcast_to(virtual_k[None], (b,) + virtual_k.shape)], axis=1)
        v = jnp.concatenate([v, jnp.broadcast_to(virtual_v[None], (b,) + virtual_v.shape)], axis=1)
        kv_len = s + VKV
        scores = jnp.einsum('bqhd,bkhd->bhqk', q, k) / SCALE
        mask = jnp.arange(kv_len)[None, :] <= jnp.arange(s)[:, None] + VKV
        scores = jnp.where(mask[None, None], scores, -jnp.inf)
        pattern = jax.nn.softmax(scores, axis=-1)
        pattern = jnp.where(jnp.isnan(pattern), 0.0, pattern)
        ratio = N_OV // N_QK
        v_g = v.reshape(b, kv_len, N_QK, ratio * D_OV)
        z = jnp.einsum('bhqk,bkhr->bqhr', pattern, v_g)
        z = z.reshape(b, s, N_OV, D_OV)
        out = jnp.einsum('bqhd,hdm->bqm', z, W_O)
        return out

    def _L0_xattn_ref(x, context, Wq, Wk, Wv, Wo, bo):
        import jax, jax.numpy as jnp
        import numpy as np
        QUERY_DIM = 128
        CONTEXT_DIM = 96
        HEADS = 8
        DIM_HEAD = 64
        INNER = HEADS * DIM_HEAD
        B, S, _ = x.shape
        L = context.shape[1]
        scale = DIM_HEAD ** (-0.5)
        q = (x @ Wq).reshape(B, S, HEADS, DIM_HEAD).transpose(0, 2, 1, 3)
        k = (context @ Wk).reshape(B, L, HEADS, DIM_HEAD).transpose(0, 2, 1, 3)
        v = (context @ Wv).reshape(B, L, HEADS, DIM_HEAD).transpose(0, 2, 1, 3)
        attn = jnp.einsum('bhsd,bhld->bhsl', q, k) * scale
        attn = jax.nn.softmax(attn, axis=-1)
        out = jnp.einsum('bhsl,bhld->bhsd', attn, v)
        out = out.transpose(0, 2, 1, 3).reshape(B, S, INNER)
        return out @ Wo + bo

    def _L0_ffn_ref(x, norm_scale, gate_w, gate_b, mlp1_w, mlp1_b, mlp2_w, mlp2_b):
        import jax, jax.numpy as jnp
        import numpy as np
        B, S, D = (1, 256, 128)
        I = 256
        E = 8
        K = 2
        LIMIT = 7.0
        ALPHA = 1.702
        EPS = 1e-05

        def _swiglu(h):
            x_glu = jnp.minimum(h[..., ::2], LIMIT)
            x_lin = jnp.clip(h[..., 1::2], -LIMIT, LIMIT)
            return x_glu * jax.nn.sigmoid(ALPHA * x_glu) * (x_lin + 1.0)

        def _moe(t, gate_w, gate_b, mlp1_w, mlp1_b, mlp2_w, mlp2_b):
            T = t.shape[0]
            logits = t @ gate_w + gate_b
            top_v, top_i = jax.lax.top_k(logits, K)
            probs = jax.nn.softmax(top_v, axis=-1)
            w = jnp.zeros((T, E), t.dtype).at[jnp.arange(T)[:, None], top_i].set(probs)

            def body(acc, ew):
                w1, b1, w2, b2, we = ew
                h = _swiglu(t @ w1 + b1)
                y = h @ w2 + b2
                return (acc + we[:, None] * y, None)
            acc0 = jnp.zeros((T, t.shape[1]), t.dtype)
            acc, _ = jax.lax.scan(body, acc0, (mlp1_w, mlp1_b, mlp2_w, mlp2_b, w.T))
            return acc
        Bx, Sx, Dx = x.shape
        ms = jnp.mean(x * x, axis=-1, keepdims=True)
        t = (x * jax.lax.rsqrt(ms + EPS) * norm_scale).reshape(Bx * Sx, Dx)
        y = _moe(t, gate_w, gate_b, mlp1_w, mlp1_b, mlp2_w, mlp2_b)
        return x + y.reshape(Bx, Sx, Dx)

    def _L1_attn_ref(x, Wq, bq, Wk, bk, Wv, bv, Wo, bo):
        import jax, jax.numpy as jnp
        import numpy as np
        B, T, D = (4, 512, 128)
        H = 16
        DK = D // H
        EPS = 1e-06

        def _phi(x):
            return jax.nn.elu(x) + 1.0
        Bq, Tq, _ = x.shape

        def heads(y):
            return y.reshape(Bq, Tq, H, DK).transpose(0, 2, 1, 3)
        q = _phi(heads(x @ Wq.T + bq))
        k = _phi(heads(x @ Wk.T + bk))
        v = heads(x @ Wv.T + bv)
        kv = jnp.einsum('bhtd,bhtm->bhdm', k, v)
        z = 1.0 / (jnp.einsum('bhtd,bhd->bht', q, k.sum(axis=2) + EPS) + EPS)
        out = jnp.einsum('bhtd,bhdm,bht->bhtm', q, kv, z)
        out = out.transpose(0, 2, 1, 3).reshape(Bq, Tq, -1)
        return out @ Wo.T + bo

    def _L1_xattn_ref(x, context, w_q, b_q, w_k, b_k, w_v, b_v, w_o, b_o):
        import jax, jax.numpy as jnp
        import numpy as np
        N_HEADS = 16
        DIMS = 128
        D_CTX = 96
        HEAD = DIMS // N_HEADS
        B, Lq, D = x.shape
        q = x @ w_q + b_q
        k = context @ w_k + b_k
        v = context @ w_v + b_v
        q = q.reshape(B, Lq, N_HEADS, HEAD)
        k = k.reshape(B, -1, N_HEADS, HEAD)
        v = v.reshape(B, -1, N_HEADS, HEAD)
        scale = 1.0 / np.sqrt(HEAD).astype(np.float32)
        scores = jnp.einsum('bqhd,bkhd->bhqk', q, k) * scale
        weights = jax.nn.softmax(scores, axis=-1)
        out = jnp.einsum('bhqk,bkhd->bqhd', weights, v).reshape(B, Lq, D)
        return out @ w_o + b_o

    def _L1_ffn_ref(x, router_w, w1, w2, shared_gate_up, shared_down, shared_gate_w):
        import jax, jax.numpy as jnp
        import numpy as np
        D = 128
        F = 128
        E = 8
        K = 2
        B, T = (2, 256)

        def _moe_forward(x, router_w, w1, w2, shared_gate_up, shared_down, shared_gate_w):
            b, t, d = x.shape
            xf = x.reshape(-1, d)
            n = xf.shape[0]
            logits = xf @ router_w
            probs = jax.nn.softmax(logits, axis=-1)
            topw, topi = jax.lax.top_k(probs, K)
            combine = jnp.zeros((n, E), dtype=probs.dtype).at[jnp.arange(n)[:, None], topi].add(topw)
            h = jax.nn.silu(jnp.einsum('nd,edf->nef', xf, w1))
            ye = jnp.einsum('nef,efd->ned', h, w2)
            routed = jnp.einsum('ne,ned->nd', combine, ye)
            gu = xf @ shared_gate_up
            gate, up = (gu[:, :F], gu[:, F:])
            shared = jax.nn.silu(gate) * up @ shared_down
            shared = jax.nn.sigmoid(xf @ shared_gate_w) * shared
            return (routed + shared).reshape(b, t, d)
        return _moe_forward(x, router_w, w1, w2, shared_gate_up, shared_down, shared_gate_w)

    def _L2_attn_ref(x, Wq, Wk, Wv, Wg, bg, Wo, ln1_w, ln1_b, ln2_w, ln2_b, W1, b1, W2, b2):
        import jax, jax.numpy as jnp
        import numpy as np
        D_MODEL = 128
        H = 16
        DH = 64
        FFN = 512
        CHUNK = 64
        LN_EPS = 1e-05

        def layer_norm(x, w, b):
            mu = x.mean(-1, keepdims=True)
            var = x.var(-1, keepdims=True)
            return (x - mu) * jax.lax.rsqrt(var + LN_EPS) * w + b

        def l2_normalize(x):
            n = jnp.sqrt(jnp.sum(x * x, axis=-1, keepdims=True))
            return x / jnp.maximum(n, 1e-12)

        def chunk_gla(q, k, v, alpha, C=CHUNK):
            B, Hh, N, D = q.shape
            nc = N // C
            q = q.reshape(B, Hh, nc, C, D)
            k = k.reshape(B, Hh, nc, C, D)
            v = v.reshape(B, Hh, nc, C, D)
            alpha = alpha.reshape(B, Hh, nc, C, D)
            log_a = jnp.log(jnp.maximum(alpha, 1e-06))
            la_cum = jnp.cumsum(log_a, axis=3)
            la_mean = la_cum.mean(-1)
            tril = jnp.tril(jnp.ones((C, C), dtype=q.dtype))
            decay = jnp.exp(la_mean[..., :, None] - la_mean[..., None, :]) * tril
            attn_intra = jnp.einsum('bhncd,bhnmd->bhncm', q, k) * decay
            o_intra = jnp.einsum('bhncm,bhnmd->bhncd', attn_intra, v)
            decay_to_end = jnp.exp(la_cum[:, :, :, -1:, :] - la_cum)
            kv_chunk = jnp.einsum('bhncf,bhnce->bhnfe', k * decay_to_end, v)
            chunk_decay = jnp.exp(log_a.sum(3))
            q_dec = q * jnp.exp(la_cum)

            def step(S, inp):
                qd, kv, cd = inp
                o = jnp.einsum('bhcd,bhde->bhce', qd, S)
                S_new = S * cd[:, :, :, None] + kv
                return (S_new, o)
            S0 = jnp.zeros((B, Hh, D, D), dtype=q.dtype)
            _, o_inter = jax.lax.scan(step, S0, (jnp.moveaxis(q_dec, 2, 0), jnp.moveaxis(kv_chunk, 2, 0), jnp.moveaxis(chunk_decay, 2, 0)))
            o_inter = jnp.moveaxis(o_inter, 0, 2)
            return (o_intra + o_inter).reshape(B, Hh, N, D)
        B, N, _ = x.shape
        xn = layer_norm(x, ln1_w, ln1_b)
        q = (xn @ Wq).reshape(B, N, H, DH).transpose(0, 2, 1, 3)
        k = (xn @ Wk).reshape(B, N, H, DH).transpose(0, 2, 1, 3)
        v = (xn @ Wv).reshape(B, N, H, DH).transpose(0, 2, 1, 3)
        q = l2_normalize(q)
        k = l2_normalize(k)
        alpha = jax.nn.sigmoid(xn @ Wg + bg).reshape(B, N, H, DH).transpose(0, 2, 1, 3)
        o = chunk_gla(q, k, v, alpha)
        o = o.transpose(0, 2, 1, 3).reshape(B, N, H * DH)
        x = x + o @ Wo
        h = layer_norm(x, ln2_w, ln2_b)
        x = x + jax.nn.gelu(h @ W1 + b1, approximate=False) @ W2 + b2
        return x

    def _L2_xattn_ref(x_text, x_vision, text_mask, vision_mask, Wq, Wk, Wv, W_film_in, b_film_in, W_film_out, b_film_out, g_norm_in, b_norm_in, g_norm_out, b_norm_out, g_ffn, b_ffn, W1, b1, W2, b2, log_dt, A_re, A_im, C_re, C_im, D_skip, mod_gate):
        import jax, jax.numpy as jnp
        import numpy as np
        B, T, DT, G, DV = (16, 64, 128, 72, 96)
        H, DH = (4, 32)
        INNER = H * DH
        HID = 4 * DT
        N_STATE = 64
        K_TOP = 32

        def layernorm(x, g, b, eps=1e-05):
            m = x.mean(-1, keepdims=True)
            v = x.var(-1, keepdims=True)
            return (x - m) * jax.lax.rsqrt(v + eps) * g + b

        def s4d(x, log_dt, A_re, A_im, C_re, C_im, D_skip):
            Bb, L, D = x.shape
            dt = jnp.exp(log_dt)
            A = A_re + 1j * A_im
            C = C_re + 1j * C_im
            dtA = dt[:, None] * A
            dC = C * (jnp.exp(dtA) - 1.0) / A
            powers = jnp.exp(dtA[:, :, None] * jnp.arange(L))
            K = 2.0 * jnp.einsum('dn,dnl->dl', dC, powers).real
            n = 2 * L
            Kf = jnp.fft.rfft(K, n=n, axis=-1)
            xf = jnp.fft.rfft(x, n=n, axis=1)
            y = jnp.fft.irfft(xf * Kf.T[None], n=n, axis=1)[:, :L]
            return y + x * D_skip
        Bb, Tt, D = x_text.shape
        Gg = x_vision.shape[1]
        Q = (x_text @ Wq).reshape(Bb, Tt, H, DH)
        K = (x_vision @ Wk).reshape(Bb, Gg, H, DH)
        scores = jnp.einsum('bthd,bghd->bhtg', Q, K) / np.sqrt(DH).astype(np.float32)
        scores = jnp.where(vision_mask[:, None, None, :], scores, -jnp.inf)
        topv, topi = jax.lax.top_k(scores, K_TOP)
        probs = jax.nn.softmax(topv, axis=-1)
        bi = jnp.arange(Bb)[:, None, None, None]
        hi = jnp.arange(H)[None, :, None, None]
        ti = jnp.arange(Tt)[None, None, :, None]
        attn = jnp.zeros_like(scores).at[bi, hi, ti, topi].set(probs)
        attn_mean = attn.mean(axis=1)
        V = x_vision @ Wv
        c_t = jnp.einsum('btg,bgd->btd', attn_mean, V)
        c_t = c_t * text_mask[..., None]
        x = layernorm(x_text, g_norm_in, b_norm_in)
        scale_in, shift_in = jnp.split(c_t @ W_film_in + b_film_in, 2, axis=-1)
        x = x * (1.0 + mod_gate * scale_in) + mod_gate * shift_in
        y = s4d(x, log_dt, A_re, A_im, C_re, C_im, D_skip)
        scale_out, shift_out = jnp.split(c_t @ W_film_out + b_film_out, 2, axis=-1)
        y = y * (1.0 + mod_gate * scale_out) + mod_gate * shift_out
        xt = x_text + y
        h = layernorm(xt, g_ffn, b_ffn)
        h = jax.nn.gelu(h @ W1 + b1, approximate=False) @ W2 + b2
        xt = xt + h
        return layernorm(xt, g_norm_out, b_norm_out)

    def _L2_ffn_ref(x, Wg, W1, b1, W2, b2):
        import jax, jax.numpy as jnp
        import numpy as np
        TOP_K = 2
        B, S, D = x.shape
        E = Wg.shape[1]
        xf = x.reshape(-1, D)
        T = xf.shape[0]
        logits = xf @ Wg
        probs = jax.nn.softmax(logits, axis=-1)
        weights, indices = jax.lax.top_k(probs, TOP_K)
        cw = jnp.zeros((T, E), dtype=x.dtype).at[jnp.arange(T)[:, None], indices].set(weights)
        out = jnp.zeros_like(xf)
        for e in range(E):
            h = jax.nn.gelu(xf @ W1[e] + b1[e], approximate=False)
            y = h @ W2[e] + b2[e]
            out = out + y * cw[:, e:e + 1]
        return out.reshape(B, S, D)

    def _L3_attn_ref(x, Wq, bq, Wk, bk, Wv, bv):
        import jax, jax.numpy as jnp
        import numpy as np
        import math
        DIM_EMB = 128
        KSQRT = math.sqrt(DIM_EMB)
        q = jnp.einsum('bte,de->btd', x, Wq) + bq
        k = jnp.einsum('bte,de->btd', x, Wk) + bk
        v = jnp.einsum('bte,de->btd', x, Wv) + bv
        dot = jnp.einsum('bqd,bkd->bqk', q, k) / KSQRT
        p = jax.nn.softmax(dot, axis=-1)
        z = jnp.einsum('bqk,bkd->bqd', p, v)
        return z

    def _L3_xattn_ref(x, context, Wq, bq, Wk, bk, Wv, bv, Wo, bo):
        import jax, jax.numpy as jnp
        import numpy as np
        IN_DIM = 128
        CTX_DIM = 96
        NUM_HEADS = 16
        HEAD_DIM = IN_DIM // NUM_HEADS
        SCALE = 1.0 / float(np.sqrt(HEAD_DIM))
        q = x @ Wq.T + bq
        k = context @ Wk.T + bk
        v = context @ Wv.T + bv
        B, NQ, _ = q.shape
        NKV = k.shape[1]
        q = q.reshape(B, NQ, NUM_HEADS, HEAD_DIM)
        k = k.reshape(B, NKV, NUM_HEADS, HEAD_DIM)
        v = v.reshape(B, NKV, NUM_HEADS, HEAD_DIM)
        attn = jnp.einsum('bihd,bjhd->bhij', q, k) * SCALE
        attn = jax.nn.softmax(attn, axis=-1)
        out = jnp.einsum('bhij,bjhd->bihd', attn, v)
        out = out.reshape(B, NQ, IN_DIM)
        return out @ Wo.T + bo

    def _L3_ffn_ref(x, scale, centroids, up_w, down_w):
        import jax, jax.numpy as jnp
        import numpy as np
        EPS = 1e-06
        N_EXPERTS = 8

        def _rms_norm(x, scale, eps=EPS):
            mean_sq = jnp.mean(x.astype(jnp.float32) ** 2, axis=-1, keepdims=True)
            s = scale.astype(jnp.float32) * jax.lax.rsqrt(mean_sq + eps)
            return x * s.astype(x.dtype)

        def _dist2(x, y):
            nx = jnp.sum(x ** 2, axis=-1)[..., :, None]
            ny = jnp.sum(y ** 2, axis=-1)[..., None, :]
            return nx + ny - 2.0 * (x @ y.T)
        skip = x
        xn = _rms_norm(x, scale)
        ids = jnp.argmin(_dist2(xn, centroids), axis=-1)
        out = jnp.zeros_like(x)
        for e in range(N_EXPERTS):
            h = jnp.einsum('bsd,dh->bsh', xn, up_w[e])
            a, g = jnp.split(h, 2, axis=-1)
            y = jnp.einsum('bsh,hd->bsd', a * jax.nn.silu(g), down_w[e])
            out = jnp.where((ids == e)[..., None], y, out)
        return out + skip
    x = _layernorm(x + _L0_attn_ref(x, L0_attn_W_Q, L0_attn_W_K, L0_attn_W_V, L0_attn_W_O, L0_attn_b_Q, L0_attn_b_K, L0_attn_b_V, L0_attn_virtual_k, L0_attn_virtual_v), axis=-1)
    x = _layernorm(x + _L0_xattn_ref(x, ctx_768, L0_xattn_Wq, L0_xattn_Wk, L0_xattn_Wv, L0_xattn_Wo, L0_xattn_bo), axis=-1)
    x = _layernorm(x + _L0_ffn_ref(x, L0_ffn_norm_scale, L0_ffn_gate_w, L0_ffn_gate_b, L0_ffn_mlp1_w, L0_ffn_mlp1_b, L0_ffn_mlp2_w, L0_ffn_mlp2_b), axis=-1)
    x = _layernorm(x + _L1_attn_ref(x, L1_attn_Wq, L1_attn_bq, L1_attn_Wk, L1_attn_bk, L1_attn_Wv, L1_attn_bv, L1_attn_Wo, L1_attn_bo), axis=-1)
    x = _layernorm(x + _L1_xattn_ref(x, ctx_768, L1_xattn_w_q, L1_xattn_b_q, L1_xattn_w_k, L1_xattn_b_k, L1_xattn_w_v, L1_xattn_b_v, L1_xattn_w_o, L1_xattn_b_o), axis=-1)
    x = _layernorm(x + _L1_ffn_ref(x, L1_ffn_router_w, L1_ffn_w1, L1_ffn_w2, L1_ffn_shared_gate_up, L1_ffn_shared_down, L1_ffn_shared_gate_w), axis=-1)
    x = _layernorm(x + _L2_attn_ref(x, L2_attn_Wq, L2_attn_Wk, L2_attn_Wv, L2_attn_Wg, L2_attn_bg, L2_attn_Wo, L2_attn_ln1_w, L2_attn_ln1_b, L2_attn_ln2_w, L2_attn_ln2_b, L2_attn_W1, L2_attn_b1, L2_attn_W2, L2_attn_b2), axis=-1)
    x = _layernorm(x + _L2_xattn_ref(x, ctx_768, mask_BxS_bf1, mask_BxS2_bf1, L2_xattn_Wq, L2_xattn_Wk, L2_xattn_Wv, L2_xattn_W_film_in, L2_xattn_b_film_in, L2_xattn_W_film_out, L2_xattn_b_film_out, L2_xattn_g_norm_in, L2_xattn_b_norm_in, L2_xattn_g_norm_out, L2_xattn_b_norm_out, L2_xattn_g_ffn, L2_xattn_b_ffn, L2_xattn_W1, L2_xattn_b1, L2_xattn_W2, L2_xattn_b2, L2_xattn_log_dt, L2_xattn_A_re, L2_xattn_A_im, L2_xattn_C_re, L2_xattn_C_im, L2_xattn_D_skip, L2_xattn_mod_gate), axis=-1)
    x = _layernorm(x + _L2_ffn_ref(x, L2_ffn_Wg, L2_ffn_W1, L2_ffn_b1, L2_ffn_W2, L2_ffn_b2), axis=-1)
    x = _layernorm(x + _L3_attn_ref(x, L3_attn_Wq, L3_attn_bq, L3_attn_Wk, L3_attn_bk, L3_attn_Wv, L3_attn_bv), axis=-1)
    x = _layernorm(x + _L3_xattn_ref(x, ctx_768, L3_xattn_Wq, L3_xattn_bq, L3_xattn_Wk, L3_xattn_bk, L3_xattn_Wv, L3_xattn_bv, L3_xattn_Wo, L3_xattn_bo), axis=-1)
    x = _layernorm(x + _L3_ffn_ref(x, L3_ffn_scale, L3_ffn_centroids, L3_ffn_up_w, L3_ffn_down_w), axis=-1)
    return x

_drawn_inputs = setup_inputs


def setup_inputs(seed=0):
    import zlib

    import numpy as np

    out = dict(_drawn_inputs(seed))
    spreads = {'L0_attn_b_Q': (0.0, 0.1),
     'L0_attn_b_K': (0.0, 0.1),
     'L0_attn_b_V': (0.0, 0.1),
     'L0_attn_virtual_v': (0.0, 0.1),
     'L0_ffn_norm_scale': (1.0, 0.2),
     'L0_ffn_gate_b': (0.0, 0.1),
     'L0_ffn_mlp1_b': (0.0, 0.1),
     'L0_ffn_mlp2_b': (0.0, 0.1),
     'L2_attn_bg': (-0.5, 0.2),
     'L2_attn_ln1_w': (1.0, 0.2),
     'L2_attn_ln1_b': (0.0, 0.1),
     'L2_attn_ln2_w': (1.0, 0.2),
     'L2_attn_ln2_b': (0.0, 0.1),
     'L2_attn_b1': (0.0, 0.1),
     'L2_attn_b2': (0.0, 0.1),
     'L2_xattn_b_film_in': (0.0, 0.1),
     'L2_xattn_b_film_out': (0.0, 0.1),
     'L2_xattn_g_norm_in': (1.0, 0.2),
     'L2_xattn_b_norm_in': (0.0, 0.1),
     'L2_xattn_g_norm_out': (1.0, 0.2),
     'L2_xattn_b_norm_out': (0.0, 0.1),
     'L2_xattn_g_ffn': (1.0, 0.2),
     'L2_xattn_b_ffn': (0.0, 0.1),
     'L2_xattn_b1': (0.0, 0.1),
     'L2_xattn_b2': (0.0, 0.1),
     'L2_xattn_A_re': (-0.5, 0.2),
     'L2_ffn_b1': (0.0, 0.1),
     'L2_ffn_b2': (0.0, 0.1),
     'L3_ffn_scale': (1.0, 0.2)}
    factors = {}
    for name, (base, spread) in spreads.items():
        noise = np.random.default_rng([zlib.crc32(name.encode()), seed]).standard_normal(out[name].shape)
        drawn = base * np.exp(spread * noise) if base else spread * noise
        out[name] = jnp.asarray(drawn.astype(out[name].dtype))
    for name, factor in factors.items():
        out[name] = (out[name] * factor).astype(out[name].dtype)
    return out
```

```python
import math
from collections import namedtuple
from contextlib import ExitStack, contextmanager
import concourse.bass as bass
from concourse import mybir

ACT = mybir.ActivationFunctionType
ALU = mybir.AluOpType
AXX = mybir.AxisListType.X
F32 = mybir.dt.float32
U8 = mybir.dt.uint8

B_ALL = 32
P = 128
NB = 8
GB = 4
NG = NB // GB
GT = GB * P
L = 77
DC = 96


class Environment:
    pass


@contextmanager
def sublayer(nc, names):
    with ExitStack() as ctx:
        sems = {}
        nums = []
        for n in names.split():
            h = ctx.enter_context(nc.semaphore(f"{n}_{nc.next_id()}"))
            sems[n] = h
            nums.append(h.num)
        yield namedtuple("Semaphores", sems)(**sems), ctx
        nums.sort()
        first = prev = nums[0]
        for v in nums[1:] + [None]:
            if v is None or v != prev + 1:
                nc.gpsimd.sem_clear(range(first, prev + 1))
                first = v
            prev = v
        nc.all_engine_barrier()


def bc(ap, shape):
    return ap.broadcast_to(shape)


def pe_transpose4(nc, tiles, bank, ident):
    for j, t in enumerate(tiles):
        ins = nc.tensor.transpose(bank[:, j * P:(j + 1) * P], t, ident)
    return ins


def dve_layernorm(nc, dve, E, s, k, src, dst, scale=None, shift=None):
    st, mv, rstd = E.ln_stats[k % 2], E.ln_mv[k % 2], E.ln_rstd[k % 2]
    for b in range(GB):
        ins = nc.vector.bn_stats(st[:, b, :], src[:, b, :])
    ins.then_inc(s.ln_stats, 1)
    dve.wait_ge(s.ln_stats, k + 1)
    for b in range(GB):
        ins = nc.vector.bn_aggr(mv[:, b, :], st[:, b, :])
    ins.then_inc(s.ln_var, 1)
    dve.wait_ge(s.ln_std, k + 1)
    nc.vector.reciprocal(rstd[:], E.ln_std[k % 2][:]).then_inc(s.ln_rstd, 1)
    dve.wait_ge(s.ln_rstd, k + 1)
    for b in range(GB):
        ins = nc.vector.tensor_scalar(dst[:, b, :], src[:, b, :], mv[:, b, 0:1], rstd[:, b:b + 1],
                                      ALU.subtract, ALU.mult)
    if scale is not None:
        ins.then_inc(s.ln_core, 1)
        dve.wait_ge(s.ln_core, 2 * k + 1)
        ins = nc.vector.tensor_tensor(dst, dst, bc(scale.unsqueeze(1), [P, GB, P]), ALU.mult)
        ins.then_inc(s.ln_core, 1)
        dve.wait_ge(s.ln_core, 2 * k + 2)
        ins = nc.vector.tensor_tensor(dst, dst, bc(shift.unsqueeze(1), [P, GB, P]), ALU.add)
    return ins


def act_layernorm(nc, act, E, s, k):
    act.wait_ge(s.ln_var, k + 1)
    nc.scalar.activation(E.ln_std[k % 2][:], E.ln_mv[k % 2][:, :, 1], ACT.Sqrt,
                         bias=E.eps5[:]).then_inc(s.ln_std, 1)


LN = " ln_stats ln_var ln_std ln_rstd ln_core"


def grp(x, g):
    return x[:, g * GB:(g + 1) * GB, :]


def alloc_common(nc, ctx, E):
    def t(n, s, d=F32):
        return ctx.enter_context(nc.sbuf_tensor(n, s, d))
    E.x = t("x_res", [P, NB, P]); E.r = t("r_res", [P, NB, P]); E.xt = t("x_T", [P, NB * P]); E.ctxT = t("ctx_T", [DC, NB, L])
    E.vmask8 = t("vmask8", [P, NB, L], U8); E.tmask8 = t("tmask8", [P, NB], U8)
    E.ln_stats = [t(f"ln_stats{i}", [P, GB, 6]) for i in range(2)]
    E.ln_mv = [t(f"ln_mv{i}", [P, GB, 2]) for i in range(2)]
    E.ln_std = [t(f"ln_std{i}", [P, GB]) for i in range(2)]
    E.ln_rstd = [t(f"ln_rstd{i}", [P, GB]) for i in range(2)]
    E.ps = ctx.enter_context(nc.psum_tensor("banks", [P, 8, 512], F32))

    def scratch(c):
        return lambda n, s: c.enter_context(nc.sbuf_tensor(f"{n}_{nc.next_id()}", s, F32))
    E.scratch = scratch


def l0_attn(nc, E):
    W, PS = E.w, E.ps
    H, D, DV, VK = 32, 32, 8, 16
    K = P + VK
    NJ = H * D // P
    NR = H // 8
    NU = 2 * NJ
    S = P + DV
    SCALE = float(D) ** -0.5
    with sublayer(nc, "xt_ps xt u_ps rotB rot v_ps v vz kz kb_even kb_odd vp s_ps ms mx nx ex rz nm pt_ps pt zt_ps zt o_ps res" + LN) as (s, ctx):
        sb = E.scratch(ctx)
        QT = sb("QT", [P, NJ, GT]); KT = sb("KT", [P, NJ, GB, P]); KB = sb("KB", [P, 2, NJ // 2, 4, P])
        VA = sb("VA", [P, NB, H * DV]); VP = sb("VP", [P, 2, 16 * S])
        SM = sb("SM", [P, 3, 8, K]); SV = sb("SV", [P, 2, 8, VK]); MX = sb("MX", [P, 2, 8]); NX = sb("NX", [P, 2, 8])
        SU = sb("SU", [P, 2, 8]); RZ = sb("RZ", [P, 2, 8])
        PT = sb("PT", [P, 2, 9, P]); ZT = sb("ZT", [P, 2, P])
        RAB = PT[:].rearrange("p a c q -> p (a c q)")
        R = E.r
        N = NB * NR
        NGR = GB * NR

        kb = lambda m: s.kb_odd if m % 2 else s.kb_even

        def rotary(n):
            return [RAB[:, (2 * (n % 2) + c) * GT:(2 * (n % 2) + c + 1) * GT] for c in range(2)]

        with nc.Block() as block:
            @block.tensor
            def _(pe):
                for g in range(NG):
                    pe_transpose4(nc, [E.x[:, g * GB + b, :] for b in range(GB)], PS[:, 6 + g, :], E.ident).then_inc(s.xt_ps, 1)
                for c in range(NB // 2):
                    if c >= 2:
                        pe.wait_ge(s.v, c - 1)
                    pe.wait_ge(s.xt, c // 2 + 1)
                    for i in range(2):
                        ins = nc.tensor.matmul(PS[:, 4 + c % 2, i * 256:(i + 1) * 256], E.xt[:, (2 * c + i) * P:(2 * c + i + 1) * P], W.wv,
                                               start=True, stop=True)
                    ins.then_inc(s.v_ps, 1)

                def project_in(g):
                    if g:
                        pe.wait_ge(s.ms, g * NGR)
                    for u in range(NU):
                        n = g * NU + u
                        if u >= 2:
                            pe.wait_ge(s.rotB, n - 1)
                        j, xt = u % NJ, E.xt[:, g * GT:(g + 1) * GT]
                        w, wf = (W.wk, W.wkf) if u < NJ else (W.wq, W.wqf)
                        nc.tensor.matmul(PS[:, 2 * (u % 2), :], w[:, j * P:(j + 1) * P], xt, start=True, stop=True)
                        nc.tensor.matmul(PS[:, 2 * (u % 2) + 1, :], wf[:, j * P:(j + 1) * P], xt, start=True, stop=True).then_inc(s.u_ps, 1)

                def scores(n):
                    g, t, r = n // NGR, n // NR, n % NR
                    b, p = t % GB, n % 2
                    if n % NGR == 0:
                        pe.wait_ge(s.rot, (g + 1) * NU)
                        pe.wait_ge(s.rotB, (g + 1) * NU)
                        pe.wait_ge(s.v, NB // 2)
                    if n % 2 == 0:
                        pe.wait_ge(kb(n // 2), 64 * (n // 4 + 1))
                    if n >= 2:
                        pe.wait_ge(s.ms, n - 1)
                    for jj in range(2):
                        j = 2 * r + jj
                        nc.tensor.matmul(PS[:, 2 * p + jj, :], QT[:, j, b * P:(b + 1) * P],
                                         KB[:, n // 2 % 2, j % 4].rearrange("p i k -> p (i k)"), start=True, stop=True)
                    if n >= 1:
                        pe.wait_ge(s.ms, n)
                    if n % NR == NR - 1 and t:
                        pe.wait_ge(s.res, t)
                    for jj in range(2):
                        j = 2 * r + jj
                        ins = nc.tensor.matmul(PS[:, 7, jj * 64:(jj + 1) * 64], QT[:, j, b * P:(b + 1) * P], W.vk[:, j, :], start=True, stop=True)
                    ins.then_inc(s.s_ps, 1)

                def mix(n):
                    r, p = n % NR, n % 2
                    z = PS[:, 6, 0:P]
                    half = lambda c: [nc.tensor.matmul(z, VP[:, n // 2 % 2, (8 * p + h) * P:(8 * p + h + 1) * P], PT[:, p, h, :],
                                                       start=p == 0 and h == 0, stop=False) for h in range(4 * c, 4 * c + 4)]
                    pe.wait_ge(s.nm, n + 1)
                    for c in range(3):
                        k = 3 * n + c
                        if k >= 2:
                            pe.wait_ge(s.pt, k - 1)
                        if c < 2:
                            for i in range(4):
                                ins = nc.tensor.transpose(PS[:, 4 + k % 2, i * P:(i + 1) * P], SM[:, n % 3, 4 * c + i, 0:P], E.ident)
                        else:
                            if p == 0:
                                pe.wait_ge(s.vp, n // 2 + 1)
                                if n >= 2:
                                    pe.wait_ge(s.zt, n // 2)
                            half(0)
                            ins = nc.tensor.transpose(PS[:, 4 + k % 2, 0:P], SV[:, p].rearrange("p h k -> p (h k)"), E.ident)
                        ins.then_inc(s.pt_ps, 1)
                    pe.wait_ge(s.pt, 3 * n + 2)
                    half(1)
                    pe.wait_ge(s.pt, 3 * n + 3)
                    nc.tensor.matmul(z, W.vv[:, r, :], PT[:, p, 8, :], start=False, stop=p == 1).then_inc(s.zt_ps, 1)

                def project(t):
                    pe.wait_ge(s.zt, 2 * t + 2)
                    if t % GB < GB - 1:
                        pe.wait_ge(s.ms, NR * (t + 1) + 3)
                    for c in range(2):
                        ins = nc.tensor.matmul(PS[:, 7, 256:256 + P], ZT[:, c, :], W.wo[:, c, :], start=c == 0, stop=c == 1)
                    ins.then_inc(s.o_ps, 1)

                for g in range(NG):
                    project_in(g)
                    for i in range(NGR + 3):
                        n = g * NGR + i
                        if i < NGR:
                            scores(n)
                        if 2 <= i < NGR + 2:
                            mix(n - 2)
                        if i >= 3 and (n - 3) % NR == NR - 1:
                            project((n - 3) // NR)

            @block.sync
            def _(sp):
                sp.wait_ge(s.kz, 1)
                for m in range(2 * NB):
                    t, c = m // 2, m % 2
                    sp.wait_ge(s.rot, t // GB * NU + NJ)
                    if m >= 2:
                        sp.wait_ge(s.s_ps, 2 * m - 2)
                    for i in range(4):
                        sp.dma_start(KB[D * i:D * (i + 1), m % 2, :, i, :], KT[D * i:D * (i + 1), 4 * c:4 * c + 4, t % GB, :]).then_inc(kb(m), 16)
                sp.wait_ge(s.kb_even, 64 * NB)
                sp.wait_ge(s.kb_odd, 64 * NB)

            @block.scalar
            def _(act):
                for g in range(NG):
                    act.wait_ge(s.xt_ps, g + 1)
                    nc.scalar.copy(E.xt[:, g * GT:(g + 1) * GT], PS[:, 6 + g, :]).then_inc(s.xt, 1)

                def values(m):
                    nc.scalar.copy(VP[:, m % 2].rearrange("k (h s) -> k h s", s=S)[:, :, 0:DV],
                                   VA[:, m // 2, (m % 2) * P:(m % 2 + 1) * P].rearrange("k (h d) -> k h d", d=DV)).then_inc(s.vp, 1)

                def output(m):
                    act.wait_ge(s.zt_ps, 2 * m + 2)
                    if m >= 2:
                        act.wait_ge(s.o_ps, m // 2)
                    nc.scalar.copy(ZT[:, m % 2, :], PS[:, 6, 0:P]).then_inc(s.zt, 1)

                act.wait_ge(s.v, NB // 2)
                act.wait_ge(s.vz, 1)
                values(0)
                values(1)
                for g in range(NG):
                    for i in range(NGR + 3):
                        n = g * NGR + i - 2
                        if 2 <= i < NGR + 2:
                            if n >= 2:
                                act.wait_ge(s.zt_ps, n - 1)
                            for c in range(3):
                                k = 3 * n + c
                                act.wait_ge(s.pt_ps, k + 1)
                                if c < 2:
                                    nc.scalar.copy(PT[:, n % 2, 4 * c:4 * c + 4, :].rearrange("p h q -> p (h q)"), PS[:, 4 + k % 2, :]).then_inc(s.pt, 1)
                                else:
                                    nc.scalar.copy(PT[:, n % 2, 8, :], PS[:, 4 + k % 2, 0:P]).then_inc(s.pt, 1)
                                if c == 0 and i > 2 and n % 2 == 0:
                                    output(n // 2 - 1)
                        elif i == NGR + 2:
                            output(n // 2 - 1)
                        if i < NGR:
                            e = n + 2
                            act.wait_ge(s.nx, e + 1)
                            if e >= 2:
                                act.wait_ge(s.rz, e - 1)
                            for h in range(8):
                                ins = nc.scalar.activation(SM[:, e % 3, h, :], SM[:, e % 3, h, :], ACT.Exp, scale=SCALE,
                                                           bias=NX[:, e % 2, h:h + 1], accum_out=SU[:, e % 2, h:h + 1])
                            ins.then_inc(s.ex, 1)
                        if (2 < i < NGR + 2 and n % 2 == 0 or i == NGR + 2) and n // 2 + 1 < 2 * NB:
                            values(n // 2 + 1)
                for g in range(NG):
                    act_layernorm(nc, act, E, s, g)

            @block.gpsimd
            def _(pool):
                nc.gpsimd.memset(KB[:], 0.0).then_inc(s.kz, 1)
                nc.gpsimd.memset(VP[:], 0.0).then_inc(s.vz, 1)
                for g in range(NG):
                    if g:
                        pool.wait_ge(s.s_ps, g * NGR)
                        pool.wait_ge(s.kb_even, 64 * GB * g)
                        pool.wait_ge(s.kb_odd, 64 * GB * g)
                    for u in range(NU):
                        n = g * NU + u
                        pool.wait_ge(s.rotB, n + 1)
                        a, b_ = rotary(n)
                        out = KT[:, u].rearrange("p b k -> p (b k)") if u < NJ else QT[:, u - NJ, :]
                        nc.gpsimd.tensor_tensor(out, a, b_, ALU.add).then_inc(s.rot, 1)
                    for n in range(g * NGR, (g + 1) * NGR):
                        pool.wait_ge(s.rz, n + 1)
                        nc.gpsimd.tensor_tensor(SM[:, n % 3, :, 0:P], SM[:, n % 3, :, 0:P], bc(RZ[:, n % 2, :].unsqueeze(2), [P, 8, P]), ALU.mult)
                        if n >= 2:
                            pool.wait_ge(s.pt_ps, 3 * (n - 1))
                        nc.gpsimd.tensor_tensor(SV[:, n % 2], SM[:, n % 3, :, P:K], bc(RZ[:, n % 2, :].unsqueeze(2), [P, 8, VK]),
                                                ALU.mult).then_inc(s.nm, 1)

            @block.vector
            def _(dve):
                for c in range(NB // 2):
                    dve.wait_ge(s.v_ps, c + 1)
                    nc.vector.tensor_tensor(VA[:, 2 * c:2 * c + 2, :], PS[:, 4 + c % 2, :].rearrange("p (b n) -> p b n", b=2),
                                            bc(W.bv.unsqueeze(1), [P, 2, H * DV]), ALU.add).then_inc(s.v, 1)

                def rotate(g):
                    for u in range(NU):
                        n = g * NU + u
                        j = u % NJ
                        bias, biasf = (W.bk, W.bkf) if u < NJ else (W.bq, W.bqf)
                        if u >= 2:
                            dve.wait_ge(s.rot, n - 1)
                        elif g:
                            dve.wait_ge(s.zt_ps, g * NGR)
                        dve.wait_ge(s.u_ps, n + 1)
                        for buf, bank, bb, table in zip(rotary(n), (0, 1), (bias, biasf), (E.cos, E.sin)):
                            ins = nc.vector.scalar_tensor_tensor(buf.rearrange("p (b q) -> p b q", b=GB),
                                                                 PS[:, 2 * (u % 2) + bank, :].rearrange("p (b q) -> p b q", b=GB), bb[:, j:j + 1],
                                                                 bc(table.unsqueeze(1), [P, GB, P]), ALU.add, ALU.mult)
                        ins.then_inc(s.rotB, 1)

                def reciprocal(n):
                    dve.wait_ge(s.ex, n + 1)
                    if n >= 2:
                        dve.wait_ge(s.nm, n - 1)
                    nc.vector.reciprocal(RZ[:, n % 2, :], SU[:, n % 2, :]).then_inc(s.rz, 1)

                def softmax_in(n):
                    if n >= 3:
                        dve.wait_ge(s.pt_ps, 3 * (n - 2))
                        dve.wait_ge(s.nm, n - 2)
                    dve.wait_ge(s.s_ps, n + 1)
                    p = n % 2
                    nc.vector.tensor_tensor(SM[:, n % 3, :, 0:P], PS[:, 2 * p:2 * p + 2, :].rearrange("p a (i k) -> p (a i) k", k=P),
                                            bc(E.causal[:, 0:P].unsqueeze(1), [P, 8, P]), ALU.add)
                    nc.vector.tensor_tensor(SM[:, n % 3, :, P:K], PS[:, 7, 0:P].rearrange("p (h k) -> p h k", k=VK),
                                            bc(E.causal[:, P:K].unsqueeze(1), [P, 8, VK]), ALU.add).then_inc(s.ms, 1)
                    if n % NGR:
                        reciprocal(n - 1)
                    dve.wait_ge(s.ms, n + 1)
                    nc.vector.tensor_reduce(MX[:, p, :], SM[:, n % 3], AXX, ALU.max).then_inc(s.mx, 1)
                    dve.wait_ge(s.mx, n + 1)
                    if n >= 2:
                        dve.wait_ge(s.ex, n - 1)
                    nc.vector.tensor_scalar(NX[:, p, :], MX[:, p, :], -SCALE, None, ALU.mult).then_inc(s.nx, 1)

                for g in range(NG):
                    rotate(g)
                    for i in range(NGR + 4):
                        n = g * NGR + i
                        if i >= 4 and (n - 4) % NR == NR - 1:
                            t = (n - 4) // NR
                            dve.wait_ge(s.o_ps, t + 1)
                            nc.vector.tensor_tensor(R[:, t, :], PS[:, 7, 256:256 + P], E.x[:, t, :], ALU.add).then_inc(s.res, 1)
                        if i < NGR:
                            softmax_in(n)
                        if i == NGR:
                            reciprocal(n - 1)
                dve.wait_ge(s.res, NB)
                for g in range(NG):
                    dve_layernorm(nc, dve, E, s, g, grp(R, g), grp(E.x, g))


def l0_xattn(nc, E, prefetch=()):
    W, PS = E.w, E.ps
    H, D = 8, 64
    NJ = H * D // P
    CG = GB * L
    proj = [("k", g, j) for g in range(NG) for j in range(NJ)] + [("q", g, j) for g in range(NG) for j in range(NJ)] + \
           [("v", t, 0) for t in range(NB)]
    NU = len(proj)
    with sublayer(nc, "xt_ps xt u_ps ua ud vz pz rb s_ps mx sub ex sm rz nm pt_ps pt zt_ps zt o_ps res w_ld" + LN) as (s, ctx):
        sb = E.scratch(ctx)
        QT = sb("QT", [P, NJ, NB * P]); KT = sb("KT", [P, NJ, NB, 2, L]); VA = sb("VA", [P, NB, H * D])
        MX = sb("MX", [P, 2, H]); SM = sb("SM", [P, 3, H, L]); SU = sb("SU", [P, 2, H]); RZ = sb("RZ", [P, 2, H])
        PT = sb("PT", [P, 2, H, P]); ZT = sb("ZT", [P, 2, NJ * P])
        XB = E.r
        on_act = [u for u in range(NU) if u % 2 == 0]
        on_dve = [u for u in range(NU) if u % 2 == 1]

        def unit_out(u):
            kind, a, j = proj[u]
            if kind == "k":
                return [(KT[o * D:(o + 1) * D, j, a * GB:(a + 1) * GB, o, :],
                         PS[o * D:(o + 1) * D, u % 4, 0:CG].rearrange("p (b l) -> p b l", l=L)) for o in range(2)]
            if kind == "v":
                return [(VA[0:L, a, :], PS[0:L, u % 4, :])]
            return [(QT[:, j, a * GT:(a + 1) * GT], PS[:, u % 4, :])]

        def done(eng, u):
            if u % 2 == 0:
                eng.wait_ge(s.ua, u // 2 + 1)
            else:
                eng.wait_ge(s.ud, u // 2 + 1)

        with nc.Block() as block:
            @block.sync
            def _(sp):
                for dst, src in prefetch:
                    sp.dma_start(dst, src).then_inc(s.w_ld, 16)
                if prefetch:
                    sp.wait_ge(s.w_ld, 16 * len(prefetch))

            @block.tensor
            def _(pe):
                for g in range(NG):
                    pe_transpose4(nc, [E.x[:, g * GB + b, :] for b in range(GB)], PS[:, 4 + g, :], E.ident).then_inc(s.xt_ps, 1)
                for u, (kind, a, j) in enumerate(proj):
                    if u >= 4:
                        done(pe, u - 4)
                    if kind == "k":
                        nc.tensor.matmul(PS[:, u % 4, 0:CG], W.wk[:, j * P:(j + 1) * P],
                                         E.ctxT[:, a * GB:(a + 1) * GB, :].rearrange("c b l -> c (b l)"), start=True, stop=True).then_inc(s.u_ps, 1)
                    elif kind == "v":
                        nc.tensor.matmul(PS[0:L, u % 4, :], E.ctxT[:, a, :], W.wv, start=True, stop=True).then_inc(s.u_ps, 1)
                    else:
                        pe.wait_ge(s.xt, a + 1)
                        nc.tensor.matmul(PS[:, u % 4, :], W.wq[:, j * P:(j + 1) * P], E.xt[:, a * GT:(a + 1) * GT],
                                         start=True, stop=True).then_inc(s.u_ps, 1)
                for u in range(NU - 4, NU):
                    done(pe, u)

                def scores(t):
                    if t >= 2:
                        pe.wait_ge(s.sub, t - 1)
                    for j in range(NJ):
                        ins = nc.tensor.matmul(PS[:, 2 * (t % 2) + j // 2, j % 2 * 2 * L:(j % 2 + 1) * 2 * L], QT[:, j, t * P:(t + 1) * P],
                                               KT[:, j, t].rearrange("p o l -> p (o l)"), start=True, stop=True)
                    ins.then_inc(s.s_ps, 1)

                def mix(t):
                    pe.wait_ge(s.nm, t + 1)
                    for a in range(2):
                        k = 2 * t + a
                        if k >= 2:
                            pe.wait_ge(s.pt, k - 1)
                        for h in range(4):
                            ins = nc.tensor.transpose(PS[0:L, 4 + a, h * P:(h + 1) * P], SM[:, t % 3, 4 * a + h, :], E.ident)
                        ins.then_inc(s.pt_ps, 1)
                    if t >= 1:
                        pe.wait_ge(s.zt, t)
                    for a in range(2):
                        pe.wait_ge(s.pt, 2 * t + a + 1)
                        for h in range(4 * a, 4 * a + 4):
                            ins = nc.tensor.matmul(PS[h % 2 * D:(h % 2 + 1) * D, 6, h // 2 * P:(h // 2 + 1) * P], VA[:, t, h * D:(h + 1) * D],
                                                   PT[:, t % 2, h, :], start=True, stop=True)
                    ins.then_inc(s.zt_ps, 1)

                def project(t):
                    pe.wait_ge(s.zt, t + 1)
                    if t >= 1:
                        pe.wait_ge(s.res, t)
                    for j in range(NJ):
                        ins = nc.tensor.matmul(PS[:, 7, 0:P], ZT[:, t % 2, j * P:(j + 1) * P], W.wo[:, j, :], start=j == 0, stop=j == NJ - 1)
                    ins.then_inc(s.o_ps, 1)

                for i in range(NB + 3):
                    if i < NB:
                        scores(i)
                    if i >= 3:
                        project(i - 3)
                    if 2 <= i < NB + 2:
                        mix(i - 2)

            @block.scalar
            def _(act):
                for g in range(NG):
                    act.wait_ge(s.xt_ps, g + 1)
                    nc.scalar.copy(E.xt[:, g * GT:(g + 1) * GT], PS[:, 4 + g, :]).then_inc(s.xt, 1)
                for u in on_act:
                    act.wait_ge(s.u_ps, u + 1)
                    if proj[u][0] == "v":
                        act.wait_ge(s.vz, 1)
                    for out, in_ in unit_out(u):
                        ins = nc.scalar.copy(out, in_)
                    ins.then_inc(s.ua, 1)
                act.wait_ge(s.pz, 1)
                for i in range(NB + 2):
                    t = i - 2
                    if t >= 0:
                        for a in range(2):
                            act.wait_ge(s.pt_ps, 2 * t + a + 1)
                            if a == 0 and t >= 2:
                                act.wait_ge(s.zt_ps, t - 1)
                            nc.scalar.copy(PT[0:L, t % 2, 4 * a:4 * a + 4, :].rearrange("p h q -> p (h q)"), PS[0:L, 4 + a, :]).then_inc(s.pt, 1)
                    if i < NB:
                        act.wait_ge(s.sub, i + 1)
                        nc.scalar.activation(SM[:, i % 3], SM[:, i % 3], ACT.Exp, scale=float(D) ** -0.5).then_inc(s.ex, 1)
                    if t >= 0:
                        act.wait_ge(s.zt_ps, t + 1)
                        if t >= 2:
                            act.wait_ge(s.o_ps, t - 1)
                        nc.scalar.copy(ZT[:, t % 2, :], PS[:, 6, :]).then_inc(s.zt, 1)
                for g in range(NG):
                    act_layernorm(nc, act, E, s, g)

            @block.gpsimd
            def _(pool):
                nc.gpsimd.memset(VA[:], 0.0).then_inc(s.vz, 1)
                nc.gpsimd.memset(PT[:], 0.0).then_inc(s.pz, 1)
                nc.gpsimd.tensor_tensor(XB[:], E.x[:], bc(W.bo.unsqueeze(1), [P, NB, P]), ALU.add).then_inc(s.rb, 1)
                for t in range(NB):
                    pool.wait_ge(s.rz, t + 1)
                    nc.gpsimd.tensor_tensor(SM[:, t % 3], SM[:, t % 3], bc(RZ[:, t % 2, :].unsqueeze(2), [P, H, L]), ALU.mult).then_inc(s.nm, 1)

            @block.vector
            def _(dve):
                for o in range(2):
                    nc.vector.memset(KT[o * D:(o + 1) * D, :, :, 1 - o, :], 0.0)
                for u in on_dve:
                    dve.wait_ge(s.u_ps, u + 1)
                    if proj[u][0] == "v":
                        dve.wait_ge(s.vz, 1)
                    for out, in_ in unit_out(u):
                        ins = nc.vector.tensor_copy(out, in_)
                    ins.then_inc(s.ud, 1)

                for i in range(NB + 3):
                    if i < NB:
                        sc = PS[:, 2 * (i % 2):2 * (i % 2) + 2, 0:4 * L].rearrange("p a (h l) -> p a h l", l=L)
                        dve.wait_ge(s.s_ps, i + 1)
                        nc.vector.tensor_reduce(MX[:, i % 2, :].rearrange("p (a h) -> p a h", a=2), sc, AXX, ALU.max).then_inc(s.mx, 1)
                        dve.wait_ge(s.mx, i + 1)
                        if i >= 3:
                            dve.wait_ge(s.pt_ps, 2 * (i - 2))
                        nc.vector.tensor_tensor(SM[:, i % 3].rearrange("p (a h) l -> p a h l", a=2), sc,
                                                bc(MX[:, i % 2, :].rearrange("p (a h) -> p a h", a=2).unsqueeze(3), [P, 2, 4, L]),
                                                ALU.subtract).then_inc(s.sub, 1)
                    if i >= 3:
                        t = i - 3
                        dve.wait_ge(s.o_ps, t + 1)
                        if t == 0:
                            dve.wait_ge(s.rb, 1)
                        nc.vector.tensor_tensor(XB[:, t, :], PS[:, 7, 0:P], XB[:, t, :], ALU.add).then_inc(s.res, 1)
                    if i < NB:
                        dve.wait_ge(s.ex, i + 1)
                        nc.vector.tensor_reduce(SU[:, i % 2, :], SM[:, i % 3], AXX, ALU.add).then_inc(s.sm, 1)
                        dve.wait_ge(s.sm, i + 1)
                        if i >= 2:
                            dve.wait_ge(s.nm, i - 1)
                        nc.vector.reciprocal(RZ[:, i % 2, :], SU[:, i % 2, :]).then_inc(s.rz, 1)
                dve.wait_ge(s.res, NB)
                for g in range(NG):
                    dve_layernorm(nc, dve, E, s, g, grp(XB, g), grp(E.x, g))


NEG = -1.0e30


def moe(nc, E, kind, names_extra=""):
    W, PS = E.w, E.ps
    rms = kind in ("swiglu", "gated")
    NE = 8
    blocks = {"swiglu": 4, "silu": 1, "gelu": 4, "gated": 4}[kind]
    hb = {"swiglu": 2, "silu": 1, "gelu": 4, "gated": 2}[kind]
    shared = kind == "silu"
    units = [(e, g) for e in range(NE) for g in range(NG)]
    if shared:
        units += [(NE, g) for g in range(NG)]
    U = len(units)
    NL = NE + 1 if shared else NE
    nblk = [2 if (shared and e == NE) else blocks for e, g in units]
    first = [sum(nblk[:u]) for u in range(U)]
    eps = {"swiglu": E.eps5, "gated": E.eps6}.get(kind)
    double = kind in ("swiglu", "gated")
    has_b2 = kind in ("swiglu", "gelu")
    M_BANK = 6
    with sublayer(nc, "rm_stats rm_var rm_m2 rm_ms rm_std rm_rstd tn xt_ps xt cn cn_ps cn_row lg_ps lg m8 m8m rep sel sub ex "
                      "selx den rden wt wt_ps wtT_ps wtT b2_ps acc0 "
                      "h_ps act_done dve_h glu sig gs gl2 lin hid y_ps acc res" + LN) as (s, ctx):
        sb = E.scratch(ctx)
        TN = sb("TN", [P, NB, P]) if rms else None
        m2 = sb("m2", [P, NG, GB]); ms = sb("ms", [P, NG, GB]); rstd = sb("rr", [P, NG, GB]); std = sb("sd", [P, NG, GB])
        LG = sb("LG", [P, NB, 16]); M8 = sb("M8", [P, NB, 8]); RP = sb("RP", [P, NB, 16])
        XS = sb("XS", [P, NB, NE]); EX = sb("EX", [P, NB, NE]); SEL = sb("SEL", [P, NB, NE]); SX = sb("SX", [P, NB, NE])
        DEN = sb("DEN", [P, NB]); WT = sb("WT", [P, NB, NL]); WTT = sb("WTT", [NE, NB * P])
        GATE = sb("GATE", [P, NB]) if shared else None
        HT = sb("HT", [P, 2, hb, GT])
        T1 = sb("T1", [P, 2, GT]); T2 = sb("T2", [P, 2, GT]); T3 = sb("T3", [P, 2, GT])
        R = sb("R", [P, NB, P])
        CN = sb("CN", [P, NE]); CNR = sb("CNR", [1, NE])
        b1p = sb("b1p", [P, NE, 2]) if kind == "swiglu" else None
        src = TN if rms else E.x

        with nc.Block() as block:
            @block.tensor
            def _(pe):
                for g in range(NG):
                    if rms:
                        pe.wait_ge(s.tn, g + 1)
                    pe_transpose4(nc, [src[:, g * GB + b, :] for b in range(GB)], PS[:, g, :], E.ident).then_inc(s.xt_ps, 1)
                if kind == "gated":
                    pe.wait_ge(s.cn, 1)
                    nc.tensor.matmul(PS[0:1, 7, 0:NE], E.minus_half[:, 0:1], CN[:], start=True, stop=True).then_inc(s.cn_ps, 1)
                    pe.wait_ge(s.cn_row, 1)
                for g in range(NG):
                    pe.wait_ge(s.xt, g + 1)
                    for b in range(GB):
                        t = g * GB + b
                        o = PS[:, M_BANK, t * NL:(t + 1) * NL]
                        brow = {"swiglu": lambda: W.gb, "gated": lambda: CNR[0:1, :]}.get(kind)
                        ins = nc.tensor.matmul(o, E.xt[:, t * P:(t + 1) * P], W.gw, start=True, stop=brow is None)
                        if brow is not None:
                            ins = nc.tensor.matmul(o, E.ones_row[0:1, :], brow(), start=False, stop=True)
                ins.then_inc(s.lg_ps, 1)

                def up(u):
                    e, g = units[u]
                    xt = E.xt[:, g * GT:(g + 1) * GT]
                    for j in range(nblk[u]):
                        q = first[u] + j
                        if q >= 4:
                            p = q - 4
                            pu = max(i for i in range(U) if first[i] <= p)
                            pj = p - first[pu]
                            if kind == "swiglu":
                                pe.wait_ge(s.dve_h, p + 1)
                            elif kind == "gelu":
                                pe.wait_ge(s.act_done, p + 1)
                            elif kind == "gated":
                                if pj % 2 == 0:
                                    pe.wait_ge(s.act_done, p // 2 + 1)
                                else:
                                    pe.wait_ge(s.dve_h, p // 2 + 1)
                            elif units[pu][0] < NE:
                                pe.wait_ge(s.act_done, pu + 1)
                            elif pj == 0:
                                pe.wait_ge(s.act_done, pu + 1)
                            else:
                                pe.wait_ge(s.dve_h, pu - NE * NG + 1)
                        elif q < 2:
                            pe.wait_ge(s.xt, q + 1)
                        if shared and e == NE:
                            w = W.sgu[:, j * P:(j + 1) * P]
                        elif kind == "silu":
                            w = W.w1[:, e, :]
                        elif kind == "gelu":
                            w = W.w1[:, e, j * P:(j + 1) * P]
                        elif kind == "swiglu":
                            w = W.w1[:, e, j % 2, (j // 2) * P:(j // 2 + 1) * P]
                        else:
                            c0 = (0 if j % 2 else 2) + j // 2
                            w = W.w1[:, e, c0 * P:(c0 + 1) * P]
                        nc.tensor.matmul(PS[:, q % 4, :], w, xt, start=True, stop=True).then_inc(s.h_ps, 1)

                def down(u):
                    e, g = units[u]
                    pe.wait_ge(s.hid, u + 1)
                    if u >= 2:
                        pe.wait_ge(s.acc, u - 1)
                    if kind == "silu":
                        w2 = [W.sd[:] if e == NE else W.w2[:, e, :]]
                    else:
                        w2 = [W.w2[:, e, j, :] for j in range(hb)]
                    for b in range(GB):
                        for j in range(len(w2)):
                            ins = nc.tensor.matmul(PS[:, 4 + u % 2, b * P:(b + 1) * P],
                                                   HT[:, u % 2, j, b * P:(b + 1) * P], w2[j],
                                                   start=j == 0, stop=j == len(w2) - 1)
                    ins.then_inc(s.y_ps, 1)

                up(0)
                if has_b2:
                    pe.wait_ge(s.wt, 1)
                    for t in range(NB):
                        o = PS[0:NE, 4 + t // GB, (t % GB) * P:(t % GB + 1) * P]
                        ins = nc.tensor.transpose(o, WT[:, t, :], E.ident)
                    ins.then_inc(s.wtT_ps, 1)
                    pe.wait_ge(s.wtT, 2)
                    for t in range(NB):
                        o = PS[:, M_BANK + t // GB, (t % GB) * P:(t % GB + 1) * P]
                        ins = nc.tensor.matmul(o, WTT[:, t * P:(t + 1) * P], W.b2, start=True, stop=True)
                    ins.then_inc(s.b2_ps, 1)
                for u in range(1, U + 1):
                    if u < U:
                        up(u)
                    down(u - 1)

            @block.scalar
            def _(act):
                if rms:
                    for g in range(NG):
                        act.wait_ge(s.rm_ms, g + 1)
                        nc.scalar.activation(std[:, g], ms[:, g], ACT.Sqrt, bias=eps[:]).then_inc(s.rm_std, 1)
                for g in range(NG):
                    act.wait_ge(s.xt_ps, g + 1)
                    nc.scalar.copy(E.xt[:, g * GT:(g + 1) * GT], PS[:, g, :]).then_inc(s.xt, 1)
                if kind != "gated":
                    act.wait_ge(s.sub, 1)
                    nc.scalar.activation(EX[:], XS[:], ACT.Exp).then_inc(s.ex, 1)
                if shared:
                    act.wait_ge(s.lg, 1)
                    nc.scalar.activation(GATE[:], PS[:, M_BANK, 0:NB * NL].rearrange("p (t e) -> p t e", e=NL)[:, :, NE],
                                         ACT.Sigmoid).then_inc(s.ex, 1)

                for u, (e, g) in enumerate(units):
                    if u >= 2 and kind in ("gelu", "silu"):
                        act.wait_ge(s.y_ps, u - 1)
                    if kind == "gelu":
                        for j in range(4):
                            act.wait_ge(s.h_ps, first[u] + j + 1)
                            ins = nc.scalar.activation(HT[:, u % 2, j, :], PS[:, (first[u] + j) % 4, :], ACT.Gelu,
                                                       bias=W.b1[:, e, j:j + 1]).then_inc(s.act_done, 1)
                            if j == 3:
                                act.wait_ge(s.act_done, first[u] + 4)
                                act.sem_inc(s.hid, 1)
                    elif kind == "silu":
                        act.wait_ge(s.h_ps, first[u] + 1)
                        if e < NE:
                            nc.scalar.activation(HT[:, u % 2, 0, :], PS[:, first[u] % 4, :], ACT.Silu).then_inc(s.act_done, 1)
                            act.wait_ge(s.act_done, u + 1)
                            act.sem_inc(s.hid, 1)
                        else:
                            nc.scalar.activation(T1[:, g, :], PS[:, first[u] % 4, :], ACT.Silu).then_inc(s.act_done, 1)
                    elif kind == "gated":
                        for j in range(2):
                            k = 2 * u + j
                            act.wait_ge(s.h_ps, first[u] + 2 * j + 1)
                            if k >= 2:
                                act.wait_ge(s.dve_h, k - 1)
                            nc.scalar.activation(T1[:, k % 2, :], PS[:, (first[u] + 2 * j) % 4, :], ACT.Silu).then_inc(s.act_done, 1)
                    else:
                        for j in range(2):
                            k = 2 * u + j
                            act.wait_ge(s.glu, k + 1)
                            if k >= 2:
                                act.wait_ge(s.gs, k - 1)
                            nc.scalar.activation(T2[:, k % 2, :], T1[:, k % 2, :], ACT.Sigmoid, scale=1.702).then_inc(s.sig, 1)
                for g in range(NG):
                    act_layernorm(nc, act, E, s, g)

            @block.gpsimd
            def _(pool):
                if kind == "swiglu":
                    for u, (e, g) in enumerate(units):
                        for j in range(2):
                            k = 2 * u + j
                            pool.wait_ge(s.sig, k + 1)
                            nc.gpsimd.tensor_tensor(T1[:, k % 2, :], T1[:, k % 2, :], T2[:, k % 2, :], ALU.mult).then_inc(s.gs, 1)

            @block.vector
            def _(dve):
                if rms:
                    for g in range(NG):
                        st, mv = E.ln_stats[g], E.ln_mv[g]
                        for b in range(GB):
                            ins = nc.vector.bn_stats(st[:, b, :], E.x[:, g * GB + b, :])
                        ins.then_inc(s.rm_stats, 1)
                        dve.wait_ge(s.rm_stats, g + 1)
                        for b in range(GB):
                            ins = nc.vector.bn_aggr(mv[:, b, :], st[:, b, :])
                        ins.then_inc(s.rm_var, 1)
                        dve.wait_ge(s.rm_var, g + 1)
                        nc.vector.tensor_tensor(m2[:, g], mv[:, :, 0], mv[:, :, 0], ALU.mult).then_inc(s.rm_m2, 1)
                        dve.wait_ge(s.rm_m2, g + 1)
                        nc.vector.tensor_tensor(ms[:, g], m2[:, g], mv[:, :, 1], ALU.add).then_inc(s.rm_ms, 1)
                    for g in range(NG):
                        dve.wait_ge(s.rm_std, g + 1)
                        nc.vector.reciprocal(rstd[:, g], std[:, g]).then_inc(s.rm_rstd, 1)
                        dve.wait_ge(s.rm_rstd, g + 1)
                        for b in range(GB):
                            t = g * GB + b
                            ins = nc.vector.scalar_tensor_tensor(TN[:, t, :], E.x[:, t, :], rstd[:, g, b:b + 1], W.scale,
                                                                 ALU.mult, ALU.mult)
                        ins.then_inc(s.tn, 1)
                if kind == "gated":
                    nc.vector.tensor_tensor(CN[:], W.gw, W.gw, ALU.mult).then_inc(s.cn, 1)
                    dve.wait_ge(s.cn_ps, 1)
                    nc.vector.tensor_copy(CNR[0:1, :], PS[0:1, 7, 0:NE]).then_inc(s.cn_row, 1)
                if kind == "swiglu":
                    nc.vector.tensor_copy(b1p[:], W.b1[:, :, 0, :])
                    nc.vector.tensor_scalar(W.b1lin, W.b1[:, :, 1, :], 1.0, None, ALU.add)
                nc.vector.memset(LG[:, :, NE:16], NEG)
                dve.wait_ge(s.lg_ps, 1)
                nc.vector.tensor_copy(LG[:, :, 0:NE], PS[:, M_BANK, 0:NB * NL].rearrange("p (t e) -> p t e", e=NL)[:, :, 0:NE]).then_inc(s.lg, 1)
                dve.wait_ge(s.lg, 1)
                for t in range(NB):
                    ins = nc.vector.max(M8[:, t, :], LG[:, t, 0:NE])
                ins.then_inc(s.m8, 1)
                dve.wait_ge(s.m8, 1)
                if kind != "gated":
                    nc.vector.tensor_tensor(XS[:], LG[:, :, 0:NE], bc(M8[:, :, 0:1], [P, NB, NE]), ALU.subtract).then_inc(s.sub, 1)
                nc.vector.memset(M8[:, :, (1 if kind == "gated" else 2):8], NEG).then_inc(s.m8m, 1)
                dve.wait_ge(s.m8m, 1)
                for t in range(NB):
                    ins = nc.vector.match_replace(RP[:, t, :], M8[:, t, :], LG[:, t, :], 2 * NEG)
                ins.then_inc(s.rep, 1)
                dve.wait_ge(s.rep, 1)
                nc.vector.tensor_tensor(WT[:, :, 0:NE] if kind == "gated" else SEL[:], RP[:, :, 0:NE], LG[:, :, 0:NE],
                                        ALU.not_equal).then_inc(s.sel, 1)
                dve.wait_ge(s.sel, 1)
                if kind == "gated":
                    nc.vector.memset(DEN[:], 0.0).then_inc(s.wt, 1)
                else:
                    dve.wait_ge(s.ex, 1)
                    nc.vector.tensor_tensor(SX[:], EX[:], SEL[:], ALU.mult).then_inc(s.selx, 1)
                    dve.wait_ge(s.selx, 1)
                    nc.vector.tensor_reduce(DEN[:], SX[:] if kind == "swiglu" else EX[:], AXX, ALU.add).then_inc(s.den, 1)
                    dve.wait_ge(s.den, 1)
                    nc.vector.reciprocal(DEN[:], DEN[:]).then_inc(s.rden, 1)
                    dve.wait_ge(s.rden, 1)
                    if shared:
                        dve.wait_ge(s.ex, 2)
                        nc.vector.tensor_copy(WT[:, :, NE], GATE[:])
                    nc.vector.tensor_tensor(WT[:, :, 0:NE], SX[:], bc(DEN[:].unsqueeze(2), [P, NB, NE]), ALU.mult).then_inc(s.wt, 1)
                dve.wait_ge(s.wt, 1)
                if has_b2:
                    dve.wait_ge(s.wtT_ps, 1)
                    for g in range(NG):
                        nc.vector.tensor_copy(WTT[:, g * GT:(g + 1) * GT], PS[0:NE, 4 + g, :]).then_inc(s.wtT, 1)

                def acc_init():
                    for g in range(NG):
                        xg = grp(E.x, g)
                        if has_b2:
                            dve.wait_ge(s.b2_ps, 1)
                            bias = PS[:, M_BANK + g, :].rearrange("p (b d) -> p b d", b=GB)
                            ins = nc.vector.scalar_tensor_tensor(grp(R, g), xg, 2.0 if double else 1.0, bias, ALU.mult, ALU.add)
                        else:
                            ins = nc.vector.tensor_scalar(grp(R, g), xg, 2.0 if double else 1.0, None, ALU.mult)
                    ins.then_inc(s.acc0, 1)

                def hidden(u):
                    e, g = units[u]
                    if u >= 2 and kind in ("gated", "swiglu"):
                        dve.wait_ge(s.y_ps, u - 1)
                    if kind == "gated":
                        for j in range(2):
                            k = 2 * u + j
                            dve.wait_ge(s.h_ps, first[u] + 2 * j + 2)
                            dve.wait_ge(s.act_done, k + 1)
                            nc.vector.tensor_tensor(HT[:, u % 2, j, :], PS[:, (first[u] + 2 * j + 1) % 4, :], T1[:, k % 2, :],
                                                    ALU.mult).then_inc(s.dve_h, 1)
                        dve.wait_ge(s.dve_h, 2 * u + 2)
                        dve.sem_inc(s.hid, 1)
                    elif kind == "silu" and e == NE:
                        dve.wait_ge(s.y_ps, u - 1)
                        dve.wait_ge(s.h_ps, first[u] + 2)
                        dve.wait_ge(s.act_done, u + 1)
                        nc.vector.tensor_tensor(HT[:, u % 2, 0, :], PS[:, (first[u] + 1) % 4, :], T1[:, g, :], ALU.mult).then_inc(s.dve_h, 1)
                        dve.wait_ge(s.dve_h, g + 1)
                        dve.sem_inc(s.hid, 1)
                    elif kind == "swiglu":
                        for j in range(2):
                            k = 2 * u + j
                            q = first[u] + 2 * j
                            dve.wait_ge(s.h_ps, q + 1)
                            if k >= 2:
                                dve.wait_ge(s.gl2, k - 1)
                            nc.vector.tensor_scalar(T1[:, k % 2, :], PS[:, q % 4, :], b1p[:, e, j:j + 1], 7.0,
                                                    ALU.add, ALU.min).then_inc(s.glu, 1)
                            dve.wait_ge(s.glu, k + 1)
                            dve.sem_inc(s.dve_h, 1)
                            dve.wait_ge(s.h_ps, q + 2)
                            nc.vector.tensor_scalar(T3[:, k % 2, :], PS[:, (q + 1) % 4, :], W.b1lin[:, e, j:j + 1], 8.0,
                                                    ALU.add, ALU.min).then_inc(s.dve_h, 1)
                        for j in range(2):
                            k = 2 * u + j
                            dve.wait_ge(s.gs, k + 1)
                            dve.wait_ge(s.dve_h, 2 * k + 2)
                            nc.vector.scalar_tensor_tensor(HT[:, u % 2, j, :], T3[:, k % 2, :], -6.0, T1[:, k % 2, :],
                                                           ALU.max, ALU.mult).then_inc(s.gl2, 1)
                        dve.wait_ge(s.gl2, 2 * u + 2)
                        dve.sem_inc(s.hid, 1)

                def combine(u):
                    e, g = units[u]
                    dve.wait_ge(s.y_ps, u + 1)
                    dve.wait_ge(s.acc, u - 1) if u >= 2 else dve.wait_ge(s.acc0, 1)
                    for b in range(GB):
                        t = g * GB + b
                        ins = nc.vector.scalar_tensor_tensor(R[:, t, :], PS[:, 4 + u % 2, b * P:(b + 1) * P], WT[:, t, e:e + 1],
                                                             R[:, t, :], ALU.mult, ALU.add)
                    ins.then_inc(s.acc, 1)

                acc_init()
                for u in range(U + 1):
                    if u < U:
                        hidden(u)
                    if u > 0:
                        combine(u - 1)
                dve.wait_ge(s.acc, U)
                for g in range(NG):
                    dve_layernorm(nc, dve, E, s, g, grp(R, g), grp(E.x, g))


def l0_ffn(nc, E): moe(nc, E, "swiglu")
def l1_ffn(nc, E): moe(nc, E, "silu")
def l2_ffn(nc, E): moe(nc, E, "gelu")
def l3_ffn(nc, E): moe(nc, E, "gated")


def l1_attn(nc, E):
    W, PS = E.w, E.ps
    H, D = 16, 8
    with sublayer(nc, "xt_ps xt qk_ps v_ps neg pos ex q v kv_ps kvm ks kvd n_ps den rz zn zt_ps zt o_ps res" + LN) as (s, ctx):
        sb = E.scratch(ctx)
        NEGP = sb("NEG", [P, 2 * NG, GT]); Q = sb("Q", [P, 2 * NG, GT])
        V = sb("V", [P, NB, P + 1])
        KVD = sb("KVD", [P, 2, P + H]); KS = sb("KS", [P, NB]); DEN = sb("DEN", [P, 2, H]); RZ = sb("RZ", [P, 2, H])
        ZN = sb("ZN", [P, 2, P]); ZT = sb("ZT", [P, 2, P]); R = sb("R", [P, NB, P])
        with nc.Block() as block:
            @block.tensor
            def _(pe):
                for g in range(NG):
                    pe_transpose4(nc, [E.x[:, g * GB + b, :] for b in range(GB)], PS[:, g, :], E.ident).then_inc(s.xt_ps, 1)
                for g in range(NG):
                    pe.wait_ge(s.xt, g + 1)
                    nc.tensor.matmul(PS[:, 2 + g, :], W.wq, E.xt[:, g * GT:(g + 1) * GT], start=True, stop=True).then_inc(s.qk_ps, 1)
                for g in range(NG):
                    for w, b0, bank, sem in ((W.wk, W.bk, 4 + g, s.qk_ps), (W.wv, W.bv, 6 + g, s.v_ps)):
                        for b in range(GB):
                            o = PS[:, bank, b * P:(b + 1) * P]
                            nc.tensor.matmul(o, E.xt[:, (g * GB + b) * P:(g * GB + b + 1) * P], w, start=True, stop=False)
                            ins = nc.tensor.matmul(o, E.ones_row[0:1, :], b0, start=False, stop=True)
                        ins.then_inc(sem, 1)

                def summary(t):
                    if t % GB == 0:
                        pe.wait_ge(s.q, NG + t // GB + 1)
                        pe.wait_ge(s.v, t // GB + 1)
                    if t >= 2:
                        pe.wait_ge(s.ks, t - 1)
                    nc.tensor.matmul(PS[:, t % 2, 0:P + 1], Q[:, NG + t // GB, (t % GB) * P:(t % GB + 1) * P], V[:, t, :],
                                     start=True, stop=True).then_inc(s.kv_ps, 1)

                def read_out(t):
                    pe.wait_ge(s.kvd, t + 1)
                    if t >= 2:
                        pe.wait_ge(s.zn, t - 1)
                    nc.tensor.matmul(PS[:, 2 + t % 2, 0:P + H], Q[:, t // GB, (t % GB) * P:(t % GB + 1) * P], KVD[:, t % 2, :],
                                     start=True, stop=True).then_inc(s.n_ps, 1)

                def project(t):
                    pe.wait_ge(s.zn, t + 1)
                    if t >= 2:
                        pe.wait_ge(s.res, t - 1)
                    else:
                        pe.wait_ge(s.q, 2 * NG)
                    nc.tensor.transpose(PS[:, 4 + t % 2, 0:P], ZN[:, t % 2, :], E.ident).then_inc(s.zt_ps, 1)
                    pe.wait_ge(s.zt, t + 1)
                    o = PS[:, 4 + t % 2, P:2 * P]
                    nc.tensor.matmul(o, ZT[:, t % 2, :], W.wo, start=True, stop=False)
                    nc.tensor.matmul(o, E.ones_row[0:1, :], W.bo, start=False, stop=True).then_inc(s.o_ps, 1)

                for t in range(NB + 2):
                    if t < NB:
                        summary(t)
                    if 1 <= t <= NB:
                        read_out(t - 1)
                    if t >= 2:
                        project(t - 2)

            @block.scalar
            def _(act):
                for g in range(NG):
                    act.wait_ge(s.xt_ps, g + 1)
                    nc.scalar.copy(E.xt[:, g * GT:(g + 1) * GT], PS[:, g, :]).then_inc(s.xt, 1)
                for c in range(2 * NG):
                    act.wait_ge(s.neg, c + 1)
                    nc.scalar.activation(NEGP[:, c, :], NEGP[:, c, :], ACT.Exp).then_inc(s.ex, 1)
                for g in range(NG):
                    act.wait_ge(s.v_ps, g + 1)
                    nc.scalar.copy(V[:, g * GB:(g + 1) * GB, 0:P], PS[:, 6 + g, :].rearrange("p (b d) -> p b d", b=GB)).then_inc(s.v, 1)
                for t in range(NB):
                    act.wait_ge(s.zt_ps, t + 1)
                    nc.scalar.copy(ZT[:, t % 2, :], PS[:, 4 + t % 2, 0:P]).then_inc(s.zt, 1)
                for g in range(NG):
                    act_layernorm(nc, act, E, s, g)

            @block.gpsimd
            def _(pool):
                nc.gpsimd.memset(V[:, :, P:P + 1], 1.0)
                for c in range(2 * NG):
                    pool.wait_ge(s.ex, c + 1)
                    pool.wait_ge(s.pos, c + 1)
                    nc.gpsimd.tensor_tensor(Q[:, c, :], Q[:, c, :], NEGP[:, c, :], ALU.add).then_inc(s.q, 1)

            @block.vector
            def _(dve):
                for c in range(2 * NG):
                    dve.wait_ge(s.qk_ps, c + 1)
                    b = W.bq if c < NG else 0.0
                    nc.vector.tensor_scalar(NEGP[:, c, :], PS[:, 2 + c, :], b, 0.0, ALU.add, ALU.min).then_inc(s.neg, 1)
                    nc.vector.tensor_scalar(Q[:, c, :], PS[:, 2 + c, :], b, 0.0, ALU.add, ALU.max).then_inc(s.pos, 1)

                def mask_summary(t):
                    dve.wait_ge(s.kv_ps, t + 1)
                    if t >= 2:
                        dve.wait_ge(s.n_ps, t - 1)
                    nc.vector.tensor_tensor(KVD[:, t % 2, 0:P], PS[:, t % 2, 0:P], E.blockmask, ALU.mult)
                    nc.vector.tensor_scalar(KS[:, t:t + 1], PS[:, t % 2, P:P + 1], 1e-6, None, ALU.add).then_inc(s.ks, 1)
                    dve.wait_ge(s.ks, t + 1)
                    nc.vector.tensor_scalar(KVD[:, t % 2, P:P + H], E.headmask, KS[:, t:t + 1], None, ALU.mult).then_inc(s.kvd, 1)

                def normalise(t):
                    dve.wait_ge(s.n_ps, t + 1)
                    n = PS[:, 2 + t % 2, :]
                    nc.vector.tensor_scalar(DEN[:, t % 2, :], n[:, P:P + H], 1e-6, None, ALU.add).then_inc(s.den, 1)
                    dve.wait_ge(s.den, t + 1)
                    nc.vector.reciprocal(RZ[:, t % 2, :], DEN[:, t % 2, :]).then_inc(s.rz, 1)
                    dve.wait_ge(s.rz, t + 1)
                    if t >= 2:
                        dve.wait_ge(s.zt_ps, t - 1)
                    nc.vector.tensor_tensor(ZN[:, t % 2, :].rearrange("p (h d) -> p h d", d=D), n[:, 0:P].rearrange("p (h d) -> p h d", d=D),
                                            bc(RZ[:, t % 2, :].unsqueeze(2), [P, H, D]), ALU.mult).then_inc(s.zn, 1)

                for t in range(NB + 2):
                    if t < NB:
                        mask_summary(t)
                    if 1 <= t <= NB:
                        normalise(t - 1)
                    if t >= 2:
                        u = t - 2
                        dve.wait_ge(s.o_ps, u + 1)
                        nc.vector.tensor_tensor(R[:, u, :], PS[:, 4 + u % 2, P:2 * P], E.x[:, u, :], ALU.add).then_inc(s.res, 1)
                dve.wait_ge(s.res, NB)
                for g in range(NG):
                    dve_layernorm(nc, dve, E, s, g, grp(R, g), grp(E.x, g))


def xattn16(nc, E):
    W, PS = E.w, E.ps
    H, D = 16, 8
    CG = GB * L
    S = P + D
    with sublayer(nc, "xt_ps xt q_ps q k_ps k v_ps v vz vb pz kd rb s_ps mx sub ex sm rz nm pt_ps pt zt_ps zt o_ps res" + LN) as (s, ctx):
        sb = E.scratch(ctx)
        QT = sb("QT", [P, NG, GT]); KT = sb("KT", [P, NB, L]); VA = sb("VA", [L, NB, P]); VB = sb("VB", [P, 2, H * S])
        KD = sb("KD", [P, 2, H, L]); MX = sb("MX", [P, 2, H]); SM = sb("SM", [P, 3, H, L])
        PT = sb("PT", [P, 2, H, P]); SU = sb("SU", [P, 2, H]); RZ = sb("RZ", [P, 2, H]); ZT = sb("ZT", [P, 2, P])
        XB = E.r
        with nc.Block() as block:
            @block.tensor
            def _(pe):
                for g in range(NG):
                    nc.tensor.matmul(PS[:, 2 + g, 0:CG], W.wk, E.ctxT[:, g * GB:(g + 1) * GB, :].rearrange("c b l -> c (b l)"),
                                     start=True, stop=True).then_inc(s.k_ps, 1)
                    for b in range(GB):
                        ins = nc.tensor.matmul(PS[0:L, 4 + g, b * P:(b + 1) * P], E.ctxT[:, g * GB + b, :], W.wv, start=True, stop=True)
                    ins.then_inc(s.v_ps, 1)
                for g in range(NG):
                    pe_transpose4(nc, [E.x[:, g * GB + b, :] for b in range(GB)], PS[:, g, :], E.ident).then_inc(s.xt_ps, 1)
                for g in range(NG):
                    pe.wait_ge(s.xt, g + 1)
                    nc.tensor.matmul(PS[:, 6 + g, :], W.wq, E.xt[:, g * GT:(g + 1) * GT], start=True, stop=True).then_inc(s.q_ps, 1)

                def scores(t):
                    pe.wait_ge(s.kd, t + 1)
                    if t % GB == 0:
                        pe.wait_ge(s.q, t // GB + 1)
                    if t >= 1:
                        pe.wait_ge(s.sub, t)
                    else:
                        pe.wait_ge(s.k, NG)
                        pe.wait_ge(s.xt, NG)
                    for a in range(4):
                        ins = nc.tensor.matmul(PS[:, a, 0:4 * L], QT[:, t // GB, (t % GB) * P:(t % GB + 1) * P],
                                               KD[:, t % 2, 4 * a:4 * a + 4, :].rearrange("p h l -> p (h l)"), start=True, stop=True)
                    ins.then_inc(s.s_ps, 1)

                def mix(t):
                    pe.wait_ge(s.nm, t + 1)
                    pe.wait_ge(s.vb, t + 1)
                    for a in range(5):
                        if a < 4:
                            k = 4 * t + a
                            if k >= 2:
                                pe.wait_ge(s.pt, k - 1)
                            else:
                                pe.wait_ge(s.v, k + 1)
                            for h in range(4):
                                ins = nc.tensor.transpose(PS[0:L, 4 + k % 2, h * P:(h + 1) * P], SM[:, t % 3, 4 * a + h, :], E.ident)
                            ins.then_inc(s.pt_ps, 1)
                        if a == 0:
                            if t < 2:
                                pe.wait_ge(s.q, NG)
                            else:
                                pe.wait_ge(s.res, t - 1)
                        else:
                            pe.wait_ge(s.pt, 4 * t + a)
                            for h in range(4 * a - 4, 4 * a):
                                ins = nc.tensor.matmul(PS[:, 6 + t % 2, 0:P], VB[:, t % 2, h * P:(h + 1) * P], PT[:, t % 2, h, :],
                                                       start=h == 0, stop=h == H - 1)
                    ins.then_inc(s.zt_ps, 1)

                def project(t):
                    pe.wait_ge(s.zt, t + 1)
                    nc.tensor.matmul(PS[:, 6 + t % 2, P:2 * P], ZT[:, t % 2, :], W.wo, start=True, stop=True).then_inc(s.o_ps, 1)

                for i in range(NB + 3):
                    if i < NB:
                        scores(i)
                    if i >= 3:
                        project(i - 3)
                    if 2 <= i < NB + 2:
                        mix(i - 2)

            @block.scalar
            def _(act):
                for g in range(NG):
                    act.wait_ge(s.xt_ps, g + 1)
                    nc.scalar.copy(E.xt[:, g * GT:(g + 1) * GT], PS[:, g, :]).then_inc(s.xt, 1)
                for g in range(NG):
                    act.wait_ge(s.q_ps, g + 1)
                    nc.scalar.activation(QT[:, g, :], PS[:, 6 + g, :], ACT.Identity, bias=W.bq).then_inc(s.q, 1)
                act.wait_ge(s.pz, 1)
                for i in range(NB + 2):
                    if i >= 2:
                        t = i - 2
                        for a in range(4):
                            k = 4 * t + a
                            act.wait_ge(s.pt_ps, k + 1)
                            if a == 0 and t >= 2:
                                act.wait_ge(s.zt_ps, t - 1)
                            nc.scalar.copy(PT[0:L, t % 2, 4 * a:4 * a + 4, :].rearrange("p h q -> p (h q)"), PS[0:L, 4 + k % 2, :]).then_inc(s.pt, 1)
                    if i < NB:
                        act.wait_ge(s.sub, i + 1)
                        nc.scalar.activation(SM[:, i % 3], SM[:, i % 3], ACT.Exp, scale=float(D) ** -0.5).then_inc(s.ex, 1)
                    if i >= 2:
                        act.wait_ge(s.zt_ps, t + 1)
                        if t >= 2:
                            act.wait_ge(s.o_ps, t - 1)
                        nc.scalar.copy(ZT[:, t % 2, :], PS[:, 6 + t % 2, 0:P]).then_inc(s.zt, 1)
                for g in range(NG):
                    act_layernorm(nc, act, E, s, g)

            @block.gpsimd
            def _(pool):
                def keys(t):
                    pool.wait_ge(s.k, t // GB + 1)
                    if t >= 2:
                        pool.wait_ge(s.s_ps, t - 1)
                    nc.gpsimd.tensor_tensor(KD[:, t % 2], bc(KT[:, t, :].unsqueeze(1), [P, H, L]),
                                            bc(E.headmask[:].unsqueeze(2), [P, H, L]), ALU.mult).then_inc(s.kd, 1)

                keys(0)
                keys(1)
                nc.gpsimd.memset(VB[:], 0.0).then_inc(s.vz, 1)
                nc.gpsimd.tensor_tensor(XB[:], E.x[:], bc(W.bo.unsqueeze(1), [P, NB, P]), ALU.add).then_inc(s.rb, 1)
                pool.wait_ge(s.vz, 1)
                for t in range(NB):
                    pool.wait_ge(s.v, t // GB + 1)
                    if t >= 2:
                        pool.wait_ge(s.zt_ps, t - 1)
                    nc.gpsimd.tensor_copy(VB[0:L, t % 2, :].rearrange("k (h s) -> k h s", s=S)[:, :, 0:D],
                                          VA[:, t, :].rearrange("k (h d) -> k h d", d=D)).then_inc(s.vb, 1)
                    pool.wait_ge(s.rz, t + 1)
                    nc.gpsimd.tensor_tensor(SM[:, t % 3], SM[:, t % 3], bc(RZ[:, t % 2, :].unsqueeze(2), [P, H, L]), ALU.mult).then_inc(s.nm, 1)
                    if t + 2 < NB:
                        keys(t + 2)

            @block.vector
            def _(dve):
                for g in range(NG):
                    dve.wait_ge(s.k_ps, g + 1)
                    nc.vector.tensor_scalar(KT[:, g * GB:(g + 1) * GB, :].rearrange("p b l -> p (b l)"), PS[:, 2 + g, 0:CG], W.bk, None,
                                            ALU.add).then_inc(s.k, 1)
                    dve.wait_ge(s.v_ps, g + 1)
                    nc.vector.tensor_tensor(VA[:, g * GB:(g + 1) * GB, :], PS[0:L, 4 + g, :].rearrange("p (b n) -> p b n", n=P),
                                            bc(W.bv[0:L].unsqueeze(1), [L, GB, P]), ALU.add).then_inc(s.v, 1)
                nc.vector.memset(PT[64:P], 0.0).then_inc(s.pz, 1)

                for i in range(NB + 3):
                    if i < NB:
                        sc = PS[:, 0:4, 0:4 * L].rearrange("p a (h l) -> p a h l", l=L)
                        dve.wait_ge(s.s_ps, i + 1)
                        nc.vector.tensor_reduce(MX[:, i % 2, :].rearrange("p (a h) -> p a h", a=4), sc, AXX, ALU.max).then_inc(s.mx, 1)
                        dve.wait_ge(s.mx, i + 1)
                        if i >= 3:
                            dve.wait_ge(s.pt_ps, 4 * (i - 2))
                        nc.vector.tensor_tensor(SM[:, i % 3].rearrange("p (a h) l -> p a h l", a=4), sc,
                                                bc(MX[:, i % 2, :].rearrange("p (a h) -> p a h", a=4).unsqueeze(3), [P, 4, 4, L]),
                                                ALU.subtract).then_inc(s.sub, 1)
                    if i >= 3:
                        t = i - 3
                        dve.wait_ge(s.o_ps, t + 1)
                        if t == 0:
                            dve.wait_ge(s.rb, 1)
                        nc.vector.tensor_tensor(XB[:, t, :], PS[:, 6 + t % 2, P:2 * P], XB[:, t, :], ALU.add).then_inc(s.res, 1)
                    if i < NB:
                        t = i
                        dve.wait_ge(s.ex, t + 1)
                        nc.vector.tensor_reduce(SU[:, t % 2, :], SM[:, t % 3], AXX, ALU.add).then_inc(s.sm, 1)
                        dve.wait_ge(s.sm, t + 1)
                        if t >= 2:
                            dve.wait_ge(s.nm, t - 1)
                        nc.vector.reciprocal(RZ[:, t % 2, :], SU[:, t % 2, :]).then_inc(s.rz, 1)
                dve.wait_ge(s.res, NB)
                for g in range(NG):
                    dve_layernorm(nc, dve, E, s, g, grp(XB, g), grp(E.x, g))


def l1_xattn(nc, E): xattn16(nc, E)
def l3_xattn(nc, E): xattn16(nc, E)


LN_MIN = math.log(1e-6)


def l2_attn(nc, E):
    gla(nc, E)
    ffn(nc, E)


def gla(nc, E):
    W, PS = E.w, E.ps
    H, D, C = 16, 64, 64
    HD = H * D
    NJ = HD // P
    ORDER = []
    for c in range(-2, NB):
        for n, t in (("G", c + 2), ("QD", c), ("Q", c + 2), ("QT", c + 1), ("S1", c), ("K", c + 2), ("e", c + 2), ("KT", c + 1),
                     ("ES", c + 1), ("O", c), ("l", c + 2), ("DF", c + 1), ("r", c + 2), ("V", c + 2), ("OT", c), ("SC", c + 1), ("OUT", c)):
            if 0 <= t < NB:
                ORDER.append((n, t))
    UNITS = [u for u in ORDER if u[0].isupper()]
    POS = {u: k for k, u in enumerate(UNITS)}

    with sublayer(nc, "xt_ps xt xn zero pair gb u eg lg la lm sq qc kc ssq ssm lss rn qn kn v0 v1 exs kqd rt dece dec qt kt qdt at s1 oe ot res" + LN) as (s, ctx):
        sb = E.scratch(ctx)
        XN = sb("XN", [P, NB, P])
        LA = sb("LA", [P, 2, HD]); QN = sb("QN", [P, 2, HD]); KN = sb("KN", [P, 2, HD])
        V0 = sb("V0", [P, 2, HD])
        RH = sb("RH", [P, 2, H, D])
        SQ = sb("SQ", [P, 2, HD]); SS = sb("SS", [P, 2, 2, H]); RN = sb("RN", [P, 2, 2, H])
        LM = sb("LM", [P, 2, H]); EX = sb("EX", [P, HD]); KQ = sb("KQ", [P, HD])
        RT = sb("RT", [P, H, C]); DEC = sb("DEC", [P, H, C])
        QB = sb("QB", [P, NJ, 2, 2, C])
        KNT = sb("KNT", [P, NJ, P])
        AT0 = sb("AT0", [P, H, C]); LH = sb("LH", [P, H, C])
        O = sb("O", [P, HD]); OT = sb("OT", [P, NJ, P])
        freed = {"G": s.gb, "Q": s.qc, "K": s.kc, "V": s.v1, "ES": s.exs, "DF": s.dece, "QT": s.qt, "KT": s.kt, "QD": s.qdt,
                 "SC": s.at, "S1": s.s1, "O": s.oe, "OT": s.ot, "OUT": s.res}

        def pair(u):
            k = POS[u]
            return PS[:, 2 * (k % 4):2 * (k % 4) + 2, :].rearrange("p a n -> p (a n)")

        def ready(eng, u):
            eng.wait_ge(s.pair, POS[u] + 1)

        with nc.Block() as block:
            @block.tensor
            def _(pe):
                for g in range(NG):
                    pe.wait_ge(s.xn, g + 1)
                    pe_transpose4(nc, [XN[:, g * GB + b, :] for b in range(GB)], PS[:, g, :], E.ident).then_inc(s.xt_ps, 1)
                pe.wait_ge(s.xt, NG)
                for k, (n, t) in enumerate(UNITS):
                    if k >= 4:
                        m, tm = UNITS[k - 4]
                        pe.wait_ge(freed[m], tm + 1)
                    pr = pair((n, t))
                    if n in "GQKV":
                        w = {"G": W.wg, "Q": W.wq, "K": W.wk, "V": W.wv}[n]
                        for a in range(2):
                            ins = nc.tensor.matmul(pr[:, a * 512:(a + 1) * 512], E.xt[:, t * P:(t + 1) * P], w[:, a * 512:(a + 1) * 512],
                                                   start=True, stop=True)
                    elif n in ("QT", "KT"):
                        pe.wait_ge(s.qn if n == "QT" else s.kn, t + 1)
                        src = (QN if n == "QT" else KN)[:, t % 2, :]
                        for j in range(NJ):
                            ins = nc.tensor.transpose(pr[:, j * P:(j + 1) * P], src[:, j * P:(j + 1) * P], E.ident)
                    elif n == "ES":
                        pe.wait_ge(s.la, t + 1)
                        for a in range(2):
                            ins = nc.tensor.matmul(pr[:, a * 512:(a + 1) * 512], E.gla_sum, LA[:, t % 2, a * 512:(a + 1) * 512], start=True, stop=True)
                    elif n == "DF":
                        pe.wait_ge(s.rt, t + 1)
                        rt = RT[:].rearrange("p h c -> p (h c)")
                        for a in range(2):
                            ins = nc.tensor.matmul(pr[:, a * 512:(a + 1) * 512], E.gla_after, rt[:, a * 512:(a + 1) * 512], start=True, stop=True)
                    elif n == "SC":
                        pe.wait_ge(s.qt, t + 1)
                        pe.wait_ge(s.kt, t + 1)
                        for j in range(NJ):
                            for c in range(2):
                                ins = nc.tensor.matmul(pr[c * C:(c + 1) * C, j * P:(j + 1) * P], KNT[:, j, c * C:(c + 1) * C],
                                                       QB[:, j, c].rearrange("p o q -> p (o q)"), start=True, stop=True)
                    elif n == "QD":
                        pe.wait_ge(s.kqd, 2 * t + 2)
                        for h in range(H):
                            ins = nc.tensor.transpose(pr[0:D, h * C:(h + 1) * C], KQ[C:P, h * D:(h + 1) * D], E.ident[C:P, C:P])
                    elif n == "S1":
                        pe.wait_ge(s.v0, t + 1)
                        for h in range(H):
                            ins = nc.tensor.matmul(pr[0:D, h * D:(h + 1) * D], KQ[:, h * D:(h + 1) * D], V0[:, t % 2, h * D:(h + 1) * D],
                                                   start=True, stop=True)
                    elif n == "O":
                        pe.wait_ge(s.at, t + 1)
                        pe.wait_ge(s.qdt, t + 1)
                        pe.wait_ge(s.s1, t + 1)
                        pe.wait_ge(s.v1, t + 1)
                        for h in range(H):
                            nc.tensor.matmul(pr[0:C, h * D:(h + 1) * D], AT0[:, h, :], V0[:, t % 2, h * D:(h + 1) * D], start=True, stop=True)
                            ins = nc.tensor.matmul(pr[C:P, h * D:(h + 1) * D], LH[:, h, :], RH[:, t % 2, h, :], start=True, stop=True)
                    elif n == "OT":
                        pe.wait_ge(s.oe, t + 1)
                        for j in range(NJ):
                            ins = nc.tensor.transpose(pr[:, j * P:(j + 1) * P], O[:, j * P:(j + 1) * P], E.ident)
                    else:
                        pe.wait_ge(s.ot, t + 1)
                        for j in range(NJ):
                            ins = nc.tensor.matmul(pr[:, 0:P], OT[:, j, :], W.wo[:, j, :], start=j == 0, stop=j == NJ - 1)
                    ins.then_inc(s.pair, 1)

            @block.scalar
            def _(act):
                for g in range(NG):
                    act_layernorm(nc, act, E, s, g)
                for g in range(NG):
                    act.wait_ge(s.xt_ps, g + 1)
                    nc.scalar.copy(E.xt[:, g * GT:(g + 1) * GT], PS[:, g, :]).then_inc(s.xt, 1)
                act.wait_ge(s.zero, 1)
                for n, t in ORDER:
                    p = t % 2
                    if n.isupper():
                        pr = pair((n, t))
                    if n in ("Q", "K"):
                        i = 2 * t + (n == "K")
                        ready(act, (n, t))
                        if i >= 2:
                            act.wait_ge(s.ssq, i - 1)
                        nc.scalar.activation(SQ[:, i % 2], pr, ACT.Square).then_inc(s.sq, 1)
                    elif n == "e":
                        act.wait_ge(s.u, t + 1)
                        nc.scalar.activation(LA[:, p], LA[:, p], ACT.Exp, scale=-1.0).then_inc(s.eg, 1)
                    elif n == "l":
                        act.wait_ge(s.eg, t + 1)
                        nc.scalar.activation(LA[:, p], LA[:, p], ACT.Ln, bias=E.one[:]).then_inc(s.lg, 1)
                        act.wait_ge(s.ssm, t + 1)
                        nc.scalar.activation(SS[:, p], SS[:, p], ACT.Ln, scale=2.0 ** 40).then_inc(s.lss, 1)
                    elif n == "r":
                        act.wait_ge(s.lss, t + 1)
                        if t >= 2:
                            act.wait_ge(s.kn, t - 1)
                        nc.scalar.activation(RN[:, p], SS[:, p], ACT.Exp, scale=-0.5, bias=E.ln2_20[:]).then_inc(s.rn, 1)
                    elif n == "V":
                        ready(act, (n, t))
                        if t >= 2:
                            ready(act, ("O", t - 2))
                        nc.scalar.copy(V0[0:C, p], pr[0:C, :]).then_inc(s.v0, 1)
                        nc.scalar.copy(RH[C:P, p].rearrange("c h e -> c (h e)"), pr[C:P, :]).then_inc(s.v1, 1)
                    elif n == "QT":
                        ready(act, (n, t))
                        if t:
                            ready(act, ("SC", t - 1))
                        for o in range(2):
                            ins = nc.scalar.copy(QB[o * D:(o + 1) * D, :, :, o, :], pr[o * D:(o + 1) * D, :].rearrange("p (j c q) -> p j c q", c=2, q=C))
                        ins.then_inc(s.qt, 1)
                    elif n == "ES":
                        ready(act, (n, t))
                        if t:
                            act.wait_ge(s.kqd, 2 * t)
                        nc.scalar.activation(EX[:], pr, ACT.Exp).then_inc(s.exs, 1)
                    elif n == "DF":
                        ready(act, (n, t))
                        if t:
                            act.wait_ge(s.at, t)
                        nc.scalar.activation(DEC[:].rearrange("p h c -> p (h c)"), pr, ACT.Exp).then_inc(s.dece, 1)
                    elif n == "QD":
                        ready(act, (n, t))
                        if t:
                            ready(act, ("O", t - 1))
                        nc.scalar.copy(LH[0:D].rearrange("p h c -> p (h c)"), pr[0:D, :]).then_inc(s.qdt, 1)
                    elif n == "O":
                        ready(act, (n, t))
                        if t:
                            ready(act, ("OT", t - 1))
                        nc.scalar.copy(O[:], pr).then_inc(s.oe, 1)

            @block.gpsimd
            def _(pool):
                nc.gpsimd.memset(QB[:], 0.0)
                nc.gpsimd.memset(V0[:], 0.0)
                nc.gpsimd.memset(AT0[:], 0.0).then_inc(s.zero, 1)
                for n, t in ORDER:
                    p = t % 2
                    if n == "QT":
                        pool.wait_ge(s.lm, t + 1)
                        if t:
                            ready(pool, ("DF", t - 1))
                        nc.gpsimd.tensor_tensor(RT[:], bc(LM[:, p].unsqueeze(2), [P, H, C]), bc(E.gla_upto.unsqueeze(1), [P, H, C]), ALU.mult).then_inc(s.rt, 1)
                    elif n == "ES":
                        pool.wait_ge(s.exs, t + 1)
                        pool.wait_ge(s.kn, t + 1)
                        if t:
                            ready(pool, ("S1", t - 1))
                        pool.wait_ge(s.rt, t + 1)
                        nc.gpsimd.tensor_tensor(KQ[C:P], QN[C:P, p], EX[C:P], ALU.mult).then_inc(s.kqd, 1)
                        pool.wait_ge(s.kqd, 2 * t + 1)
                        nc.gpsimd.tensor_tensor(KQ[0:C], KN[0:C, p], EX[0:C], ALU.mult).then_inc(s.kqd, 1)
                    elif n == "DF":
                        pool.wait_ge(s.dece, t + 1)
                        nc.gpsimd.tensor_tensor(DEC[:], DEC[:], bc(E.gla_tril.unsqueeze(1), [P, H, C]), ALU.mult).then_inc(s.dec, 1)
                    elif n == "r":
                        pool.wait_ge(s.rn, t + 1)
                        for i, (buf, raw, done) in enumerate(((QN, s.qc, s.qn), (KN, s.kc, s.kn))):
                            pool.wait_ge(raw, t + 1)
                            x = buf[:, p].rearrange("p (h d) -> p h d", d=D)
                            nc.gpsimd.tensor_tensor(x, x, bc(RN[:, p, i, :].unsqueeze(2), [P, H, D]), ALU.mult).then_inc(done, 1)

            @block.vector
            def _(dve):
                for g in range(NG):
                    dve_layernorm(nc, dve, E, s, g, grp(E.x, g), grp(XN, g), W.ln1w, W.ln1b).then_inc(s.xn, 1)
                for n, t in ORDER:
                    p = t % 2
                    if n.isupper():
                        pr = pair((n, t))
                    if n == "G":
                        ready(dve, (n, t))
                        if t >= 2:
                            ready(dve, ("ES", t - 2))
                            dve.wait_ge(s.lm, t - 1)
                        nc.vector.tensor_tensor(LA[:, p], pr, W.bg, ALU.add).then_inc(s.gb, 1)
                        dve.wait_ge(s.gb, t + 1)
                        nc.vector.tensor_scalar(LA[:, p], LA[:, p], -20.0, None, ALU.max).then_inc(s.u, 1)
                    elif n in ("Q", "K"):
                        i = 2 * t + (n == "K")
                        dve.wait_ge(s.sq, i + 1)
                        if t >= 2:
                            ready(dve, ("KT", t - 2))
                            dve.wait_ge(s.kqd, 2 * (t - 1))
                            dve.wait_ge(s.rn, t - 1)
                        nc.vector.tensor_copy((QN if n == "Q" else KN)[:, p], pr).then_inc(s.qc if n == "Q" else s.kc, 1)
                        nc.vector.tensor_reduce(SS[:, p, i % 2, :], SQ[:, i % 2].rearrange("p (h d) -> p h d", d=D), AXX, ALU.add).then_inc(s.ssq, 1)
                        if n == "K":
                            dve.wait_ge(s.ssq, i + 1)
                            nc.vector.tensor_scalar(SS[:, p], SS[:, p], 1e-24, None, ALU.max).then_inc(s.ssm, 1)
                    elif n == "l":
                        dve.wait_ge(s.lg, t + 1)
                        nc.vector.tensor_scalar(LA[:, p], LA[:, p], -1.0, LN_MIN, ALU.mult, ALU.max).then_inc(s.la, 1)
                    elif n == "r":
                        dve.wait_ge(s.la, t + 1)
                        if t >= 2:
                            dve.wait_ge(s.rt, t - 1)
                        nc.vector.tensor_reduce(LM[:, p], LA[:, p].rearrange("p (h d) -> p h d", d=D), AXX, ALU.add).then_inc(s.lm, 1)
                    elif n == "KT":
                        ready(dve, (n, t))
                        if t:
                            ready(dve, ("SC", t - 1))
                        nc.vector.tensor_copy(KNT[:].rearrange("p j q -> p (j q)"), pr).then_inc(s.kt, 1)
                    elif n == "SC":
                        ready(dve, (n, t))
                        dve.wait_ge(s.dec, t + 1)
                        dve.wait_ge(s.zero, 1)
                        if t:
                            ready(dve, ("O", t - 1))
                        prh = pr.rearrange("p (h c) -> p h c", c=C)
                        nc.vector.tensor_tensor(AT0[0:C], prh[0:C], DEC[0:C], ALU.mult)
                        nc.vector.tensor_tensor(LH[C:P], prh[C:P], DEC[C:P], ALU.mult).then_inc(s.at, 1)
                    elif n == "S1":
                        ready(dve, (n, t))
                        if t >= 2:
                            ready(dve, ("O", t - 2))
                        nc.vector.tensor_copy(RH[0:D, p].rearrange("p h e -> p (h e)"), pr[0:D, :]).then_inc(s.s1, 1)
                    elif n == "OT":
                        ready(dve, (n, t))
                        if t:
                            ready(dve, ("OUT", t - 1))
                        nc.vector.tensor_copy(OT[:].rearrange("p j q -> p (j q)"), pr).then_inc(s.ot, 1)
                    elif n == "OUT":
                        ready(dve, (n, t))
                        nc.vector.tensor_tensor(E.r[:, t, :], pr[:, 0:P], E.x[:, t, :], ALU.add).then_inc(s.res, 1)


def ffn(nc, E, post_norm=False):
    W, PS = E.w, E.ps
    NH = 4
    with sublayer(nc, "xn xt_ps xt h_ps hid y_ps xr res po pr" + LN) as (s, ctx):
        sb = E.scratch(ctx)
        XN = sb("XN", [P, NB, P]); HT = sb("HT", [P, NG, NH, GT]); R = sb("R", [P, NB, P])
        with nc.Block() as block:
            @block.tensor
            def _(pe):
                for g in range(NG):
                    pe.wait_ge(s.xn, g + 1)
                    pe_transpose4(nc, [XN[:, g * GB + b, :] for b in range(GB)], PS[:, 6 + g, :], E.ident).then_inc(s.xt_ps, 1)
                for g in range(NG):
                    pe.wait_ge(s.xt, g + 1)
                    for j in range(NH):
                        k = g * NH + j
                        if k >= 4:
                            pe.wait_ge(s.hid, k - 3)
                        nc.tensor.matmul(PS[:, k % 4, :], W.fw1[:, j * P:(j + 1) * P], E.xt[:, g * GT:(g + 1) * GT], start=True, stop=True).then_inc(s.h_ps, 1)
                for g in range(NG):
                    pe.wait_ge(s.hid, (g + 1) * NH)
                    for b in range(GB):
                        o = PS[:, 4 + g, b * P:(b + 1) * P]
                        for j in range(NH):
                            ins = nc.tensor.matmul(o, HT[:, g, j, b * P:(b + 1) * P], W.fw2[:, j, :], start=j == 0, stop=j == NH - 1)
                    ins.then_inc(s.y_ps, 1)

            @block.scalar
            def _(act):
                for g in range(NG):
                    act_layernorm(nc, act, E, s, g)
                for g in range(NG):
                    act.wait_ge(s.xt_ps, g + 1)
                    nc.scalar.copy(E.xt[:, g * GT:(g + 1) * GT], PS[:, 6 + g, :]).then_inc(s.xt, 1)
                for k in range(NG * NH):
                    act.wait_ge(s.h_ps, k + 1)
                    nc.scalar.activation(HT[:, k // NH, k % NH, :], PS[:, k % 4, :], ACT.Gelu, bias=W.fb1[:, k % NH:k % NH + 1]).then_inc(s.hid, 1)
                for k in range(NG * (2 if post_norm else 1)):
                    act_layernorm(nc, act, E, s, NG + k)

            @block.gpsimd
            def _(pool):
                nc.gpsimd.tensor_tensor(R[:], E.r[:], bc(W.fb2.unsqueeze(1), [P, NB, P]), ALU.add).then_inc(s.xr, 1)
                if not post_norm:
                    pool.wait_ge(s.xr, 1)
                    nc.gpsimd.tensor_tensor(R[:], R[:], E.x[:], ALU.add).then_inc(s.xr, 1)

            @block.vector
            def _(dve):
                for g in range(NG):
                    dve_layernorm(nc, dve, E, s, g, grp(E.r, g), grp(XN, g), W.ln2w, W.ln2b).then_inc(s.xn, 1)
                dve.wait_ge(s.xr, 1 if post_norm else 2)
                for g in range(NG):
                    dve.wait_ge(s.y_ps, g + 1)
                    nc.vector.tensor_tensor(grp(R, g), grp(R, g), PS[:, 4 + g, :].rearrange("p (b d) -> p b d", b=GB), ALU.add).then_inc(s.res, 1)
                    dve.wait_ge(s.res, g + 1)
                    if post_norm:
                        dve_layernorm(nc, dve, E, s, NG + g, grp(R, g), grp(R, g), W.gout, W.bout).then_inc(s.po, 1)
                    else:
                        dve_layernorm(nc, dve, E, s, NG + g, grp(R, g), grp(E.x, g))
                if post_norm:
                    for g in range(NG):
                        dve.wait_ge(s.po, g + 1)
                        nc.vector.tensor_tensor(grp(R, g), grp(R, g), grp(E.x, g), ALU.add).then_inc(s.pr, 1)
                        dve.wait_ge(s.pr, g + 1)
                        dve_layernorm(nc, dve, E, s, 2 * NG + g, grp(R, g), grp(E.x, g))


MAGIC = 1.5 * 2.0 ** 23
TWO_PI_HI = 6.28125
TWO_PI_LO = 2 * math.pi - TWO_PI_HI


def l2_xattn_in(nc, E, prefetch=(), stores=None):
    W, PS = E.w, E.ps
    H, D, TOP = 4, 32, 32
    CG = GB * L
    NRD = TOP // 8
    with sublayer(nc, "xt_ps xt q_ps q k_ps k v_ps v xn tm mb s_ps sc m8 wk sub ex ne nx exn den rden wh aw att at_ps at c_ps ct f_ps f x1 x2 mk w_ld st" + LN) as (s, ctx):
        sb = E.scratch(ctx)
        U = sb("U", [P, NB, P]); FO = sb("FO", [P, NB, 2 * P])
        vmask = sb("vmask", [P, NB, L]); tmask = sb("tmask", [P, NB])
        QT = sb("QT", [P, NG, GT]); KT = sb("KT", [P, NB, L]); V = sb("V", [L, NB, P]); XN = sb("XN", [P, NB, P])
        MB = sb("MB", [P, NB, L]); TM = sb("TM", [P, NB])
        SC = sb("SC", [P, NG, H, GB, L]); WK = sb("WK", [P, H, GB, L]); M8 = sb("M8", [P, NG, NRD, H, GB, 8])
        EX = sb("EX", [P, NG, H, GB, L]); DEN = sb("DEN", [P, NG, H, GB]); WH = sb("WH", [P, NG, H, GB])
        ATT = sb("ATT", [P, NG, GB, L]); ATT_T = sb("ATT_T", [L, NG, GT]); CT = sb("CT", [P, NG, GT])
        F = sb("F", [P, 2, 2 * P])
        with nc.Block() as block:
            @block.sync
            def _(sp):
                for dst, src in prefetch:
                    sp.dma_start(dst, src).then_inc(s.w_ld, 16)
                sp.dma_start(stores[2], E.x[:]).then_inc(s.st, 16)
                sp.wait_ge(s.x2, NB)
                sp.dma_start(stores[0], U[:]).then_inc(s.st, 16)
                sp.dma_start(stores[1], FO[:]).then_inc(s.st, 16)
                sp.wait_ge(s.w_ld, 16 * len(prefetch))
                sp.wait_ge(s.st, 48)

            @block.tensor
            def _(pe):
                for g in range(NG):
                    pe_transpose4(nc, [E.x[:, g * GB + b, :] for b in range(GB)], PS[:, g, :], E.ident).then_inc(s.xt_ps, 1)
                for g in range(NG):
                    nc.tensor.matmul(PS[:, 2 + g, 0:CG], W.wk, E.ctxT[:, g * GB:(g + 1) * GB, :].rearrange("c b l -> c (b l)"),
                                     start=True, stop=True).then_inc(s.k_ps, 1)
                    for b in range(GB):
                        ins = nc.tensor.matmul(PS[0:L, 4 + g, b * P:(b + 1) * P], E.ctxT[:, g * GB + b, :], W.wv, start=True, stop=True)
                    ins.then_inc(s.v_ps, 1)
                for g in range(NG):
                    pe.wait_ge(s.xt, g + 1)
                    nc.tensor.matmul(PS[:, 6 + g, :], W.wq, E.xt[:, g * GT:(g + 1) * GT], start=True, stop=True).then_inc(s.q_ps, 1)
                for g in range(NG):
                    pe.wait_ge(s.q, NG)
                    pe.wait_ge(s.k, NG)
                    pe.wait_ge(s.v, NG)
                    for b in range(GB):
                        for h in range(H):
                            ins = nc.tensor.matmul(PS[:, 4 * g + h, b * L:(b + 1) * L], QT[h * D:(h + 1) * D, g, b * P:(b + 1) * P],
                                                   KT[h * D:(h + 1) * D, g * GB + b, :], start=True, stop=True)
                    ins.then_inc(s.s_ps, 1)
                pe.wait_ge(s.sc, NG)
                for g in range(NG):
                    pe.wait_ge(s.att, g + 1)
                    for b in range(GB):
                        ins = nc.tensor.transpose(PS[0:L, g, b * P:(b + 1) * P], ATT[:, g, b, :], E.ident)
                    ins.then_inc(s.at_ps, 1)
                    pe.wait_ge(s.at, g + 1)
                    for b in range(GB):
                        ins = nc.tensor.matmul(PS[:, 2 + g, b * P:(b + 1) * P], V[:, g * GB + b, :], ATT_T[:, g, b * P:(b + 1) * P],
                                               start=True, stop=True)
                    ins.then_inc(s.c_ps, 1)
                    pe.wait_ge(s.ct, g + 1)
                    for b in range(GB):
                        t = g * GB + b
                        if t >= 4:
                            pe.wait_ge(s.f, t - 3)
                        nc.tensor.matmul(PS[:, 4 + t % 4, :], CT[:, g, b * P:(b + 1) * P], W.wf, start=True, stop=False)
                        nc.tensor.matmul(PS[:, 4 + t % 4, :], E.ones_row[0:1, :], W.bf, start=False, stop=True).then_inc(s.f_ps, 1)

            @block.scalar
            def _(act):
                for g in range(NG):
                    act.wait_ge(s.xt_ps, g + 1)
                    nc.scalar.copy(E.xt[:, g * GT:(g + 1) * GT], PS[:, g, :]).then_inc(s.xt, 1)
                for g in range(NG):
                    act.wait_ge(s.q_ps, g + 1)
                    nc.scalar.copy(QT[:, g, :], PS[:, 6 + g, :]).then_inc(s.q, 1)
                for g in range(NG):
                    act_layernorm(nc, act, E, s, g)
                for g in range(NG):
                    act.wait_ge(s.sub, g + 1)
                    nc.scalar.activation(EX[:, g], EX[:, g], ACT.Exp, scale=float(D) ** -0.5).then_inc(s.ex, 1)
                for g in range(NG):
                    act.wait_ge(s.at_ps, g + 1)
                    nc.scalar.copy(ATT_T[:, g, :], PS[0:L, g, :]).then_inc(s.at, 1)
                    act.wait_ge(s.c_ps, g + 1)
                    nc.scalar.copy(CT[:, g, :], PS[:, 2 + g, :]).then_inc(s.ct, 1)

            @block.gpsimd
            def _(pool):
                for g in range(NG):
                    pool.wait_ge(s.m8, NRD * g + 1)
                    nc.gpsimd.tensor_tensor(EX[:, g], SC[:, g], bc(M8[:, g, 0, :, :, 0:1], [P, H, GB, L]), ALU.subtract).then_inc(s.sub, 1)
                for g in range(NG):
                    pool.wait_ge(s.wh, g + 1)
                    nc.gpsimd.tensor_tensor(EX[:, g], EX[:, g], bc(WH[:, g].unsqueeze(3), [P, H, GB, L]), ALU.mult).then_inc(s.aw, 1)

            @block.vector
            def _(dve):
                for g in range(NG):
                    dve.wait_ge(s.k_ps, g + 1)
                    nc.vector.tensor_copy(KT[:, g * GB:(g + 1) * GB, :].rearrange("p b l -> p (b l)"), PS[:, 2 + g, 0:CG]).then_inc(s.k, 1)
                for g in range(NG):
                    dve.wait_ge(s.v_ps, g + 1)
                    nc.vector.tensor_copy(V[:, g * GB:(g + 1) * GB, :].rearrange("p b d -> p (b d)"), PS[0:L, 4 + g, :]).then_inc(s.v, 1)
                nc.vector.tensor_copy(vmask[:], E.vmask8[:])
                nc.vector.tensor_copy(tmask[:], E.tmask8[:]).then_inc(s.mk, 1)
                dve.wait_ge(s.mk, 1)
                nc.vector.tensor_scalar(MB[:], vmask[:], 1e30, -1e30, ALU.mult, ALU.add).then_inc(s.mb, 1)
                nc.vector.tensor_scalar(TM[:], tmask[:], 1.0 / H, None, ALU.mult).then_inc(s.tm, 1)
                for g in range(NG):
                    dve_layernorm(nc, dve, E, s, g, grp(E.x, g), grp(XN, g), W.gin, W.bin).then_inc(s.xn, 1)
                dve.wait_ge(s.mb, 1)
                for g in range(NG):
                    dve.wait_ge(s.s_ps, g + 1)
                    nc.vector.tensor_tensor(SC[:, g], PS[:, 4 * g:4 * g + 4, 0:CG].rearrange("p h (b l) -> p h b l", b=GB),
                                            bc(MB[:, g * GB:(g + 1) * GB, :].unsqueeze(1), [P, H, GB, L]), ALU.add).then_inc(s.sc, 1)
                for g in range(NG):
                    dve.wait_ge(s.sc, g + 1)
                    if g:
                        dve.wait_ge(s.ne, g)
                    for r in range(NRD):
                        src = SC[:, g] if r == 0 else WK[:]
                        for h in range(H):
                            for b in range(GB):
                                ins = nc.vector.max(M8[:, g, r, h, b, :], src[:, h, b, :])
                        ins.then_inc(s.m8, 1)
                        dve.wait_ge(s.m8, NRD * g + r + 1)
                        for h in range(H):
                            for b in range(GB):
                                ins = nc.vector.match_replace(WK[:, h, b, :], M8[:, g, r, h, b, :], src[:, h, b, :], -3e38)
                        ins.then_inc(s.wk, 1)
                        dve.wait_ge(s.wk, NRD * g + r + 1)
                    dve.wait_ge(s.sub, g + 1)
                    nc.vector.tensor_tensor(SC[:, g], WK[:], SC[:, g], ALU.not_equal).then_inc(s.ne, 1)
                    dve.wait_ge(s.ne, g + 1)
                    dve.wait_ge(s.ex, g + 1)
                    nc.vector.tensor_tensor(EX[:, g], EX[:, g], SC[:, g], ALU.mult).then_inc(s.nx, 1)
                    dve.wait_ge(s.nx, g + 1)
                    nc.vector.tensor_reduce(DEN[:, g], EX[:, g], AXX, ALU.add).then_inc(s.den, 1)
                    dve.wait_ge(s.den, g + 1)
                    nc.vector.reciprocal(DEN[:, g], DEN[:, g]).then_inc(s.rden, 1)
                    dve.wait_ge(s.rden, g + 1)
                    dve.wait_ge(s.tm, 1)
                    nc.vector.tensor_tensor(WH[:, g], DEN[:, g], bc(TM[:, g * GB:(g + 1) * GB].unsqueeze(1), [P, H, GB]), ALU.mult).then_inc(s.wh, 1)
                for g in range(NG):
                    dve.wait_ge(s.aw, g + 1)
                    nc.vector.tensor_reduce(ATT[:, g], EX[:, g].rearrange("p h b l -> p b l h"), AXX, ALU.add).then_inc(s.att, 1)
                dve.wait_ge(s.xn, NG)
                for t in range(NB):
                    f = PS[:, 4 + t % 4, :]
                    dve.wait_ge(s.f_ps, t + 1)
                    if t >= 2:
                        dve.wait_ge(s.x2, t - 1)
                    nc.vector.tensor_scalar(F[:, t % 2, :], f[:, 0:2 * P], W.mg, None, ALU.mult)
                    nc.vector.tensor_scalar(FO[:, t, :], f[:, 2 * P:4 * P], W.mg, None, ALU.mult).then_inc(s.f, 1)
                    dve.wait_ge(s.f, t + 1)
                    nc.vector.scalar_tensor_tensor(U[:, t, :], F[:, t % 2, 0:P], 1.0, XN[:, t, :], ALU.add, ALU.mult).then_inc(s.x1, 1)
                    dve.wait_ge(s.x1, t + 1)
                    nc.vector.tensor_tensor(U[:, t, :], U[:, t, :], F[:, t % 2, P:2 * P], ALU.add).then_inc(s.x2, 1)


def s4d_kernel(nc, E, k_dram):
    W = E.w
    N = 64
    LC = 16
    NCH = P // LC
    with sublayer(nc, "dt dta ph era kk kr r1 r2 rc er sh si co1 co num0 num a2 ra prod dcr m1 m2 d1 w k0 k_st z" ) as (s, ctx):
        sb = E.scratch(ctx)
        DT = sb("DT", [P, 1]); ARE = sb("ARE", [P, N]); AIM = sb("AIM", [P, N])
        PH = sb("PH", [P, 2, LC, N]); KK = sb("KK", [P, 2, LC, N]); RC = sb("RC", [P, 2, LC, N])
        ER = sb("ER", [P, 2, LC, N]); SH = sb("SH", [P, 2, LC, N]); SI = sb("SI", [P, 2, LC, N])
        NR_ = sb("NR", [P, N]); NI = sb("NI", [P, N]); T = [sb(f"T{i}", [P, N]) for i in range(8)]
        KP = sb("KP", [P, 2 * P])
        DCR = sb("DCR", [P, N]); DCI = sb("DCI", [P, N])
        full = [P, LC, N]
        with nc.Block() as block:
            @block.scalar
            def _(act):
                nc.scalar.activation(DT[:], W.log_dt, ACT.Exp).then_inc(s.dt, 1)
                for c in range(NCH):
                    p = c % 2
                    act.wait_ge(s.era, c + 1)
                    nc.scalar.activation(ER[:, p], ER[:, p], ACT.Exp).then_inc(s.er, 1)
                    act.wait_ge(s.rc, c + 1)
                    if c >= 2:
                        act.wait_ge(s.w, c - 1)
                    nc.scalar.activation(SH[:, p], RC[:, p], ACT.Sin, scale=0.5).then_inc(s.sh, 1)
                    nc.scalar.activation(SI[:, p], RC[:, p], ACT.Sin).then_inc(s.si, 1)
                    act.wait_ge(s.sh, c + 1)
                    nc.scalar.activation(SH[:, p], SH[:, p], ACT.Square).then_inc(s.co1, 1)

            @block.gpsimd
            def _(pool):
                for c in range(NCH):
                    p = c % 2
                    pool.wait_ge(s.dta, 2)
                    lt = bc(E.times[:, c * LC:(c + 1) * LC].unsqueeze(2), full)
                    if c >= 2:
                        pool.wait_ge(s.r2, c - 1)
                        pool.wait_ge(s.w, c - 1)
                    nc.gpsimd.tensor_tensor(PH[:, p], bc(AIM[:].unsqueeze(1), full), lt, ALU.mult).then_inc(s.ph, 1)
                    nc.gpsimd.tensor_tensor(ER[:, p], bc(ARE[:].unsqueeze(1), full), lt, ALU.mult).then_inc(s.era, 1)

            @block.vector
            def _(dve):
                v = nc.vector
                v.memset(KP[:, 0:P], 0.0)
                dve.wait_ge(s.dt, 1)
                v.tensor_scalar(ARE[:], W.a_re, DT[:], None, ALU.mult).then_inc(s.dta, 1)
                v.tensor_scalar(AIM[:], W.a_im, DT[:], None, ALU.mult).then_inc(s.dta, 1)

                def reduce_angle(c):
                    p = c % 2
                    dve.wait_ge(s.ph, c + 1)
                    v.tensor_scalar(KK[:, p], PH[:, p], 1.0 / (2 * math.pi), MAGIC, ALU.mult, ALU.add).then_inc(s.kk, 1)
                    dve.wait_ge(s.kk, c + 1)
                    v.tensor_scalar(KK[:, p], KK[:, p], MAGIC, None, ALU.subtract).then_inc(s.kr, 1)
                    dve.wait_ge(s.kr, c + 1)
                    v.scalar_tensor_tensor(PH[:, p], KK[:, p], -TWO_PI_HI, PH[:, p], ALU.mult, ALU.add).then_inc(s.r1, 1)
                    dve.wait_ge(s.r1, c + 1)
                    if c >= 2:
                        dve.wait_ge(s.si, c - 1)
                    v.scalar_tensor_tensor(RC[:, p], KK[:, p], -TWO_PI_LO, PH[:, p], ALU.mult, ALU.add).then_inc(s.r2, 1)
                    dve.wait_ge(s.r2, c + 1)
                    v.tensor_scalar(RC[:, p], RC[:, p], 3.1415925, -3.1415925, ALU.min, ALU.max).then_inc(s.rc, 1)

                def coefficients():
                    er, co, si = ER[:, 0, 1, :], SH[:, 0, 1, :], SI[:, 0, 1, :]
                    n = [0]

                    def link(ins):
                        n[0] += 1
                        ins.then_inc(s.prod, 1)
                        dve.wait_ge(s.prod, n[0])
                    link(v.tensor_tensor(NR_[:], er, co, ALU.mult))
                    link(v.tensor_scalar(NR_[:], NR_[:], 1.0, None, ALU.subtract))
                    link(v.tensor_tensor(NI[:], er, si, ALU.mult))
                    link(v.tensor_tensor(T[0][:], W.a_re, W.a_re, ALU.mult))
                    link(v.tensor_tensor(T[1][:], W.a_im, W.a_im, ALU.mult))
                    link(v.tensor_tensor(T[0][:], T[0][:], T[1][:], ALU.add))
                    link(v.reciprocal(T[0][:], T[0][:]))
                    link(v.tensor_tensor(T[1][:], W.c_re, NR_[:], ALU.mult))
                    link(v.tensor_tensor(T[2][:], W.c_im, NI[:], ALU.mult))
                    link(v.tensor_tensor(T[1][:], T[1][:], T[2][:], ALU.subtract))
                    link(v.tensor_tensor(T[2][:], W.c_re, NI[:], ALU.mult))
                    link(v.tensor_tensor(T[3][:], W.c_im, NR_[:], ALU.mult))
                    link(v.tensor_tensor(T[2][:], T[2][:], T[3][:], ALU.add))
                    link(v.tensor_tensor(T[3][:], T[1][:], W.a_re, ALU.mult))
                    link(v.tensor_tensor(T[4][:], T[2][:], W.a_im, ALU.mult))
                    link(v.tensor_tensor(T[3][:], T[3][:], T[4][:], ALU.add))
                    link(v.tensor_tensor(T[5][:], T[2][:], W.a_re, ALU.mult))
                    link(v.tensor_tensor(T[6][:], T[1][:], W.a_im, ALU.mult))
                    link(v.tensor_tensor(T[5][:], T[5][:], T[6][:], ALU.subtract))
                    link(v.tensor_tensor(DCR[:], T[3][:], T[0][:], ALU.mult))
                    link(v.tensor_tensor(DCI[:], T[5][:], T[0][:], ALU.mult))
                    link(v.tensor_scalar(DCR[:], DCR[:], 2.0, None, ALU.mult))
                    link(v.tensor_scalar(DCI[:], DCI[:], 2.0, None, ALU.mult))

                def accumulate(c):
                    p = c % 2
                    dve.wait_ge(s.co1, c + 1)
                    v.tensor_scalar(SH[:, p], SH[:, p], -2.0, 1.0, ALU.mult, ALU.add).then_inc(s.co, 1)
                    dve.wait_ge(s.co, c + 1)
                    dve.wait_ge(s.er, c + 1)
                    dve.wait_ge(s.si, c + 1)
                    if c == 0:
                        coefficients()
                    v.tensor_tensor(SH[:, p], SH[:, p], bc(DCR[:].unsqueeze(1), full), ALU.mult).then_inc(s.m1, 1)
                    v.tensor_tensor(SI[:, p], SI[:, p], bc(DCI[:].unsqueeze(1), full), ALU.mult).then_inc(s.m2, 1)
                    dve.wait_ge(s.m1, c + 1)
                    dve.wait_ge(s.m2, c + 1)
                    v.tensor_tensor(SH[:, p], SH[:, p], SI[:, p], ALU.subtract).then_inc(s.d1, 1)
                    dve.wait_ge(s.d1, c + 1)
                    v.tensor_tensor(SH[:, p], SH[:, p], ER[:, p], ALU.mult).then_inc(s.num, 1)
                    dve.wait_ge(s.num, c + 1)
                    v.tensor_reduce(KP[:, P + c * LC:P + (c + 1) * LC], SH[:, p], AXX, ALU.add).then_inc(s.w, 1)

                reduce_angle(0)
                for c in range(NCH):
                    if c + 1 < NCH:
                        reduce_angle(c + 1)
                    accumulate(c)
                dve.wait_ge(s.w, NCH)
                v.tensor_tensor(KP[:, P:P + 1], KP[:, P:P + 1], W.dskip, ALU.add).then_inc(s.z, 1)

            @block.sync
            def _(sp):
                sp.wait_ge(s.z, 1)
                sp.dma_start(k_dram, KP[:]).then_inc(s.k_st, 16)
                sp.wait_ge(s.k_st, 16)


def s4d_conv(nc, E, k_dram, u_dram, y_dram, prefetch):
    PS = E.ps
    DCH = 16
    NCH = P // DCH
    with sublayer(nc, "u_ld t_ld0 t_ld1 ur_ps ur y_ps y y_st w_ld") as (s, ctx):
        sb = E.scratch(ctx)
        U = sb("U", [P, B_ALL, P]); Y = sb("Y", [P, B_ALL, P]); T = sb("T", [P, 2, DCH, P]); UR = sb("UR", [P, B_ALL, P])
        t_ld = [s.t_ld0, s.t_ld1]
        with nc.Block() as block:
            @block.sync
            def _(sp):
                sp.dma_start(U[:], u_dram).then_inc(s.u_ld, 16)
                for c in range(NCH):
                    if c >= 2:
                        sp.wait_ge(s.y_ps, c - 1)
                    src = k_dram[c * DCH:(c + 1) * DCH, :]
                    toeplitz = bass.AP(tensor=src.tensor, offset=src.offset + 1, ap=[[1, P], [2 * P, DCH], [1, P]])
                    sp.dma_start(T[:, c % 2], toeplitz).then_inc(t_ld[c % 2], 16)
                sp.wait_ge(s.y, NCH)
                sp.dma_start(y_dram, Y[:]).then_inc(s.y_st, 16)
                sp.wait_ge(s.y_st, 16)

            @block.scalar
            def _(act):
                for dst, src in prefetch:
                    act.dma_start(dst, src).then_inc(s.w_ld, 16)
                act.wait_ge(s.w_ld, 16 * len(prefetch))

            @block.tensor
            def _(pe):
                pe.wait_ge(s.u_ld, 16)
                for c in range(8):
                    nc.tensor.matmul(PS[:, c, :], E.flip, U[:, 4 * c:4 * c + 4, :].rearrange("p b d -> p (b d)"), start=True, stop=True).then_inc(s.ur_ps, 1)
                pe.wait_ge(s.ur, 8)
                for c in range(NCH):
                    pe.wait_ge(t_ld[c % 2], 16 * (c // 2 + 1))
                    for i in range(DCH):
                        ins = nc.tensor.matmul(PS[:, c, i * B_ALL:(i + 1) * B_ALL], T[:, c % 2, i, :], UR[:, :, c * DCH + i], start=True, stop=True)
                    ins.then_inc(s.y_ps, 1)

            @block.vector
            def _(dve):
                for c in range(8):
                    dve.wait_ge(s.ur_ps, c + 1)
                    nc.vector.tensor_copy(UR[:, 4 * c:4 * c + 4, :].rearrange("p b d -> p (b d)"), PS[:, c, :]).then_inc(s.ur, 1)
                for c in range(NCH):
                    dve.wait_ge(s.y_ps, c + 1)
                    nc.vector.tensor_copy(Y[:, :, c * DCH:(c + 1) * DCH], PS[:, c, :].rearrange("p (i b) -> p b i", i=DCH)).then_inc(s.y, 1)


def l2_xattn_out(nc, E):
    with sublayer(nc, "m1 m2 m3") as (s, ctx):
        with nc.Block() as block:
            @block.vector
            def _(dve):
                nc.vector.scalar_tensor_tensor(E.r[:], E.fo[:, :, 0:P], 1.0, E.u[:], ALU.add, ALU.mult).then_inc(s.m1, 1)
                dve.wait_ge(s.m1, 1)
                nc.vector.tensor_tensor(E.r[:], E.r[:], E.fo[:, :, P:2 * P], ALU.add).then_inc(s.m2, 1)
                dve.wait_ge(s.m2, 1)
                nc.vector.tensor_tensor(E.r[:], E.r[:], E.x[:], ALU.add).then_inc(s.m3, 1)
    ffn(nc, E, post_norm=True)


def l3_attn(nc, E):
    W = E.w
    PS = E.ps
    with sublayer(nc, "xt_ps xt qk_ps qk v_ps v s_ps mx sub ex pt_ps pt z_ps rz zn res" + LN) as (s, ctx):
        sb = E.scratch(ctx)
        QT = sb("QT", [P, 2, GT]); KT = sb("KT", [P, 2, GT]); VA = sb("VA", [P, 2, GB, P + 1])
        nmax = sb("nmax", [P, 2, GB]); SM = sb("SM", [P, 2, GB, P]); PT = sb("PT", [P, 2, GB, P])
        rz = sb("rz", [P, 2, GB]); R = sb("R", [P, NB, P])
        with nc.Block() as block:
            @block.tensor
            def _(pe):
                for g in range(NG):
                    pe_transpose4(nc, [E.x[:, g * GB + b, :] for b in range(GB)], PS[:, g, :], E.ident).then_inc(s.xt_ps, 1)
                for g in range(NG):
                    pe.wait_ge(s.xt, g + 1)
                    xt = E.xt[:, g * GT:(g + 1) * GT]
                    nc.tensor.matmul(PS[:, 2 + g, :], W.wq, xt, start=True, stop=True)
                    nc.tensor.matmul(PS[:, 4 + g, :], W.wk, xt, start=True, stop=True).then_inc(s.qk_ps, 1)
                    for b in range(GB):
                        o = PS[:, 6 + g, b * P:(b + 1) * P]
                        nc.tensor.matmul(o, xt[:, b * P:(b + 1) * P], W.wv, start=True, stop=False)
                        ins = nc.tensor.matmul(o, E.ones_row[0:1, :], W.bv, start=False, stop=True)
                    ins.then_inc(s.v_ps, 1)
                for g in range(NG):
                    pe.wait_ge(s.qk, 2 * g + 2)
                    for b in range(GB):
                        ins = nc.tensor.matmul(PS[:, g, b * P:(b + 1) * P], QT[:, g, b * P:(b + 1) * P],
                                               KT[:, g, b * P:(b + 1) * P], start=True, stop=True)
                    ins.then_inc(s.s_ps, 1)
                for g in range(NG):
                    pe.wait_ge(s.ex, g + 1)
                    pe_transpose4(nc, [SM[:, g, b, :] for b in range(GB)], PS[:, 2 + g, :], E.ident).then_inc(s.pt_ps, 1)
                for g in range(NG):
                    pe.wait_ge(s.pt, g + 1)
                    pe.wait_ge(s.v, g + 1)
                    for b in range(GB):
                        o = PS[:, (4 if b < 2 else 6) + g, (b % 2) * (P + 1):(b % 2 + 1) * (P + 1)]
                        ins = nc.tensor.matmul(o, PT[:, g, b, :], VA[:, g, b, :], start=True, stop=True)
                    ins.then_inc(s.z_ps, 1)

            @block.scalar
            def _(act):
                for g in range(NG):
                    act.wait_ge(s.xt_ps, g + 1)
                    nc.scalar.copy(E.xt[:, g * GT:(g + 1) * GT], PS[:, g, :]).then_inc(s.xt, 1)
                for g in range(NG):
                    act.wait_ge(s.qk_ps, g + 1)
                    nc.scalar.activation(QT[:, g, :], PS[:, 2 + g, :], ACT.Identity, bias=W.bq).then_inc(s.qk, 1)
                    nc.scalar.activation(KT[:, g, :], PS[:, 4 + g, :], ACT.Identity, bias=W.bk).then_inc(s.qk, 1)
                for g in range(NG):
                    act.wait_ge(s.sub, g + 1)
                    nc.scalar.activation(SM[:, g], SM[:, g], ACT.Exp, scale=float(P) ** -0.5).then_inc(s.ex, 1)
                for g in range(NG):
                    act.wait_ge(s.pt_ps, g + 1)
                    nc.scalar.copy(PT[:, g].rearrange("p b q -> p (b q)"), PS[:, 2 + g, :]).then_inc(s.pt, 1)
                for g in range(NG):
                    act_layernorm(nc, act, E, s, g)

            @block.vector
            def _(dve):
                for g in range(NG):
                    nc.vector.memset(VA[:, g, :, P:P + 1], 1.0)
                    dve.wait_ge(s.v_ps, g + 1)
                    nc.vector.tensor_copy(VA[:, g, :, 0:P], PS[:, 6 + g, :].rearrange("p (b d) -> p b d", b=GB)).then_inc(s.v, 1)
                for g in range(NG):
                    sc = PS[:, g, :].rearrange("p (b k) -> p b k", b=GB)
                    dve.wait_ge(s.s_ps, g + 1)
                    nc.vector.tensor_reduce(nmax[:, g, :], sc, AXX, ALU.max).then_inc(s.mx, 1)
                    dve.wait_ge(s.mx, g + 1)
                    nc.vector.tensor_tensor(SM[:, g], sc, bc(nmax[:, g, :].unsqueeze(2), [P, GB, P]), ALU.subtract).then_inc(s.sub, 1)
                for g in range(NG):
                    dve.wait_ge(s.z_ps, g + 1)
                    for h in range(2):
                        z = PS[:, 4 + 2 * h + g, 0:2 * (P + 1)].rearrange("p (b d) -> p b d", b=2)
                        ins = nc.vector.reciprocal(rz[:, g, 2 * h:2 * h + 2], z[:, :, P])
                    ins.then_inc(s.rz, 1)
                    dve.wait_ge(s.rz, g + 1)
                    for b in range(GB):
                        z = PS[:, 4 + 2 * (b // 2) + g, (b % 2) * (P + 1):(b % 2) * (P + 1) + P]
                        ins = nc.vector.scalar_tensor_tensor(R[:, g * GB + b, :], z, rz[:, g, b:b + 1],
                                                             E.x[:, g * GB + b, :], ALU.mult, ALU.add)
                    ins.then_inc(s.res, 1)
                    dve.wait_ge(s.res, g + 1)
                    dve_layernorm(nc, dve, E, s, g, grp(R, g), grp(E.x, g))


PASSES = B_ALL // NB

LAYER_A = ["l0_xattn", "l0_ffn", "l1_attn", "l1_xattn", "l1_ffn", "l2_mix"]
LAYER_B = ["l2_ffw", "l2_ffn", "l3_attn", "l3_xattn", "l3_ffn"]


def load_weights(nc, ctx, E, dram, layers):
    todo = []
    for layer in layers:
        w = {}
        for key, ap in dram.items():
            if key.startswith(layer + "__"):
                t = ctx.enter_context(nc.sbuf_tensor("sb_" + key, list(ap.shape), F32))
                w[key[len(layer) + 2:]] = t[:]
                todo.append((t[:], ap))
        if layer == "l0_ffn":
            w["b1lin"] = ctx.enter_context(nc.sbuf_tensor("sb_b1lin", [P, 8, 2], F32))[:]
        E.weights[layer] = namedtuple("Weights", w)(**w)
    return todo


def load_block(nc, todo):
    with sublayer(nc, "ld_sp ld_act") as (s, ctx):
        with nc.Block() as block:
            @block.sync
            def _(sp):
                part = todo[0::2]
                for dst, src in part:
                    sp.dma_start(dst, src).then_inc(s.ld_sp, 16)
                if part:
                    sp.wait_ge(s.ld_sp, 16 * len(part))

            @block.scalar
            def _(act):
                part = todo[1::2]
                for dst, src in part:
                    act.dma_start(dst, src).then_inc(s.ld_act, 16)
                if part:
                    act.wait_ge(s.ld_act, 16 * len(part))


def store_block(nc, todo):
    with sublayer(nc, "st") as (s, ctx):
        with nc.Block() as block:
            @block.sync
            def _(sp):
                for dst, src in todo:
                    sp.dma_start(dst, src).then_inc(s.st, 16)
                sp.wait_ge(s.st, 16 * len(todo))


def decoder(nc, dram, out):
    with ExitStack() as top:
        E = Environment()
        E.weights = {}
        alloc_common(nc, top, E)
        scratch_dram = lambda n, shape: nc.dram_tensor(n, shape, F32, kind="Internal").ap()
        k_dram = scratch_dram("s4d_k_dram", [P, 2 * P])
        u_dram = scratch_dram("s4d_u_dram", [P, B_ALL, P])
        y_dram = scratch_dram("s4d_y_dram", [P, B_ALL, P])
        x_dram = scratch_dram("x_mid_dram", [P, B_ALL, P])
        fo_dram = scratch_dram("film_dram", [P, B_ALL, 2 * P])

        def consts(ctx, which):
            todo, c = [], {}
            for key, ap in dram.items():
                if key.startswith(which):
                    t = ctx.enter_context(nc.sbuf_tensor("sb_" + key, list(ap.shape), F32))
                    c[key[len(which):]] = t[:]
                    todo.append((t[:], ap))
            return c, todo

        c, common = consts(top, "c_")
        E.ident, E.ones_row, E.eps5, E.eps6, E.one = c["ident"], c["ones_row"], c["eps5"], c["eps6"], c["one"]
        E.minus_half, E.ln2_20, E.headmask, E.flip = c["minus_half"], c["ln2_20"], c["headmask"], c["flip"]

        def run(layer, fn, **kw):
            E.w = E.weights[layer]
            fn(nc, E, **kw)

        with ExitStack() as first:
            with ExitStack() as pre:
                c, todo = consts(pre, "k_")
                E.times = c["times"]
                load_block(nc, load_weights(nc, pre, E, dram, ["s4d"]) + common + todo)
                run("s4d", s4d_kernel, k_dram=k_dram)
            c, todo = consts(first, "a_")
            E.blockmask, E.cos, E.sin, E.causal = c["blockmask"], c["cos"], c["sin"], c["causal"]
            E.gla_sum, E.gla_after, E.gla_upto, E.gla_tril = c["gla_sum"], c["gla_after"], c["gla_upto"], c["gla_tril"]
            todo += load_weights(nc, first, E, dram, LAYER_A)
            SHARED = 7812
            shared = first.enter_context(nc.sbuf_tensor("shared_weights", [P, SHARED], F32))
            turns = {}
            for layer in ("l0_attn", "l2_attn"):
                w, at, pairs = {}, 0, []
                for key, ap in dram.items():
                    if key.startswith(layer + "__"):
                        shape = list(ap.shape)
                        n = 1
                        for d in shape[1:]:
                            n *= d
                        t = shared[0:shape[0], at:at + n]
                        if len(shape) == 3:
                            t = t.rearrange("p (a b) -> p a b", a=shape[1])
                        w[key[len(layer) + 2:]] = t
                        pairs.append((t, ap))
                        at += n
                assert at <= SHARED, at
                E.weights[layer], turns[layer] = namedtuple("Weights", w)(**w), pairs
            load_block(nc, todo + turns["l0_attn"])
            with nc.Fori(0, PASSES) as i:
                mine = lambda ap: ap[:, bass.ds(i * NB, NB)]
                load_block(nc, [(E.x[:], mine(dram["x"])), (E.ctxT[:], mine(dram["ctxT"])),
                                (E.vmask8[:], mine(dram["vmask"])), (E.tmask8[:], mine(dram["tmask"]))])
                run("l0_attn", l0_attn)
                run("l0_xattn", l0_xattn, prefetch=turns["l2_attn"])
                run("l0_ffn", l0_ffn)
                run("l1_attn", l1_attn)
                run("l1_xattn", l1_xattn)
                run("l1_ffn", l1_ffn)
                run("l2_attn", l2_attn)
                run("l2_mix", l2_xattn_in, prefetch=turns["l0_attn"],
                    stores=(mine(u_dram), mine(fo_dram), mine(x_dram)))

        with ExitStack() as second:
            todo = load_weights(nc, second, E, dram, LAYER_B)
            E.w = None
            s4d_conv(nc, E, k_dram, u_dram, y_dram, todo)
            with nc.Fori(0, PASSES) as i:
                mine = lambda ap: ap[:, bass.ds(i * NB, NB)]
                with ExitStack() as mix:
                    E.u = mix.enter_context(nc.sbuf_tensor("s4d_out", [P, NB, P], F32))
                    E.fo = mix.enter_context(nc.sbuf_tensor("film_out", [P, NB, 2 * P], F32))
                    load_block(nc, [(E.x[:], mine(x_dram)), (E.u[:], mine(y_dram)), (E.fo[:], mine(fo_dram)), (E.ctxT[:], mine(dram["ctxT"]))])
                    run("l2_ffw", l2_xattn_out)
                run("l2_ffn", l2_ffn)
                run("l3_attn", l3_attn)
                run("l3_xattn", l3_xattn)
                run("l3_ffn", l3_ffn)
                store_block(nc, [(mine(out), E.x[:])])


def layout(i):
    import numpy as np

    col = lambda v: v.reshape(-1, 1)
    row = lambda v: v.reshape(1, -1)
    rep = lambda v: np.broadcast_to(v.reshape(1, -1), (P, v.size))
    split = lambda w: w.reshape(w.shape[0] // P, P, w.shape[1]).transpose(1, 0, 2)
    esplit = lambda w: w.reshape(w.shape[0], w.shape[1] // P, P, w.shape[2]).transpose(2, 0, 1, 3)
    d = {}

    def put(layer, **arrays):
        for k, a in arrays.items():
            d[f"{layer}__{k}"] = a

    g = lambda n: i["L0_attn_" + n]
    l0 = {}
    for n in "QK":
        w, b = g("W_" + n).transpose(1, 0, 2), g("b_" + n)
        l0["w" + n.lower()] = w.reshape(P, 1024)
        l0["w" + n.lower() + "f"] = w.reshape(P, 32, 2, 16)[:, :, ::-1].reshape(P, 1024)
        l0["b" + n.lower()] = b.reshape(8, P).T
        l0["b" + n.lower() + "f"] = b.reshape(32, 2, 16)[:, ::-1].reshape(8, P).T
    vv = np.zeros((8, 16, 4, 16, 8), np.float32)
    v = g("virtual_v").reshape(16, 4, 8, 8)
    vk = np.zeros((4, 32, 8, 4, 16), np.float32)
    for h in range(8):
        for r in range(4):
            vv[h, :, r, 8 * (r % 2) + h, :] = v[:, r, h, :]
    for h in range(4):
        vk[h, :, :, h, :] = g("virtual_k").reshape(16, 8, 4, 32)[:, :, h].transpose(2, 1, 0)
    put("l0_attn", **l0, wv=g("W_V")[:, :, 0].T, bv=rep(g("b_V")), wo=split(g("W_O")[:, 0, :]),
        vk=vk.reshape(P, 8, 64), vv=vv.reshape(P, 4, P))
    g = lambda n: i["L0_xattn_" + n]
    put("l0_xattn", wq=g("Wq"), wk=g("Wk"), wv=g("Wv"), wo=split(g("Wo")), bo=rep(g("bo")))
    g = lambda n: i["L0_ffn_" + n]
    put("l0_ffn", scale=rep(g("norm_scale")), gw=g("gate_w"), gb=row(g("gate_b")),
        w1=g("mlp1_w").reshape(8, P, 256, 2).transpose(1, 0, 3, 2), b1=g("mlp1_b").reshape(8, 2, P, 2).transpose(2, 0, 3, 1),
        w2=esplit(g("mlp2_w")), b2=g("mlp2_b"))
    g = lambda n: i["L1_attn_" + n]
    put("l1_attn", wq=g("Wq").T, wk=g("Wk").T, wv=g("Wv").T, wo=g("Wo").T, bq=col(g("bq")), bk=row(g("bk")), bv=row(g("bv")), bo=row(g("bo")))
    g = lambda n: i["L1_xattn_" + n]
    put("l1_xattn", wq=g("w_q"), wk=g("w_k"), wv=g("w_v"), wo=g("w_o"), bq=col(g("b_q")), bk=col(g("b_k")), bv=rep(g("b_v")), bo=rep(g("b_o")))
    g = lambda n: i["L1_ffn_" + n]
    put("l1_ffn", gw=np.concatenate([g("router_w"), g("shared_gate_w")], 1), w1=g("w1").transpose(1, 0, 2), w2=g("w2").transpose(1, 0, 2),
        sgu=g("shared_gate_up"), sd=g("shared_down"))
    g = lambda n: i["L2_attn_" + n]
    put("l2_attn", wq=g("Wq"), wk=g("Wk"), wv=g("Wv"), wg=g("Wg"), bg=rep(g("bg")), wo=split(g("Wo")), ln1w=rep(g("ln1_w")), ln1b=rep(g("ln1_b")),
        ln2w=rep(g("ln2_w")), ln2b=rep(g("ln2_b")), fw1=g("W1"), fb1=g("b1").reshape(4, P).T, fw2=split(g("W2")), fb2=rep(g("b2")))
    g = lambda n: i["L2_xattn_" + n]
    put("l2_mix", wq=g("Wq"), wk=g("Wk"), wv=g("Wv"), wf=np.concatenate([g("W_film_in"), g("W_film_out")], 1),
        bf=row(np.concatenate([g("b_film_in"), g("b_film_out")])), gin=rep(g("g_norm_in")), bin=rep(g("b_norm_in")),
        mg=np.broadcast_to(g("mod_gate").reshape(1, 1), (P, 1)))
    put("s4d", log_dt=col(g("log_dt")), a_re=g("A_re"), a_im=g("A_im"), c_re=g("C_re"), c_im=g("C_im"), dskip=col(g("D_skip")))
    put("l2_ffw", ln2w=rep(g("g_ffn")), ln2b=rep(g("b_ffn")), gout=rep(g("g_norm_out")), bout=rep(g("b_norm_out")),
        fw1=g("W1"), fb1=g("b1").reshape(4, P).T, fw2=split(g("W2")), fb2=rep(g("b2")))
    g = lambda n: i["L2_ffn_" + n]
    put("l2_ffn", gw=g("Wg"), w1=g("W1").transpose(1, 0, 2), b1=g("b1").reshape(8, 4, P).transpose(2, 0, 1), w2=esplit(g("W2")), b2=g("b2"))
    g = lambda n: i["L3_attn_" + n]
    put("l3_attn", wq=g("Wq").T, wk=g("Wk").T, wv=g("Wv").T, bq=col(g("bq")), bk=col(g("bk")), bv=row(g("bv")))
    g = lambda n: i["L3_xattn_" + n]
    put("l3_xattn", wq=g("Wq").T, wk=g("Wk").T, wv=g("Wv").T, wo=g("Wo").T, bq=col(g("bq")), bk=col(g("bk")), bv=rep(g("bv")), bo=rep(g("bo")))
    g = lambda n: i["L3_ffn_" + n]
    put("l3_ffn", scale=rep(g("scale")), gw=g("centroids").T, w1=g("up_w").transpose(1, 0, 2), w2=esplit(g("down_w")))
    d["x"] = i["x"].transpose(1, 0, 2)
    d["ctxT"] = i["ctx_768"].transpose(2, 0, 1)
    d["vmask"] = np.broadcast_to(i["mask_BxS2_bf1"].view(np.uint8)[None], (P, B_ALL, L))
    d["tmask"] = i["mask_BxS_bf1"].view(np.uint8).T
    return {k: np.ascontiguousarray(a) for k, a in d.items()} | shape_constants()


def shape_constants():
    import numpy as np

    f = np.float32
    p, q = np.arange(P)[:, None], np.arange(P)[None]
    full = lambda v: np.full((P, 1), v, f)
    c = {"c_ident": np.eye(P, dtype=f), "c_ones_row": np.ones((1, P), f), "c_eps5": full(1e-5), "c_eps6": full(1e-6),
         "c_minus_half": full(-0.5), "c_one": full(1), "c_ln2_20": full(20 * np.log(2)),
         "c_headmask": (p // 8 == np.arange(16)[None]).astype(f), "a_blockmask": (p // 8 == q // 8).astype(f),
         "k_times": np.broadcast_to(np.arange(P, dtype=f), (P, P)).copy()}
    c["c_flip"] = np.eye(P, dtype=f)[::-1].copy()
    freq = f(10000.0) ** (np.arange(16, dtype=f) / f(16))
    angle = np.arange(P, dtype=f)[None] / np.concatenate([freq, freq])[:, None]
    sign = np.where(np.arange(32) < 16, -1, 1)[:, None]
    c["a_cos"] = np.tile(np.cos(angle), (4, 1)).astype(f)
    c["a_sin"] = np.tile(np.sin(angle) * sign, (4, 1)).astype(f)
    c["a_causal"] = np.where(np.arange(P + 16)[None] <= p + 16, 0, -1e30).astype(f)
    same = p // 64 == q // 64
    c["a_gla_sum"] = (same & np.where(q < 64, p > q, p <= q)).astype(f)
    c["a_gla_after"] = (same & (p > q)).astype(f)
    upto = p % 64 <= np.arange(64)[None]
    c["a_gla_upto"] = (upto / 64.0).astype(f)
    c["a_gla_tril"] = upto.astype(f)
    return c


def kernel(**inputs):
    import numpy as _np
    import concourse.bacc as _bacc
    from concourse import mybir as _mybir
    from concourse.bass_utils import run_bass_kernel_spmd as _run

    nc = _bacc.Bacc("TRN2", target_bir_lowering=False, num_devices=1)
    arrays, dram = {}, {}
    for name, a in layout({k: _np.asarray(v) for k, v in inputs.items()}).items():
        arrays[f"in_{name}_dram"] = a
        dram[name] = nc.dram_tensor(f"in_{name}_dram", a.shape, _mybir.dt.from_np(a.dtype), kind="ExternalInput").ap()
    out = nc.dram_tensor("out_0_dram", (P, B_ALL, P), F32, kind="ExternalOutput").ap()
    decoder(nc, dram, out)
    r = _run(nc, [arrays], core_ids=[0])
    return r.results[0]["out_0_dram"].transpose(1, 0, 2)
```

```python
import math
from collections import namedtuple
from contextlib import ExitStack, contextmanager
import concourse.bass as bass
from concourse import mybir

ACT = mybir.ActivationFunctionType
ALU = mybir.AluOpType
AXX = mybir.AxisListType.X
F32 = mybir.dt.float32
U8 = mybir.dt.uint8

B_ALL = 32
P = 128
NB = 8
GB = 4
NG = NB // GB
GT = GB * P
L = 77
DC = 96


class Environment:
    pass


@contextmanager
def sublayer(nc, names):
    with ExitStack() as ctx:
        sems = {}
        nums = []
        for n in names.split():
            h = ctx.enter_context(nc.semaphore(f"{n}_{nc.next_id()}"))
            sems[n] = h
            nums.append(h.num)
        yield namedtuple("Semaphores", sems)(**sems), ctx
        nums.sort()
        first = prev = nums[0]
        for v in nums[1:] + [None]:
            if v is None or v != prev + 1:
                nc.gpsimd.sem_clear(range(first, prev + 1))
                first = v
            prev = v
        nc.all_engine_barrier()


def bc(ap, shape):
    return ap.broadcast_to(shape)


def pe_transpose4(nc, tiles, bank, ident):
    for j, t in enumerate(tiles):
        ins = nc.tensor.transpose(bank[:, j * P:(j + 1) * P], t, ident)
    return ins


def dve_ln_stats(nc, dve, E, s, k, src):
    st, mv = E.ln_stats[k % 2], E.ln_mv[k % 2]
    for b in range(GB):
        ins = nc.vector.bn_stats(st[:, b, :], src[:, b, :])
    ins.then_inc(s.ln_stats, 1)
    dve.wait_ge(s.ln_stats, k + 1)
    for b in range(GB):
        ins = nc.vector.bn_aggr(mv[:, b, :], st[:, b, :])
    ins.then_inc(s.ln_var, 1)


def dve_ln_apply(nc, dve, E, s, k, src, dst, scale=None, shift=None):
    mv, rstd = E.ln_mv[k % 2], E.ln_rstd[k % 2]
    dve.wait_ge(s.ln_std, k + 1)
    nc.vector.reciprocal(rstd[:], E.ln_std[k % 2][:]).then_inc(s.ln_rstd, 1)
    dve.wait_ge(s.ln_rstd, k + 1)
    for b in range(GB):
        ins = nc.vector.tensor_scalar(dst[:, b, :], src[:, b, :], mv[:, b, 0:1], rstd[:, b:b + 1],
                                      ALU.subtract, ALU.mult)
    if scale is not None:
        ins.then_inc(s.ln_core, 1)
        dve.wait_ge(s.ln_core, 2 * k + 1)
        ins = nc.vector.tensor_tensor(dst, dst, bc(scale.unsqueeze(1), [P, GB, P]), ALU.mult)
        ins.then_inc(s.ln_core, 1)
        dve.wait_ge(s.ln_core, 2 * k + 2)
        ins = nc.vector.tensor_tensor(dst, dst, bc(shift.unsqueeze(1), [P, GB, P]), ALU.add)
    return ins


def dve_layernorm(nc, dve, E, s, k, src, dst, scale=None, shift=None):
    dve_ln_stats(nc, dve, E, s, k, src)
    return dve_ln_apply(nc, dve, E, s, k, src, dst, scale, shift)


def act_table(nc, E, func):
    nc.scalar.activation(E.act_warm[:], E.eps5[:], func)


def act_layernorm(nc, act, E, s, k):
    act.wait_ge(s.ln_var, k + 1)
    nc.scalar.activation(E.ln_std[k % 2][:], E.ln_mv[k % 2][:, :, 1], ACT.Sqrt,
                         bias=E.eps5[:]).then_inc(s.ln_std, 1)


LN = " ln_stats ln_var ln_std ln_rstd ln_core"


def grp(x, g):
    return x[:, g * GB:(g + 1) * GB, :]


def alloc_common(nc, ctx, E):
    def t(n, s, d=F32):
        return ctx.enter_context(nc.sbuf_tensor(n, s, d))
    E.x = t("x_res", [P, NB, P]); E.r = t("r_res", [P, NB, P]); E.xt = t("x_T", [P, NB * P]); E.ctxT = t("ctx_T", [DC, NB, L])
    E.vmask8 = t("vmask8", [P, NB, L], U8); E.tmask8 = t("tmask8", [P, NB], U8)
    E.act_warm = t("act_warm", [P, 1])
    E.ln_stats = [t(f"ln_stats{i}", [P, GB, 6]) for i in range(2)]
    E.ln_mv = [t(f"ln_mv{i}", [P, GB, 2]) for i in range(2)]
    E.ln_std = [t(f"ln_std{i}", [P, GB]) for i in range(2)]
    E.ln_rstd = [t(f"ln_rstd{i}", [P, GB]) for i in range(2)]
    E.ps = ctx.enter_context(nc.psum_tensor("banks", [P, 8, 512], F32))

    def scratch(c):
        return lambda n, s: c.enter_context(nc.sbuf_tensor(f"{n}_{nc.next_id()}", s, F32))
    E.scratch = scratch


def l0_attn(nc, E):
    W, PS = E.w, E.ps
    H, D, DV, VK = 32, 32, 8, 16
    K = P + VK
    NJ = H * D // P
    NR = H // 8
    N = NB * NR
    PB = 2
    NP = NB // PB
    PTOK = PB * P
    NPR = PB * NR
    NU = 2 * NJ
    NPROD = NU + 1
    S = P + DV
    SCALE = float(D) ** -0.5
    with sublayer(nc, "xt_ps xt u_ps rotB rot v vz kz kb_even kb_odd vp s_ps ms mx nx ex rz nm pt_ps pt zt_ps zt o_ps res" + LN) as (s, ctx):
        sb = E.scratch(ctx)
        QT = sb("QT", [P, 2, NJ, PTOK]); KT = sb("KT", [P, 2, NJ, PB, P]); KB = sb("KB", [P, 2, NJ // 2, 4, P])
        RA = sb("RA", [P, 2, PTOK]); RB = sb("RB", [P, 2, PTOK])
        VA = sb("VA", [P, 2, PB, H * DV]); VP = sb("VP", [P, 2, 16 * S])
        SM = sb("SM", [P, 3, 8, K]); SV = sb("SV", [P, 2, 8, VK]); MX = sb("MX", [P, 2, 8]); NX = sb("NX", [P, 2, 8])
        SU = sb("SU", [P, 2, 8]); RZ = sb("RZ", [P, 2, 8])
        PT = sb("PT", [P, 2, 9, P]); ZT = sb("ZT", [P, 2, P])
        R = E.r

        kb = lambda m: s.kb_odd if m % 2 else s.kb_even

        def pieces(n):
            p, i = n // NPR + 1, n % NPR
            return [(p, u) for u in range(NPROD * i // NPR, NPROD * (i + 1) // NPR)] if p < NP else []

        FIRST = [(0, u) for u in range(NPROD)]

        def piece_read(eng, p, u):
            if u == 0:
                eng.wait_ge(s.v, p + 1)
            else:
                eng.wait_ge(s.rotB, NU * p + u)

        with nc.Block() as block:
            @block.tensor
            def _(pe):
                for g in range(NG):
                    pe_transpose4(nc, [E.x[:, g * GB + b, :] for b in range(GB)], PS[:, 6 + g, :], E.ident).then_inc(s.xt_ps, 1)

                def produce(p, u):
                    k = NPROD * p + u
                    bank = PS[:, 2 + k % 2, :]
                    if k >= 2:
                        piece_read(pe, (k - 2) // NPROD, (k - 2) % NPROD)
                    pe.wait_ge(s.xt, p * PB // GB + 1)
                    xt = E.xt[:, p * PTOK:(p + 1) * PTOK]
                    if u == 0:
                        for b in range(PB):
                            ins = nc.tensor.matmul(bank[:, b * 256:(b + 1) * 256], xt[:, b * P:(b + 1) * P], W.wv, start=True, stop=True)
                    else:
                        j = (u - 1) % NJ
                        for c, w in enumerate((W.wk, W.wkf) if u <= NJ else (W.wq, W.wqf)):
                            ins = nc.tensor.matmul(bank[:, c * PTOK:(c + 1) * PTOK], w[:, j * P:(j + 1) * P], xt, start=True, stop=True)
                    ins.then_inc(s.u_ps, 1)

                def scores(n):
                    p, t, r = n // NPR, n // NR, n % NR
                    b = t % PB
                    pe.wait_ge(s.rot, NU * p + NJ + (2 * r + 2 if b == 0 else NJ))
                    if n % 2 == 0:
                        pe.wait_ge(kb(n // 2), 64 * (n // 4 + 1))
                    if n >= 1:
                        pe.wait_ge(s.ms, n)
                    for jj in range(2):
                        j = 2 * r + jj
                        nc.tensor.matmul(PS[:, jj, :], QT[:, p % 2, j, b * P:(b + 1) * P],
                                         KB[:, n // 2 % 2, j % 4].rearrange("p i k -> p (i k)"), start=True, stop=True)
                    if n == 0:
                        pe.wait_ge(s.xt, NG)
                    if n % NR == NR - 1 and t:
                        pe.wait_ge(s.res, t)
                    for jj in range(2):
                        j = 2 * r + jj
                        ins = nc.tensor.matmul(PS[:, 7, jj * 64:(jj + 1) * 64], QT[:, p % 2, j, b * P:(b + 1) * P], W.vk[:, j, :], start=True, stop=True)
                    ins.then_inc(s.s_ps, 1)

                def mix(n, between):
                    r, p = n % NR, n % 2
                    z = PS[:, 6, 0:P]
                    half = lambda c: [nc.tensor.matmul(z, VP[:, n // 2 % 2, (8 * p + h) * P:(8 * p + h + 1) * P], PT[:, p, h, :],
                                                       start=p == 0 and h == 0, stop=False) for h in range(4 * c, 4 * c + 4)]
                    pe.wait_ge(s.nm, n + 1)
                    for c in range(3):
                        if c == 2:
                            for p_, u in between:
                                produce(p_, u)
                        k = 3 * n + c
                        if k >= 2:
                            pe.wait_ge(s.pt, k - 1)
                        if c < 2:
                            for i in range(4):
                                ins = nc.tensor.transpose(PS[:, 4 + k % 2, i * P:(i + 1) * P], SM[:, n % 3, 4 * c + i, 0:P], E.ident)
                        else:
                            if p == 0:
                                pe.wait_ge(s.vp, n // 2 + 1)
                                if n >= 2:
                                    pe.wait_ge(s.zt, n // 2)
                            half(0)
                            ins = nc.tensor.transpose(PS[:, 4 + k % 2, 0:P], SV[:, p].rearrange("p h k -> p (h k)"), E.ident)
                        ins.then_inc(s.pt_ps, 1)
                    pe.wait_ge(s.pt, 3 * n + 2)
                    half(1)
                    pe.wait_ge(s.pt, 3 * n + 3)
                    nc.tensor.matmul(z, W.vv[:, r, :], PT[:, p, 8, :], start=False, stop=p == 1).then_inc(s.zt_ps, 1)

                def project(t):
                    pe.wait_ge(s.zt, 2 * t + 2)
                    if t < NB - 1:
                        pe.wait_ge(s.ms, NR * (t + 1) + 3)
                    for c in range(2):
                        ins = nc.tensor.matmul(PS[:, 7, 256:256 + P], ZT[:, c, :], W.wo[:, c, :], start=c == 0, stop=c == 1)
                    ins.then_inc(s.o_ps, 1)

                for p, u in FIRST:
                    produce(p, u)
                for n in range(N + 3):
                    if n < N:
                        scores(n)
                    if n < 2:
                        for p, u in pieces(n):
                            produce(p, u)
                    elif n < N + 2:
                        mix(n - 2, pieces(n) if n < N else [])
                    if n >= 3 and (n - 3) % NR == NR - 1:
                        project((n - 3) // NR)

            @block.sync
            def _(sp):
                sp.wait_ge(s.kz, 1)
                for m in range(2 * NB):
                    t, c = m // 2, m % 2
                    sp.wait_ge(s.rot, t // PB * NU + (NJ // 2 if c == 0 and t % PB == 0 else NJ))
                    if m >= 2:
                        sp.wait_ge(s.s_ps, 2 * m - 2)
                    for i in range(4):
                        sp.dma_start(KB[D * i:D * (i + 1), m % 2, :, i, :],
                                     KT[D * i:D * (i + 1), t // PB % 2, 4 * c:4 * c + 4, t % PB, :]).then_inc(kb(m), 16)
                sp.wait_ge(s.kb_even, 64 * NB)
                sp.wait_ge(s.kb_odd, 64 * NB)

            @block.scalar
            def _(act):
                act_table(nc, E, ACT.Exp)
                for g in range(NG):
                    act.wait_ge(s.xt_ps, g + 1)
                    nc.scalar.copy(E.xt[:, g * GT:(g + 1) * GT], PS[:, 6 + g, :]).then_inc(s.xt, 1)

                def values(m):
                    t = m // 2
                    act.wait_ge(s.v, t // PB + 1)
                    nc.scalar.copy(VP[:, m % 2].rearrange("k (h s) -> k h s", s=S)[:, :, 0:DV],
                                   VA[:, t // PB % 2, t % PB, (m % 2) * P:(m % 2 + 1) * P].rearrange("k (h d) -> k h d", d=DV)).then_inc(s.vp, 1)

                def output(m):
                    act.wait_ge(s.zt_ps, 2 * m + 2)
                    if m >= 2:
                        act.wait_ge(s.o_ps, m // 2)
                    nc.scalar.copy(ZT[:, m % 2, :], PS[:, 6, 0:P]).then_inc(s.zt, 1)

                act.wait_ge(s.vz, 1)
                values(0)
                values(1)
                for e in range(N + 3):
                    n = e - 2
                    if 0 <= n < N:
                        if n >= 2:
                            act.wait_ge(s.zt_ps, n - 1)
                        for c in range(3):
                            k = 3 * n + c
                            act.wait_ge(s.pt_ps, k + 1)
                            if c < 2:
                                nc.scalar.copy(PT[:, n % 2, 4 * c:4 * c + 4, :].rearrange("p h q -> p (h q)"), PS[:, 4 + k % 2, :]).then_inc(s.pt, 1)
                            else:
                                nc.scalar.copy(PT[:, n % 2, 8, :], PS[:, 4 + k % 2, 0:P]).then_inc(s.pt, 1)
                            if c == 0 and n and n % 2 == 0:
                                output(n // 2 - 1)
                    elif n == N:
                        output(n // 2 - 1)
                    if e < N:
                        act.wait_ge(s.nx, e + 1)
                        if e >= 2:
                            act.wait_ge(s.rz, e - 1)
                        for h in range(8):
                            ins = nc.scalar.activation(SM[:, e % 3, h, :], SM[:, e % 3, h, :], ACT.Exp, scale=SCALE,
                                                       bias=NX[:, e % 2, h:h + 1], accum_out=SU[:, e % 2, h:h + 1])
                        ins.then_inc(s.ex, 1)
                    if e == N - 1:
                        act_layernorm(nc, act, E, s, 0)
                    if n and n % 2 == 0 and 0 < n < N and n // 2 + 1 < 2 * NB:
                        values(n // 2 + 1)
                act_layernorm(nc, act, E, s, 1)

            @block.gpsimd
            def _(pool):
                nc.gpsimd.memset(KB[:], 0.0).then_inc(s.kz, 1)
                nc.gpsimd.memset(VP[:], 0.0).then_inc(s.vz, 1)

                def rotate(p, u):
                    if u == 0:
                        return
                    q = NU * p + u - 1
                    if p >= 2 and u == 1:
                        pool.wait_ge(s.s_ps, NPR * (p - 1))
                    pool.wait_ge(s.rotB, q + 1)
                    out = KT[:, p % 2, u - 1].rearrange("p b k -> p (b k)") if u <= NJ else QT[:, p % 2, u - 1 - NJ, :]
                    nc.gpsimd.tensor_tensor(out, RA[:, q % 2, :], RB[:, q % 2, :], ALU.add).then_inc(s.rot, 1)

                for p, u in FIRST:
                    rotate(p, u)
                for e in range(N + 1):
                    n = e - 1
                    if n >= 0:
                        pool.wait_ge(s.rz, n + 1)
                        nc.gpsimd.tensor_tensor(SM[:, n % 3, :, 0:P], SM[:, n % 3, :, 0:P], bc(RZ[:, n % 2, :].unsqueeze(2), [P, 8, P]), ALU.mult)
                        if n >= 2:
                            pool.wait_ge(s.pt_ps, 3 * (n - 1))
                        nc.gpsimd.tensor_tensor(SV[:, n % 2], SM[:, n % 3, :, P:K], bc(RZ[:, n % 2, :].unsqueeze(2), [P, 8, VK]),
                                                ALU.mult).then_inc(s.nm, 1)
                    if e < N:
                        for p, u in pieces(e):
                            rotate(p, u)

            @block.vector
            def _(dve):
                def read(p, u):
                    k = NPROD * p + u
                    bank = PS[:, 2 + k % 2, :]
                    dve.wait_ge(s.u_ps, k + 1)
                    if u == 0:
                        if p >= 2:
                            dve.wait_ge(s.vp, 2 * PB * (p - 1))
                        nc.vector.tensor_tensor(VA[:, p % 2], bank.rearrange("p (b n) -> p b n", b=PB),
                                                bc(W.bv.unsqueeze(1), [P, PB, H * DV]), ALU.add).then_inc(s.v, 1)
                        return
                    q, j = NU * p + u - 1, (u - 1) % NJ
                    if q >= 2:
                        dve.wait_ge(s.rot, q - 1)
                    biases = (W.bk, W.bkf) if u <= NJ else (W.bq, W.bqf)
                    for c, (buf, bb, table) in enumerate(zip((RA, RB), biases, (E.cos, E.sin))):
                        ins = nc.vector.scalar_tensor_tensor(buf[:, q % 2, :].rearrange("p (b q) -> p b q", b=PB),
                                                             bank[:, c * PTOK:(c + 1) * PTOK].rearrange("p (b q) -> p b q", b=PB), bb[:, j:j + 1],
                                                             bc(table.unsqueeze(1), [P, PB, P]), ALU.add, ALU.mult)
                    ins.then_inc(s.rotB, 1)

                def reciprocal(n):
                    dve.wait_ge(s.ex, n + 1)
                    if n >= 2:
                        dve.wait_ge(s.nm, n - 1)
                    nc.vector.reciprocal(RZ[:, n % 2, :], SU[:, n % 2, :]).then_inc(s.rz, 1)

                def softmax_in(n):
                    if n >= 3:
                        dve.wait_ge(s.pt_ps, 3 * (n - 2))
                        dve.wait_ge(s.nm, n - 2)
                    dve.wait_ge(s.s_ps, n + 1)
                    p = n % 2
                    nc.vector.tensor_tensor(SM[:, n % 3, :, 0:P], PS[:, 0:2, :].rearrange("p a (i k) -> p (a i) k", k=P),
                                            bc(E.causal[:, 0:P].unsqueeze(1), [P, 8, P]), ALU.add)
                    nc.vector.tensor_tensor(SM[:, n % 3, :, P:K], PS[:, 7, 0:P].rearrange("p (h k) -> p h k", k=VK),
                                            bc(E.causal[:, P:K].unsqueeze(1), [P, 8, VK]), ALU.add).then_inc(s.ms, 1)
                    if n:
                        reciprocal(n - 1)
                    dve.wait_ge(s.ms, n + 1)
                    nc.vector.tensor_reduce(MX[:, p, :], SM[:, n % 3], AXX, ALU.max).then_inc(s.mx, 1)
                    dve.wait_ge(s.mx, n + 1)
                    if n >= 2:
                        dve.wait_ge(s.ex, n - 1)
                    nc.vector.tensor_scalar(NX[:, p, :], MX[:, p, :], -SCALE, None, ALU.mult).then_inc(s.nx, 1)

                for p, u in FIRST:
                    read(p, u)
                for n in range(N + 4):
                    if n >= 4 and (n - 4) % NR == NR - 1:
                        t = (n - 4) // NR
                        dve.wait_ge(s.o_ps, t + 1)
                        nc.vector.tensor_tensor(R[:, t, :], PS[:, 7, 256:256 + P], E.x[:, t, :], ALU.add).then_inc(s.res, 1)
                    if n < N:
                        softmax_in(n)
                        for p, u in pieces(n):
                            read(p, u)
                    if n == N:
                        reciprocal(n - 1)
                    if n == NR * GB + NPR:
                        dve.wait_ge(s.res, GB)
                        dve_ln_stats(nc, dve, E, s, 0, grp(R, 0))
                    if n == N + 1:
                        dve_ln_apply(nc, dve, E, s, 0, grp(R, 0), grp(E.x, 0))
                dve.wait_ge(s.res, NB)
                dve_layernorm(nc, dve, E, s, 1, grp(R, 1), grp(E.x, 1))


def l0_xattn(nc, E, prefetch=()):
    W, PS = E.w, E.ps
    H, D = 8, 64
    NJ = H * D // P
    CG = GB * L
    proj = [("k", g, j) for g in range(NG) for j in range(NJ)] + [("q", g, j) for g in range(NG) for j in range(NJ)] + \
           [("v", t, 0) for t in range(NB)]
    NU = len(proj)
    with sublayer(nc, "xt_ps xt u_ps ua ud vz pz rb s_ps mx sub ex sm rz nm pt_ps pt zt_ps zt o_ps res w_ld" + LN) as (s, ctx):
        sb = E.scratch(ctx)
        QT = sb("QT", [P, NJ, NB * P]); KT = sb("KT", [P, NJ, NB, 2, L]); VA = sb("VA", [P, NB, H * D])
        MX = sb("MX", [P, 2, H]); SM = sb("SM", [P, 3, H, L]); SU = sb("SU", [P, 2, H]); RZ = sb("RZ", [P, 2, H])
        PT = sb("PT", [P, 2, H, P]); ZT = sb("ZT", [P, 2, NJ * P])
        XB = E.r
        on_act = [u for u in range(NU) if u % 2 == 0]
        on_dve = [u for u in range(NU) if u % 2 == 1]

        def unit_out(u):
            kind, a, j = proj[u]
            if kind == "k":
                return [(KT[o * D:(o + 1) * D, j, a * GB:(a + 1) * GB, o, :],
                         PS[o * D:(o + 1) * D, u % 4, 0:CG].rearrange("p (b l) -> p b l", l=L)) for o in range(2)]
            if kind == "v":
                return [(VA[0:L, a, :], PS[0:L, u % 4, :])]
            return [(QT[:, j, a * GT:(a + 1) * GT], PS[:, u % 4, :])]

        def done(eng, u):
            if u % 2 == 0:
                eng.wait_ge(s.ua, u // 2 + 1)
            else:
                eng.wait_ge(s.ud, u // 2 + 1)

        with nc.Block() as block:
            @block.sync
            def _(sp):
                for dst, src in prefetch:
                    sp.dma_start(dst, src).then_inc(s.w_ld, 16)
                if prefetch:
                    sp.wait_ge(s.w_ld, 16 * len(prefetch))

            @block.tensor
            def _(pe):
                for g in range(NG):
                    pe_transpose4(nc, [E.x[:, g * GB + b, :] for b in range(GB)], PS[:, 4 + g, :], E.ident).then_inc(s.xt_ps, 1)
                for u, (kind, a, j) in enumerate(proj):
                    if u >= 4:
                        done(pe, u - 4)
                    if kind == "k":
                        nc.tensor.matmul(PS[:, u % 4, 0:CG], W.wk[:, j * P:(j + 1) * P],
                                         E.ctxT[:, a * GB:(a + 1) * GB, :].rearrange("c b l -> c (b l)"), start=True, stop=True).then_inc(s.u_ps, 1)
                    elif kind == "v":
                        nc.tensor.matmul(PS[0:L, u % 4, :], E.ctxT[:, a, :], W.wv, start=True, stop=True).then_inc(s.u_ps, 1)
                    else:
                        pe.wait_ge(s.xt, a + 1)
                        nc.tensor.matmul(PS[:, u % 4, :], W.wq[:, j * P:(j + 1) * P], E.xt[:, a * GT:(a + 1) * GT],
                                         start=True, stop=True).then_inc(s.u_ps, 1)
                for u in range(NU - 4, NU):
                    done(pe, u)

                def scores(t):
                    if t >= 2:
                        pe.wait_ge(s.sub, t - 1)
                    for j in range(NJ):
                        ins = nc.tensor.matmul(PS[:, 2 * (t % 2) + j // 2, j % 2 * 2 * L:(j % 2 + 1) * 2 * L], QT[:, j, t * P:(t + 1) * P],
                                               KT[:, j, t].rearrange("p o l -> p (o l)"), start=True, stop=True)
                    ins.then_inc(s.s_ps, 1)

                def transposes(t):
                    pe.wait_ge(s.nm, t + 1)
                    for a in range(2):
                        k = 2 * t + a
                        if k >= 2:
                            pe.wait_ge(s.pt, k - 1)
                        for h in range(4):
                            ins = nc.tensor.transpose(PS[0:L, 4 + a, h * P:(h + 1) * P], SM[:, t % 3, 4 * a + h, :], E.ident)
                        ins.then_inc(s.pt_ps, 1)

                def mix(t):
                    if t >= 1:
                        pe.wait_ge(s.zt, t)
                    for a in range(2):
                        pe.wait_ge(s.pt, 2 * t + a + 1)
                        for h in range(4 * a, 4 * a + 4):
                            ins = nc.tensor.matmul(PS[h % 2 * D:(h % 2 + 1) * D, 6, h // 2 * P:(h // 2 + 1) * P], VA[:, t, h * D:(h + 1) * D],
                                                   PT[:, t % 2, h, :], start=True, stop=True)
                    ins.then_inc(s.zt_ps, 1)

                def project(t):
                    pe.wait_ge(s.zt, t + 1)
                    if t >= 1:
                        pe.wait_ge(s.res, t)
                    for j in range(NJ):
                        ins = nc.tensor.matmul(PS[:, 7, 0:P], ZT[:, t % 2, j * P:(j + 1) * P], W.wo[:, j, :], start=j == 0, stop=j == NJ - 1)
                    ins.then_inc(s.o_ps, 1)

                for i in range(NB + 3):
                    if 2 <= i < NB + 2:
                        transposes(i - 2)
                    if i < NB:
                        scores(i)
                    if i >= 3:
                        project(i - 3)
                    if 2 <= i < NB + 2:
                        mix(i - 2)

            @block.scalar
            def _(act):
                act_table(nc, E, ACT.Exp)
                for g in range(NG):
                    act.wait_ge(s.xt_ps, g + 1)
                    nc.scalar.copy(E.xt[:, g * GT:(g + 1) * GT], PS[:, 4 + g, :]).then_inc(s.xt, 1)
                for u in on_act:
                    act.wait_ge(s.u_ps, u + 1)
                    if proj[u][0] == "v":
                        act.wait_ge(s.vz, 1)
                    for out, in_ in unit_out(u):
                        ins = nc.scalar.copy(out, in_)
                    ins.then_inc(s.ua, 1)
                act.wait_ge(s.pz, 1)
                for i in range(NB + 2):
                    t = i - 2
                    if t >= 0:
                        for a in range(2):
                            act.wait_ge(s.pt_ps, 2 * t + a + 1)
                            if a == 0 and t >= 2:
                                act.wait_ge(s.zt_ps, t - 1)
                            nc.scalar.copy(PT[0:L, t % 2, 4 * a:4 * a + 4, :].rearrange("p h q -> p (h q)"), PS[0:L, 4 + a, :]).then_inc(s.pt, 1)
                    if i < NB:
                        act.wait_ge(s.sub, i + 1)
                        nc.scalar.activation(SM[:, i % 3], SM[:, i % 3], ACT.Exp, scale=float(D) ** -0.5).then_inc(s.ex, 1)
                    if i == NB - 1:
                        act_layernorm(nc, act, E, s, 0)
                    if t >= 0:
                        act.wait_ge(s.zt_ps, t + 1)
                        if t >= 2:
                            act.wait_ge(s.o_ps, t - 1)
                        nc.scalar.copy(ZT[:, t % 2, :], PS[:, 6, :]).then_inc(s.zt, 1)
                act_layernorm(nc, act, E, s, 1)

            @block.gpsimd
            def _(pool):
                nc.gpsimd.memset(VA[:], 0.0).then_inc(s.vz, 1)
                nc.gpsimd.memset(PT[:], 0.0).then_inc(s.pz, 1)
                nc.gpsimd.tensor_tensor(XB[:], E.x[:], bc(W.bo.unsqueeze(1), [P, NB, P]), ALU.add).then_inc(s.rb, 1)
                for t in range(NB):
                    pool.wait_ge(s.rz, t + 1)
                    nc.gpsimd.tensor_tensor(SM[:, t % 3], SM[:, t % 3], bc(RZ[:, t % 2, :].unsqueeze(2), [P, H, L]), ALU.mult).then_inc(s.nm, 1)

            @block.vector
            def _(dve):
                for o in range(2):
                    nc.vector.memset(KT[o * D:(o + 1) * D, :, :, 1 - o, :], 0.0)
                for u in on_dve:
                    dve.wait_ge(s.u_ps, u + 1)
                    if proj[u][0] == "v":
                        dve.wait_ge(s.vz, 1)
                    for out, in_ in unit_out(u):
                        ins = nc.vector.tensor_copy(out, in_)
                    ins.then_inc(s.ud, 1)

                for i in range(NB + 3):
                    if i < NB:
                        sc = PS[:, 2 * (i % 2):2 * (i % 2) + 2, 0:4 * L].rearrange("p a (h l) -> p a h l", l=L)
                        dve.wait_ge(s.s_ps, i + 1)
                        nc.vector.tensor_reduce(MX[:, i % 2, :].rearrange("p (a h) -> p a h", a=2), sc, AXX, ALU.max).then_inc(s.mx, 1)
                        dve.wait_ge(s.mx, i + 1)
                        if i >= 3:
                            dve.wait_ge(s.pt_ps, 2 * (i - 2))
                        nc.vector.tensor_tensor(SM[:, i % 3].rearrange("p (a h) l -> p a h l", a=2), sc,
                                                bc(MX[:, i % 2, :].rearrange("p (a h) -> p a h", a=2).unsqueeze(3), [P, 2, 4, L]),
                                                ALU.subtract).then_inc(s.sub, 1)
                    if i >= 3:
                        t = i - 3
                        dve.wait_ge(s.o_ps, t + 1)
                        if t == 0:
                            dve.wait_ge(s.rb, 1)
                        nc.vector.tensor_tensor(XB[:, t, :], PS[:, 7, 0:P], XB[:, t, :], ALU.add).then_inc(s.res, 1)
                        if t == GB - 1:
                            dve.wait_ge(s.res, GB)
                            dve_ln_stats(nc, dve, E, s, 0, grp(XB, 0))
                    if i == NB:
                        dve_ln_apply(nc, dve, E, s, 0, grp(XB, 0), grp(E.x, 0))
                    if i < NB:
                        dve.wait_ge(s.ex, i + 1)
                        nc.vector.tensor_reduce(SU[:, i % 2, :], SM[:, i % 3], AXX, ALU.add).then_inc(s.sm, 1)
                        dve.wait_ge(s.sm, i + 1)
                        if i >= 2:
                            dve.wait_ge(s.nm, i - 1)
                        nc.vector.reciprocal(RZ[:, i % 2, :], SU[:, i % 2, :]).then_inc(s.rz, 1)
                dve.wait_ge(s.res, NB)
                dve_layernorm(nc, dve, E, s, 1, grp(XB, 1), grp(E.x, 1))


NEG = -1.0e30


def moe(nc, E, kind, coming=(), store=None):
    W, PS = E.w, E.ps
    rms = kind in ("swiglu", "gated")
    NE = 8
    blocks = {"swiglu": 4, "silu": 1, "gelu": 4, "gated": 4}[kind]
    hb = {"swiglu": 2, "silu": 1, "gelu": 4, "gated": 2}[kind]
    shared = kind == "silu"
    units = [(e, g) for e in range(NE) for g in range(NG)]
    if shared:
        units += [(NE, g) for g in range(NG)]
    U = len(units)
    NL = NE + 1 if shared else NE
    nblk = [2 if (shared and e == NE) else blocks for e, g in units]
    first = [sum(nblk[:u]) for u in range(U)]
    eps = {"swiglu": E.eps5, "gated": E.eps6}.get(kind)
    double = kind in ("swiglu", "gated")
    has_b2 = kind in ("swiglu", "gelu")
    M_BANK = 6
    with sublayer(nc, "rm_stats rm_var rm_m2 rm_ms rm_std rm_rstd tn xt_ps xt cn cn_ps cn_row lg_ps lg m8 m8m rep sel sub ex "
                      "selx den rden wt wt_ps wtT_ps wtT b2_ps acc0 accb b1 "
                      "xo c_ld st h_ps act_done dve_h glu sig gs gl2 lin hid y_ps acc res" + LN) as (s, ctx):
        sb = E.scratch(ctx)
        TN = sb("TN", [P, NB, P]) if rms else None
        m2 = sb("m2", [P, NG, GB]); ms = sb("ms", [P, NG, GB]); rstd = sb("rr", [P, NG, GB]); std = sb("sd", [P, NG, GB])
        LG = sb("LG", [P, NB, 16]); M8 = sb("M8", [P, NB, 8]); RP = sb("RP", [P, NB, 16])
        XS = sb("XS", [P, NB, NE]); EX = sb("EX", [P, NB, NE]); SEL = sb("SEL", [P, NB, NE]); SX = sb("SX", [P, NB, NE])
        DEN = sb("DEN", [P, NB]); WT = sb("WT", [P, NB, NL]); WTT = sb("WTT", [NE, NB * P])
        GATE = sb("GATE", [P, NB]) if shared else None
        HT = sb("HT", [P, 2, hb, GT])
        T1 = sb("T1", [P, 2, GT]); T2 = sb("T2", [P, 2, GT]); T3 = sb("T3", [P, 2, GT])
        R = sb("R", [P, NB, P])
        CN = sb("CN", [P, NE]); CNR = sb("CNR", [P, NE]); HALF = sb("HALF", [P, P]) if kind == "gated" else None
        b1p = sb("b1p", [P, NE, 2]) if kind == "swiglu" else None
        src = TN if rms else E.x

        with nc.Block() as block:
            @block.tensor
            def _(pe):
                for g in range(NG):
                    if rms:
                        pe.wait_ge(s.tn, g + 1)
                    pe_transpose4(nc, [src[:, g * GB + b, :] for b in range(GB)], PS[:, g, :], E.ident).then_inc(s.xt_ps, 1)
                def logits():
                    for g in range(NG):
                        pe.wait_ge(s.xt, g + 1)
                        for b in range(GB):
                            t = g * GB + b
                            ins = nc.tensor.matmul(PS[:, M_BANK, t * NL:(t + 1) * NL], E.xt[:, t * P:(t + 1) * P], W.gw, start=True, stop=True)
                    ins.then_inc(s.lg_ps, 1)
                    if kind == "gated":
                        pe.wait_ge(s.cn, 1)
                        nc.tensor.matmul(PS[:, 7, 0:NE], HALF[:], CN[:], start=True, stop=True).then_inc(s.cn_ps, 1)

                def up(u):
                    e, g = units[u]
                    xt = E.xt[:, g * GT:(g + 1) * GT]
                    for j in range(nblk[u]):
                        q = first[u] + j
                        if q >= 4:
                            p = q - 4
                            pu = max(i for i in range(U) if first[i] <= p)
                            pj = p - first[pu]
                            if kind == "swiglu":
                                pe.wait_ge(s.dve_h, p + 1)
                            elif kind == "gelu":
                                pe.wait_ge(s.act_done, p + 1)
                            elif kind == "gated":
                                if pj % 2 == 0:
                                    pe.wait_ge(s.act_done, p // 2 + 1)
                                else:
                                    pe.wait_ge(s.dve_h, p // 2 + 1)
                            elif units[pu][0] < NE:
                                pe.wait_ge(s.act_done, pu + 1)
                            elif pj == 0:
                                pe.wait_ge(s.act_done, pu + 1)
                            else:
                                pe.wait_ge(s.dve_h, pu - NE * NG + 1)
                        elif q < 2:
                            pe.wait_ge(s.xt, max(q, g) + 1)
                        if shared and e == NE:
                            w = W.sgu[:, j * P:(j + 1) * P]
                        elif kind == "silu":
                            w = W.w1[:, e, :]
                        elif kind == "gelu":
                            w = W.w1[:, e, j * P:(j + 1) * P]
                        elif kind == "swiglu":
                            w = W.w1[:, e, j % 2, (j // 2) * P:(j // 2 + 1) * P]
                        else:
                            c0 = (0 if j % 2 else 2) + j // 2
                            w = W.w1[:, e, c0 * P:(c0 + 1) * P]
                        nc.tensor.matmul(PS[:, q % 4, :], w, xt, start=True, stop=True).then_inc(s.h_ps, 1)

                def down(u):
                    e, g = units[u]
                    pe.wait_ge(s.hid, u + 1)
                    if u >= 2:
                        pe.wait_ge(s.acc, u - 1)
                    if kind == "silu":
                        w2 = [W.sd[:] if e == NE else W.w2[:, e, :]]
                    else:
                        w2 = [W.w2[:, e, j, :] for j in range(hb)]
                    for b in range(GB):
                        for j in range(len(w2)):
                            ins = nc.tensor.matmul(PS[:, 4 + u % 2, b * P:(b + 1) * P],
                                                   HT[:, u % 2, j, b * P:(b + 1) * P], w2[j],
                                                   start=j == 0, stop=j == len(w2) - 1)
                    ins.then_inc(s.y_ps, 1)

                up(0)
                logits()
                for u in range(1, U + 1):
                    if has_b2 and u == 3:
                        pe.wait_ge(s.wt, 1)
                        for t in range(NB):
                            o = PS[0:NE, M_BANK + t // GB, (t % GB) * P:(t % GB + 1) * P]
                            ins = nc.tensor.transpose(o, WT[:, t, :], E.ident)
                        ins.then_inc(s.wtT_ps, 1)
                    if has_b2 and u == 5:
                        pe.wait_ge(s.wtT, 2)
                        for t in range(NB):
                            o = PS[:, M_BANK + t // GB, (t % GB) * P:(t % GB + 1) * P]
                            ins = nc.tensor.matmul(o, WTT[:, t * P:(t + 1) * P], W.b2, start=True, stop=True)
                        ins.then_inc(s.b2_ps, 1)
                    if u < U:
                        up(u)
                    down(u - 1)

            @block.sync
            def _(sp):
                for dst, part in coming:
                    sp.dma_start(dst, part).then_inc(s.c_ld, 16)
                if coming:
                    sp.wait_ge(s.c_ld, 16 * len(coming))
                if store:
                    for g in range(NG):
                        sp.wait_ge(s.xo, g + 1)
                        sp.dma_start(store[g], grp(E.x, g)).then_inc(s.st, 16)
                    sp.wait_ge(s.st, 16 * NG)

            @block.scalar
            def _(act):
                if rms:
                    for g in range(NG):
                        act.wait_ge(s.rm_ms, g + 1)
                        nc.scalar.activation(std[:, g], ms[:, g], ACT.Sqrt, bias=eps[:]).then_inc(s.rm_std, 1)
                for g in range(NG):
                    act.wait_ge(s.xt_ps, g + 1)
                    nc.scalar.copy(E.xt[:, g * GT:(g + 1) * GT], PS[:, g, :]).then_inc(s.xt, 1)
                for u, (e, g) in enumerate(units):
                    if u == 2 and kind != "gated":
                        act.wait_ge(s.sub, 1)
                        nc.scalar.activation(EX[:], XS[:], ACT.Exp).then_inc(s.ex, 1)
                        if shared:
                            nc.scalar.activation(GATE[:], PS[:, M_BANK, 0:NB * NL].rearrange("p (t e) -> p t e", e=NL)[:, :, NE],
                                                 ACT.Sigmoid).then_inc(s.ex, 1)
                    if u >= 2 and kind in ("gelu", "silu"):
                        act.wait_ge(s.y_ps, u - 1)
                    if kind == "gelu":
                        for j in range(4):
                            act.wait_ge(s.h_ps, first[u] + j + 1)
                            ins = nc.scalar.activation(HT[:, u % 2, j, :], PS[:, (first[u] + j) % 4, :], ACT.Gelu,
                                                       bias=W.b1[:, e, j:j + 1]).then_inc(s.act_done, 1)
                            if j == 3:
                                act.wait_ge(s.act_done, first[u] + 4)
                                act.sem_inc(s.hid, 1)
                    elif kind == "silu":
                        act.wait_ge(s.h_ps, first[u] + 1)
                        if e < NE:
                            nc.scalar.activation(HT[:, u % 2, 0, :], PS[:, first[u] % 4, :], ACT.Silu).then_inc(s.act_done, 1)
                            act.wait_ge(s.act_done, u + 1)
                            act.sem_inc(s.hid, 1)
                        else:
                            nc.scalar.activation(T1[:, g, :], PS[:, first[u] % 4, :], ACT.Silu).then_inc(s.act_done, 1)
                    elif kind == "gated":
                        for j in range(2):
                            k = 2 * u + j
                            act.wait_ge(s.h_ps, first[u] + 2 * j + 1)
                            if k >= 2:
                                act.wait_ge(s.dve_h, k - 1)
                            nc.scalar.activation(T1[:, k % 2, :], PS[:, (first[u] + 2 * j) % 4, :], ACT.Silu).then_inc(s.act_done, 1)
                    else:
                        for j in range(2):
                            k = 2 * u + j
                            act.wait_ge(s.glu, k + 1)
                            if k >= 2:
                                act.wait_ge(s.gs, k - 1)
                            nc.scalar.activation(T2[:, k % 2, :], T1[:, k % 2, :], ACT.Sigmoid, scale=1.702).then_inc(s.sig, 1)
                act_table(nc, E, ACT.Sqrt)
                for g in range(NG):
                    act_layernorm(nc, act, E, s, g)

            @block.gpsimd
            def _(pool):
                if kind == "swiglu":
                    for u, (e, g) in enumerate(units):
                        for j in range(2):
                            k = 2 * u + j
                            pool.wait_ge(s.sig, k + 1)
                            nc.gpsimd.tensor_tensor(T1[:, k % 2, :], T1[:, k % 2, :], T2[:, k % 2, :], ALU.mult).then_inc(s.gs, 1)

            @block.vector
            def _(dve):
                if rms:
                    for g in range(NG):
                        st, mv = E.ln_stats[g], E.ln_mv[g]
                        for b in range(GB):
                            ins = nc.vector.bn_stats(st[:, b, :], E.x[:, g * GB + b, :])
                        ins.then_inc(s.rm_stats, 1)
                        dve.wait_ge(s.rm_stats, g + 1)
                        for b in range(GB):
                            ins = nc.vector.bn_aggr(mv[:, b, :], st[:, b, :])
                        ins.then_inc(s.rm_var, 1)
                        dve.wait_ge(s.rm_var, g + 1)
                        nc.vector.tensor_tensor(m2[:, g], mv[:, :, 0], mv[:, :, 0], ALU.mult).then_inc(s.rm_m2, 1)
                        dve.wait_ge(s.rm_m2, g + 1)
                        nc.vector.tensor_tensor(ms[:, g], m2[:, g], mv[:, :, 1], ALU.add).then_inc(s.rm_ms, 1)
                    for g in range(NG):
                        dve.wait_ge(s.rm_std, g + 1)
                        nc.vector.reciprocal(rstd[:, g], std[:, g]).then_inc(s.rm_rstd, 1)
                        dve.wait_ge(s.rm_rstd, g + 1)
                        for b in range(GB):
                            t = g * GB + b
                            ins = nc.vector.scalar_tensor_tensor(TN[:, t, :], E.x[:, t, :], rstd[:, g, b:b + 1], W.scale,
                                                                 ALU.mult, ALU.mult)
                        ins.then_inc(s.tn, 1)
                if kind == "gated":
                    nc.vector.memset(HALF[:], -0.5)
                    nc.vector.tensor_tensor(CN[:], W.gw, W.gw, ALU.mult).then_inc(s.cn, 1)
                if kind == "swiglu":
                    nc.vector.tensor_copy(b1p[:], W.b1[:, :, 0, :])
                    nc.vector.tensor_scalar(W.b1lin, W.b1[:, :, 1, :], 1.0, None, ALU.add).then_inc(s.b1, 1)
                    dve.wait_ge(s.b1, 1)
                def acc_init():
                    for g in range(NG):
                        ins = nc.vector.tensor_scalar(grp(R, g), grp(E.x, g), 2.0 if double else 1.0, None, ALU.mult)
                    ins.then_inc(s.acc0, 1)

                def route():
                    nc.vector.memset(LG[:, :, NE:16], NEG)
                    dve.wait_ge(s.lg_ps, 1)
                    logits = PS[:, M_BANK, 0:NB * NL].rearrange("p (t e) -> p t e", e=NL)[:, :, 0:NE]
                    if kind == "swiglu":
                        nc.vector.tensor_tensor(LG[:, :, 0:NE], logits, bc(W.gb.unsqueeze(1), [P, NB, NE]), ALU.add).then_inc(s.lg, 1)
                    elif kind == "gated":
                        dve.wait_ge(s.cn_ps, 1)
                        nc.vector.tensor_copy(CNR[:], PS[:, 7, 0:NE]).then_inc(s.cn_row, 1)
                        dve.wait_ge(s.cn_row, 1)
                        nc.vector.tensor_tensor(LG[:, :, 0:NE], logits, bc(CNR[:].unsqueeze(1), [P, NB, NE]), ALU.add).then_inc(s.lg, 1)
                    else:
                        nc.vector.tensor_copy(LG[:, :, 0:NE], logits).then_inc(s.lg, 1)
                    dve.wait_ge(s.lg, 1)
                    for t in range(NB):
                        ins = nc.vector.max(M8[:, t, :], LG[:, t, 0:NE])
                    ins.then_inc(s.m8, 1)
                    dve.wait_ge(s.m8, 1)
                    if kind != "gated":
                        nc.vector.tensor_tensor(XS[:], LG[:, :, 0:NE], bc(M8[:, :, 0:1], [P, NB, NE]), ALU.subtract).then_inc(s.sub, 1)
                    nc.vector.memset(M8[:, :, (1 if kind == "gated" else 2):8], NEG).then_inc(s.m8m, 1)
                    dve.wait_ge(s.m8m, 1)
                    for t in range(NB):
                        ins = nc.vector.match_replace(RP[:, t, :], M8[:, t, :], LG[:, t, :], 2 * NEG)
                    ins.then_inc(s.rep, 1)
                    dve.wait_ge(s.rep, 1)
                    nc.vector.tensor_tensor(WT[:, :, 0:NE] if kind == "gated" else SEL[:], RP[:, :, 0:NE], LG[:, :, 0:NE],
                                            ALU.not_equal).then_inc(s.sel, 1)
                    dve.wait_ge(s.sel, 1)
                    if kind == "gated":
                        nc.vector.memset(DEN[:], 0.0).then_inc(s.wt, 1)
                    else:
                        dve.wait_ge(s.ex, 1)
                        nc.vector.tensor_tensor(SX[:], EX[:], SEL[:], ALU.mult).then_inc(s.selx, 1)
                        dve.wait_ge(s.selx, 1)
                        nc.vector.tensor_reduce(DEN[:], SX[:] if kind == "swiglu" else EX[:], AXX, ALU.add).then_inc(s.den, 1)
                        dve.wait_ge(s.den, 1)
                        nc.vector.reciprocal(DEN[:], DEN[:]).then_inc(s.rden, 1)
                        dve.wait_ge(s.rden, 1)
                        if shared:
                            dve.wait_ge(s.ex, 2)
                            nc.vector.tensor_copy(WT[:, :, NE], GATE[:])
                        nc.vector.tensor_tensor(WT[:, :, 0:NE], SX[:], bc(DEN[:].unsqueeze(2), [P, NB, NE]), ALU.mult).then_inc(s.wt, 1)

                def hidden(u):
                    e, g = units[u]
                    if u >= 2 and kind in ("gated", "swiglu"):
                        dve.wait_ge(s.y_ps, u - 1)
                    if kind == "gated":
                        for j in range(2):
                            k = 2 * u + j
                            dve.wait_ge(s.h_ps, first[u] + 2 * j + 2)
                            dve.wait_ge(s.act_done, k + 1)
                            nc.vector.tensor_tensor(HT[:, u % 2, j, :], PS[:, (first[u] + 2 * j + 1) % 4, :], T1[:, k % 2, :],
                                                    ALU.mult).then_inc(s.dve_h, 1)
                        dve.wait_ge(s.dve_h, 2 * u + 2)
                        dve.sem_inc(s.hid, 1)
                    elif kind == "silu" and e == NE:
                        dve.wait_ge(s.y_ps, u - 1)
                        dve.wait_ge(s.h_ps, first[u] + 2)
                        dve.wait_ge(s.act_done, u + 1)
                        nc.vector.tensor_tensor(HT[:, u % 2, 0, :], PS[:, (first[u] + 1) % 4, :], T1[:, g, :], ALU.mult).then_inc(s.dve_h, 1)
                        dve.wait_ge(s.dve_h, g + 1)
                        dve.sem_inc(s.hid, 1)
                    elif kind == "swiglu":
                        for j in range(2):
                            k = 2 * u + j
                            q = first[u] + 2 * j
                            dve.wait_ge(s.h_ps, q + 1)
                            if k >= 2:
                                dve.wait_ge(s.gl2, k - 1)
                            nc.vector.tensor_scalar(T1[:, k % 2, :], PS[:, q % 4, :], b1p[:, e, j:j + 1], 7.0,
                                                    ALU.add, ALU.min).then_inc(s.glu, 1)
                            dve.wait_ge(s.glu, k + 1)
                            dve.sem_inc(s.dve_h, 1)
                            dve.wait_ge(s.h_ps, q + 2)
                            nc.vector.tensor_scalar(T3[:, k % 2, :], PS[:, (q + 1) % 4, :], W.b1lin[:, e, j:j + 1], 8.0,
                                                    ALU.add, ALU.min).then_inc(s.dve_h, 1)
                        for j in range(2):
                            k = 2 * u + j
                            dve.wait_ge(s.gs, k + 1)
                            dve.wait_ge(s.dve_h, 2 * k + 2)
                            nc.vector.scalar_tensor_tensor(HT[:, u % 2, j, :], T3[:, k % 2, :], -6.0, T1[:, k % 2, :],
                                                           ALU.max, ALU.mult).then_inc(s.gl2, 1)
                        dve.wait_ge(s.gl2, 2 * u + 2)
                        dve.sem_inc(s.hid, 1)

                def combine(u):
                    e, g = units[u]
                    dve.wait_ge(s.y_ps, u + 1)
                    if u == 0:
                        dve.wait_ge(s.wt, 1)
                        dve.wait_ge(s.acc0, 1)
                    if u >= 2:
                        dve.wait_ge(s.acc, u - 1)
                    for b in range(GB):
                        t = g * GB + b
                        ins = nc.vector.scalar_tensor_tensor(R[:, t, :], PS[:, 4 + u % 2, b * P:(b + 1) * P], WT[:, t, e:e + 1],
                                                             R[:, t, :], ALU.mult, ALU.add)
                    ins.then_inc(s.acc, 1)

                acc_init()
                hidden(0)
                hidden(1)
                route()
                for u in range(1, U + 1):
                    if 2 <= u < U:
                        hidden(u)
                    combine(u - 1)
                    if has_b2 and u == 3:
                        dve.wait_ge(s.wtT_ps, 1)
                        for g in range(NG):
                            nc.vector.tensor_copy(WTT[:, g * GT:(g + 1) * GT], PS[0:NE, M_BANK + g, :]).then_inc(s.wtT, 1)
                    if has_b2 and u == 5:
                        dve.wait_ge(s.b2_ps, 1)
                        dve.wait_ge(s.acc, u)
                        for g in range(NG):
                            ins = nc.vector.tensor_tensor(grp(R, g), grp(R, g), PS[:, M_BANK + g, :].rearrange("p (b d) -> p b d", b=GB), ALU.add)
                        ins.then_inc(s.accb, 1)
                        dve.wait_ge(s.accb, 1)
                    if u == U - 1:
                        dve.wait_ge(s.acc, U - 1)
                        dve_layernorm(nc, dve, E, s, 0, grp(R, 0), grp(E.x, 0)).then_inc(s.xo, 1)
                dve.wait_ge(s.acc, U)
                dve_layernorm(nc, dve, E, s, 1, grp(R, 1), grp(E.x, 1)).then_inc(s.xo, 1)


def l0_ffn(nc, E): moe(nc, E, "swiglu")
def l1_ffn(nc, E): moe(nc, E, "silu")
def l2_ffn(nc, E): moe(nc, E, "gelu")
def l3_ffn(nc, E, **kw): moe(nc, E, "gated", **kw)


def l1_attn(nc, E):
    W, PS = E.w, E.ps
    H, D = 16, 8
    with sublayer(nc, "xt_ps xt qk_ps v_ps neg pos ex q v kv_ps kvm ks kvd n_ps den rz zn zt_ps zt o_ps rb res" + LN) as (s, ctx):
        sb = E.scratch(ctx)
        NEGP = sb("NEG", [P, 2 * NG, GT]); Q = sb("Q", [P, 2 * NG, GT])
        V = sb("V", [P, NB, P + 1])
        KVD = sb("KVD", [P, 2, P + H]); KS = sb("KS", [P, NB]); DEN = sb("DEN", [P, 2, H]); RZ = sb("RZ", [P, 2, H])
        ZN = sb("ZN", [P, 2, P]); ZT = sb("ZT", [P, 2, P]); R = E.r
        with nc.Block() as block:
            @block.tensor
            def _(pe):
                for g in range(NG):
                    pe_transpose4(nc, [E.x[:, g * GB + b, :] for b in range(GB)], PS[:, g, :], E.ident).then_inc(s.xt_ps, 1)
                for g in range(NG):
                    pe.wait_ge(s.xt, g + 1)
                    nc.tensor.matmul(PS[:, 2 + g, :], W.wq, E.xt[:, g * GT:(g + 1) * GT], start=True, stop=True).then_inc(s.qk_ps, 1)
                for g in range(NG):
                    for w, b0, bank, sem in ((W.wk, W.bk, 4 + g, s.qk_ps), (W.wv, None, 6 + g, s.v_ps)):
                        for b in range(GB):
                            o = PS[:, bank, b * P:(b + 1) * P]
                            ins = nc.tensor.matmul(o, E.xt[:, (g * GB + b) * P:(g * GB + b + 1) * P], w, start=True, stop=b0 is None)
                            if b0 is not None:
                                ins = nc.tensor.matmul(o, E.ones_row[0:1, :], b0, start=False, stop=True)
                        ins.then_inc(sem, 1)

                def summary(t):
                    if t % GB == 0:
                        pe.wait_ge(s.q, NG + t // GB + 1)
                        pe.wait_ge(s.v, t // GB + 1)
                    if t >= 2:
                        pe.wait_ge(s.ks, t - 1)
                    nc.tensor.matmul(PS[:, t % 2, 0:P + 1], Q[:, NG + t // GB, (t % GB) * P:(t % GB + 1) * P], V[:, t, :],
                                     start=True, stop=True).then_inc(s.kv_ps, 1)

                def read_out(t):
                    pe.wait_ge(s.kvd, t + 1)
                    if t >= 2:
                        pe.wait_ge(s.zn, t - 1)
                    nc.tensor.matmul(PS[:, 2 + t % 2, 0:P + H], Q[:, t // GB, (t % GB) * P:(t % GB + 1) * P], KVD[:, t % 2, :],
                                     start=True, stop=True).then_inc(s.n_ps, 1)

                def project(t):
                    pe.wait_ge(s.zn, t + 1)
                    if t >= 2:
                        pe.wait_ge(s.res, t - 1)
                    else:
                        pe.wait_ge(s.q, 2 * NG)
                    nc.tensor.transpose(PS[:, 4 + t % 2, 0:P], ZN[:, t % 2, :], E.ident).then_inc(s.zt_ps, 1)
                    pe.wait_ge(s.zt, t + 1)
                    o = PS[:, 4 + t % 2, P:2 * P]
                    nc.tensor.matmul(o, ZT[:, t % 2, :], W.wo, start=True, stop=True).then_inc(s.o_ps, 1)

                for t in range(NB + 2):
                    if t < NB:
                        summary(t)
                    if 1 <= t <= NB:
                        read_out(t - 1)
                    if t >= 2:
                        project(t - 2)

            @block.scalar
            def _(act):
                for g in range(NG):
                    act.wait_ge(s.xt_ps, g + 1)
                    nc.scalar.copy(E.xt[:, g * GT:(g + 1) * GT], PS[:, g, :]).then_inc(s.xt, 1)
                for c in range(2 * NG):
                    act.wait_ge(s.neg, c + 1)
                    nc.scalar.activation(NEGP[:, c, :], NEGP[:, c, :], ACT.Exp).then_inc(s.ex, 1)
                act_table(nc, E, ACT.Sqrt)
                for t in range(NB):
                    act.wait_ge(s.zt_ps, t + 1)
                    nc.scalar.copy(ZT[:, t % 2, :], PS[:, 4 + t % 2, 0:P]).then_inc(s.zt, 1)
                    if t == GB:
                        act_layernorm(nc, act, E, s, 0)
                act_layernorm(nc, act, E, s, 1)

            @block.gpsimd
            def _(pool):
                nc.gpsimd.memset(V[:, :, P:P + 1], 1.0)
                nc.gpsimd.tensor_tensor(R[:], E.x[:], bc(W.bo.unsqueeze(1), [P, NB, P]), ALU.add).then_inc(s.rb, 1)
                for c in range(2 * NG):
                    pool.wait_ge(s.ex, c + 1)
                    pool.wait_ge(s.pos, c + 1)
                    nc.gpsimd.tensor_tensor(Q[:, c, :], Q[:, c, :], NEGP[:, c, :], ALU.add).then_inc(s.q, 1)

            @block.vector
            def _(dve):
                for c in range(2 * NG):
                    dve.wait_ge(s.qk_ps, c + 1)
                    b = W.bq if c < NG else 0.0
                    nc.vector.tensor_scalar(NEGP[:, c, :], PS[:, 2 + c, :], b, 0.0, ALU.add, ALU.min).then_inc(s.neg, 1)
                    nc.vector.tensor_scalar(Q[:, c, :], PS[:, 2 + c, :], b, 0.0, ALU.add, ALU.max).then_inc(s.pos, 1)

                for g in range(NG):
                    dve.wait_ge(s.v_ps, g + 1)
                    nc.vector.tensor_tensor(V[:, g * GB:(g + 1) * GB, 0:P], PS[:, 6 + g, :].rearrange("p (b d) -> p b d", b=GB),
                                            bc(W.bv.unsqueeze(1), [P, GB, P]), ALU.add).then_inc(s.v, 1)

                def mask_summary(t):
                    dve.wait_ge(s.kv_ps, t + 1)
                    if t >= 2:
                        dve.wait_ge(s.n_ps, t - 1)
                    nc.vector.tensor_tensor(KVD[:, t % 2, 0:P], PS[:, t % 2, 0:P], E.blockmask, ALU.mult)
                    nc.vector.tensor_scalar(KS[:, t:t + 1], PS[:, t % 2, P:P + 1], 1e-6, None, ALU.add).then_inc(s.ks, 1)
                    dve.wait_ge(s.ks, t + 1)
                    nc.vector.tensor_scalar(KVD[:, t % 2, P:P + H], E.headmask, KS[:, t:t + 1], None, ALU.mult).then_inc(s.kvd, 1)

                def normalise(t):
                    dve.wait_ge(s.n_ps, t + 1)
                    n = PS[:, 2 + t % 2, :]
                    nc.vector.tensor_scalar(DEN[:, t % 2, :], n[:, P:P + H], 1e-6, None, ALU.add).then_inc(s.den, 1)
                    dve.wait_ge(s.den, t + 1)
                    nc.vector.reciprocal(RZ[:, t % 2, :], DEN[:, t % 2, :]).then_inc(s.rz, 1)
                    dve.wait_ge(s.rz, t + 1)
                    if t >= 2:
                        dve.wait_ge(s.zt_ps, t - 1)
                    nc.vector.tensor_tensor(ZN[:, t % 2, :].rearrange("p (h d) -> p h d", d=D), n[:, 0:P].rearrange("p (h d) -> p h d", d=D),
                                            bc(RZ[:, t % 2, :].unsqueeze(2), [P, H, D]), ALU.mult).then_inc(s.zn, 1)

                for t in range(NB + 2):
                    if t < NB:
                        mask_summary(t)
                    if 1 <= t <= NB:
                        normalise(t - 1)
                    if t >= 2:
                        u = t - 2
                        dve.wait_ge(s.o_ps, u + 1)
                        if u == 0:
                            dve.wait_ge(s.rb, 1)
                        nc.vector.tensor_tensor(R[:, u, :], PS[:, 4 + u % 2, P:2 * P], R[:, u, :], ALU.add).then_inc(s.res, 1)
                    if t == GB + 1:
                        dve.wait_ge(s.res, GB)
                        dve_ln_stats(nc, dve, E, s, 0, grp(R, 0))
                    if t == NB:
                        dve_ln_apply(nc, dve, E, s, 0, grp(R, 0), grp(E.x, 0))
                dve.wait_ge(s.res, NB)
                dve_layernorm(nc, dve, E, s, 1, grp(R, 1), grp(E.x, 1))


def xattn16(nc, E):
    W, PS = E.w, E.ps
    H, D = 16, 8
    CG = GB * L
    S = P + D
    with sublayer(nc, "xt_ps xt q_ps q k_ps k v_ps v vz vb pz kd rb s_ps mx sub ex sm rz nm pt_ps pt zt_ps zt o_ps res" + LN) as (s, ctx):
        sb = E.scratch(ctx)
        QT = sb("QT", [P, NG, GT]); KT = sb("KT", [P, NB, L]); VA = sb("VA", [L, NB, P]); VB = sb("VB", [P, 2, H * S])
        KD = sb("KD", [P, 2, H, L]); MX = sb("MX", [P, 2, H]); SM = sb("SM", [P, 3, H, L])
        PT = sb("PT", [P, 2, H, P]); SU = sb("SU", [P, 2, H]); RZ = sb("RZ", [P, 2, H]); ZT = sb("ZT", [P, 2, P])
        XB = E.r
        with nc.Block() as block:
            @block.tensor
            def _(pe):
                for g in range(NG):
                    nc.tensor.matmul(PS[:, 2 + g, 0:CG], W.wk, E.ctxT[:, g * GB:(g + 1) * GB, :].rearrange("c b l -> c (b l)"),
                                     start=True, stop=True).then_inc(s.k_ps, 1)
                    for b in range(GB):
                        ins = nc.tensor.matmul(PS[0:L, 4 + g, b * P:(b + 1) * P], E.ctxT[:, g * GB + b, :], W.wv, start=True, stop=True)
                    ins.then_inc(s.v_ps, 1)
                for g in range(NG):
                    pe_transpose4(nc, [E.x[:, g * GB + b, :] for b in range(GB)], PS[:, g, :], E.ident).then_inc(s.xt_ps, 1)
                for g in range(NG):
                    pe.wait_ge(s.xt, g + 1)
                    nc.tensor.matmul(PS[:, 6 + g, :], W.wq, E.xt[:, g * GT:(g + 1) * GT], start=True, stop=True).then_inc(s.q_ps, 1)

                def scores(t):
                    pe.wait_ge(s.kd, t + 1)
                    if t % GB == 0:
                        pe.wait_ge(s.q, t // GB + 1)
                    if t >= 1:
                        pe.wait_ge(s.sub, t)
                    else:
                        pe.wait_ge(s.k, NG)
                        pe.wait_ge(s.xt, NG)
                    for a in range(4):
                        ins = nc.tensor.matmul(PS[:, a, 0:4 * L], QT[:, t // GB, (t % GB) * P:(t % GB + 1) * P],
                                               KD[:, t % 2, 4 * a:4 * a + 4, :].rearrange("p h l -> p (h l)"), start=True, stop=True)
                    ins.then_inc(s.s_ps, 1)

                def transpose4(t, a):
                    k = 4 * t + a
                    if k >= 2:
                        pe.wait_ge(s.pt, k - 1)
                    else:
                        pe.wait_ge(s.v, k + 1)
                    for h in range(4):
                        ins = nc.tensor.transpose(PS[0:L, 4 + k % 2, h * P:(h + 1) * P], SM[:, t % 3, 4 * a + h, :], E.ident)
                    ins.then_inc(s.pt_ps, 1)

                def mix(t, i):
                    pe.wait_ge(s.nm, t + 1)
                    pe.wait_ge(s.vb, t + 1)
                    transpose4(t, 0)
                    transpose4(t, 1)
                    if i < NB:
                        scores(i)
                    if i >= 3:
                        project(i - 3)
                    if t < 2:
                        pe.wait_ge(s.q, NG)
                    else:
                        pe.wait_ge(s.res, t - 1)
                    for a in range(4):
                        pe.wait_ge(s.pt, 4 * t + a + 1)
                        for h in range(4 * a, 4 * a + 4):
                            ins = nc.tensor.matmul(PS[:, 6 + t % 2, 0:P], VB[:, t % 2, h * P:(h + 1) * P], PT[:, t % 2, h, :],
                                                   start=h == 0, stop=h == H - 1)
                        if a < 2:
                            transpose4(t, a + 2)
                    ins.then_inc(s.zt_ps, 1)

                def project(t):
                    pe.wait_ge(s.zt, t + 1)
                    nc.tensor.matmul(PS[:, 6 + t % 2, P:2 * P], ZT[:, t % 2, :], W.wo, start=True, stop=True).then_inc(s.o_ps, 1)

                for i in range(NB + 3):
                    if i < 2:
                        scores(i)
                    elif i < NB + 2:
                        mix(i - 2, i)
                    else:
                        project(i - 3)

            @block.scalar
            def _(act):
                act_table(nc, E, ACT.Exp)
                for g in range(NG):
                    act.wait_ge(s.xt_ps, g + 1)
                    nc.scalar.copy(E.xt[:, g * GT:(g + 1) * GT], PS[:, g, :]).then_inc(s.xt, 1)
                for g in range(NG):
                    act.wait_ge(s.q_ps, g + 1)
                    nc.scalar.activation(QT[:, g, :], PS[:, 6 + g, :], ACT.Identity, bias=W.bq).then_inc(s.q, 1)
                act.wait_ge(s.pz, 1)
                for i in range(NB + 2):
                    if i >= 2:
                        t = i - 2
                        for a in range(4):
                            k = 4 * t + a
                            act.wait_ge(s.pt_ps, k + 1)
                            if a == 0 and t >= 2:
                                act.wait_ge(s.zt_ps, t - 1)
                            nc.scalar.copy(PT[0:L, t % 2, 4 * a:4 * a + 4, :].rearrange("p h q -> p (h q)"), PS[0:L, 4 + k % 2, :]).then_inc(s.pt, 1)
                    if i < NB:
                        act.wait_ge(s.sub, i + 1)
                        nc.scalar.activation(SM[:, i % 3], SM[:, i % 3], ACT.Exp, scale=float(D) ** -0.5).then_inc(s.ex, 1)
                    if i == NB - 1:
                        act_layernorm(nc, act, E, s, 0)
                    if i >= 2:
                        act.wait_ge(s.zt_ps, t + 1)
                        if t >= 2:
                            act.wait_ge(s.o_ps, t - 1)
                        nc.scalar.copy(ZT[:, t % 2, :], PS[:, 6 + t % 2, 0:P]).then_inc(s.zt, 1)
                act_layernorm(nc, act, E, s, 1)

            @block.gpsimd
            def _(pool):
                def keys(t):
                    pool.wait_ge(s.k, t // GB + 1)
                    if t >= 2:
                        pool.wait_ge(s.s_ps, t - 1)
                    nc.gpsimd.tensor_tensor(KD[:, t % 2], bc(KT[:, t, :].unsqueeze(1), [P, H, L]),
                                            bc(E.headmask[:].unsqueeze(2), [P, H, L]), ALU.mult).then_inc(s.kd, 1)

                keys(0)
                keys(1)
                nc.gpsimd.memset(VB[:], 0.0).then_inc(s.vz, 1)
                nc.gpsimd.tensor_tensor(XB[:], E.x[:], bc(W.bo.unsqueeze(1), [P, NB, P]), ALU.add).then_inc(s.rb, 1)
                pool.wait_ge(s.vz, 1)
                for t in range(NB):
                    pool.wait_ge(s.v, t // GB + 1)
                    if t >= 2:
                        pool.wait_ge(s.zt_ps, t - 1)
                    nc.gpsimd.tensor_copy(VB[0:L, t % 2, :].rearrange("k (h s) -> k h s", s=S)[:, :, 0:D],
                                          VA[:, t, :].rearrange("k (h d) -> k h d", d=D)).then_inc(s.vb, 1)
                    pool.wait_ge(s.rz, t + 1)
                    nc.gpsimd.tensor_tensor(SM[:, t % 3], SM[:, t % 3], bc(RZ[:, t % 2, :].unsqueeze(2), [P, H, L]), ALU.mult).then_inc(s.nm, 1)
                    if t + 2 < NB:
                        keys(t + 2)

            @block.vector
            def _(dve):
                for g in range(NG):
                    dve.wait_ge(s.k_ps, g + 1)
                    nc.vector.tensor_scalar(KT[:, g * GB:(g + 1) * GB, :].rearrange("p b l -> p (b l)"), PS[:, 2 + g, 0:CG], W.bk, None,
                                            ALU.add).then_inc(s.k, 1)
                    dve.wait_ge(s.v_ps, g + 1)
                    nc.vector.tensor_tensor(VA[:, g * GB:(g + 1) * GB, :], PS[0:L, 4 + g, :].rearrange("p (b n) -> p b n", n=P),
                                            bc(W.bv[0:L].unsqueeze(1), [L, GB, P]), ALU.add).then_inc(s.v, 1)
                nc.vector.memset(PT[64:P], 0.0).then_inc(s.pz, 1)

                for i in range(NB + 3):
                    if i < NB:
                        sc = PS[:, 0:4, 0:4 * L].rearrange("p a (h l) -> p a h l", l=L)
                        dve.wait_ge(s.s_ps, i + 1)
                        nc.vector.tensor_reduce(MX[:, i % 2, :].rearrange("p (a h) -> p a h", a=4), sc, AXX, ALU.max).then_inc(s.mx, 1)
                        dve.wait_ge(s.mx, i + 1)
                        if i >= 3:
                            dve.wait_ge(s.pt_ps, 4 * (i - 2))
                        nc.vector.tensor_tensor(SM[:, i % 3].rearrange("p (a h) l -> p a h l", a=4), sc,
                                                bc(MX[:, i % 2, :].rearrange("p (a h) -> p a h", a=4).unsqueeze(3), [P, 4, 4, L]),
                                                ALU.subtract).then_inc(s.sub, 1)
                    if i >= 3:
                        t = i - 3
                        dve.wait_ge(s.o_ps, t + 1)
                        if t == 0:
                            dve.wait_ge(s.rb, 1)
                        nc.vector.tensor_tensor(XB[:, t, :], PS[:, 6 + t % 2, P:2 * P], XB[:, t, :], ALU.add).then_inc(s.res, 1)
                        if t == GB - 1:
                            dve.wait_ge(s.res, GB)
                            dve_ln_stats(nc, dve, E, s, 0, grp(XB, 0))
                    if i == NB:
                        dve_ln_apply(nc, dve, E, s, 0, grp(XB, 0), grp(E.x, 0))
                    if i < NB:
                        t = i
                        dve.wait_ge(s.ex, t + 1)
                        nc.vector.tensor_reduce(SU[:, t % 2, :], SM[:, t % 3], AXX, ALU.add).then_inc(s.sm, 1)
                        dve.wait_ge(s.sm, t + 1)
                        if t >= 2:
                            dve.wait_ge(s.nm, t - 1)
                        nc.vector.reciprocal(RZ[:, t % 2, :], SU[:, t % 2, :]).then_inc(s.rz, 1)
                dve.wait_ge(s.res, NB)
                dve_layernorm(nc, dve, E, s, 1, grp(XB, 1), grp(E.x, 1))


def l1_xattn(nc, E): xattn16(nc, E)
def l3_xattn(nc, E): xattn16(nc, E)


LN_MIN = math.log(1e-6)


def l2_attn(nc, E):
    gla(nc, E)
    ffn(nc, E)


def gla(nc, E):
    W, PS = E.w, E.ps
    H, D, C = 16, 64, 64
    HD = H * D
    NJ = HD // P
    ORDER = []
    for c in range(-2, NB):
        for n, t in (("G", c + 2), ("QD", c), ("Q", c + 2), ("QT", c + 1), ("S1", c), ("K", c + 2), ("e", c + 2), ("KT", c + 1),
                     ("ES", c + 1), ("O", c), ("l", c + 2), ("DF", c + 1), ("r", c + 2), ("V", c + 2), ("OT", c), ("SC", c + 1), ("OUT", c)):
            if 0 <= t < NB:
                ORDER.append((n, t))
    UNITS = [u for u in ORDER if u[0].isupper()]
    POS = {u: k for k, u in enumerate(UNITS)}

    with sublayer(nc, "xt_ps xt xn zero pair gb u eg lg la lm sq qc kc ssq ssm lss rn qn kn v0 v1 exs kqd rt dece dec qt kt qdt at s1 oe ot res" + LN) as (s, ctx):
        sb = E.scratch(ctx)
        XN = sb("XN", [P, NB, P])
        LA = sb("LA", [P, 2, HD]); QN = sb("QN", [P, 2, HD]); KN = sb("KN", [P, 2, HD])
        V0 = sb("V0", [P, 2, HD])
        RH = sb("RH", [P, 2, H, D])
        SQ = sb("SQ", [P, 2, HD]); SS = sb("SS", [P, 2, 2, H]); RN = sb("RN", [P, 2, 2, H])
        LM = sb("LM", [P, 2, H]); EX = sb("EX", [P, HD]); KQ = sb("KQ", [P, HD])
        RT = sb("RT", [P, H, C]); DEC = sb("DEC", [P, H, C])
        QB = sb("QB", [P, NJ, 2, 2, C])
        KNT = sb("KNT", [P, NJ, P])
        AT0 = sb("AT0", [P, H, C]); LH = sb("LH", [P, H, C])
        O = sb("O", [P, HD]); OT = sb("OT", [P, NJ, P])
        freed = {"G": s.gb, "Q": s.qc, "K": s.kc, "V": s.v1, "ES": s.exs, "DF": s.dece, "QT": s.qt, "KT": s.kt, "QD": s.qdt,
                 "SC": s.at, "S1": s.s1, "O": s.oe, "OT": s.ot, "OUT": s.res}

        def pair(u):
            k = POS[u]
            return PS[:, 2 * (k % 4):2 * (k % 4) + 2, :].rearrange("p a n -> p (a n)")

        def ready(eng, u):
            eng.wait_ge(s.pair, POS[u] + 1)

        with nc.Block() as block:
            @block.tensor
            def _(pe):
                for g in range(NG):
                    pe.wait_ge(s.xn, g + 1)
                    pe_transpose4(nc, [XN[:, g * GB + b, :] for b in range(GB)], PS[:, g, :], E.ident).then_inc(s.xt_ps, 1)
                pe.wait_ge(s.xt, NG)
                for k, (n, t) in enumerate(UNITS):
                    if k >= 4:
                        m, tm = UNITS[k - 4]
                        pe.wait_ge(freed[m], tm + 1)
                    pr = pair((n, t))
                    if n in "GQKV":
                        w = {"G": W.wg, "Q": W.wq, "K": W.wk, "V": W.wv}[n]
                        for a in range(2):
                            ins = nc.tensor.matmul(pr[:, a * 512:(a + 1) * 512], E.xt[:, t * P:(t + 1) * P], w[:, a * 512:(a + 1) * 512],
                                                   start=True, stop=True)
                    elif n in ("QT", "KT"):
                        pe.wait_ge(s.qn if n == "QT" else s.kn, t + 1)
                        src = (QN if n == "QT" else KN)[:, t % 2, :]
                        for j in range(NJ):
                            ins = nc.tensor.transpose(pr[:, j * P:(j + 1) * P], src[:, j * P:(j + 1) * P], E.ident)
                    elif n == "ES":
                        pe.wait_ge(s.la, t + 1)
                        for a in range(2):
                            ins = nc.tensor.matmul(pr[:, a * 512:(a + 1) * 512], E.gla_sum, LA[:, t % 2, a * 512:(a + 1) * 512], start=True, stop=True)
                    elif n == "DF":
                        pe.wait_ge(s.rt, t + 1)
                        rt = RT[:].rearrange("p h c -> p (h c)")
                        for a in range(2):
                            ins = nc.tensor.matmul(pr[:, a * 512:(a + 1) * 512], E.gla_after, rt[:, a * 512:(a + 1) * 512], start=True, stop=True)
                    elif n == "SC":
                        pe.wait_ge(s.qt, t + 1)
                        pe.wait_ge(s.kt, t + 1)
                        for j in range(NJ):
                            for c in range(2):
                                ins = nc.tensor.matmul(pr[c * C:(c + 1) * C, j * P:(j + 1) * P], KNT[:, j, c * C:(c + 1) * C],
                                                       QB[:, j, c].rearrange("p o q -> p (o q)"), start=True, stop=True)
                    elif n == "QD":
                        pe.wait_ge(s.kqd, 2 * t + 2)
                        for h in range(H):
                            ins = nc.tensor.transpose(pr[0:D, h * C:(h + 1) * C], KQ[C:P, h * D:(h + 1) * D], E.ident[C:P, C:P])
                    elif n == "S1":
                        pe.wait_ge(s.v0, t + 1)
                        for h in range(H):
                            ins = nc.tensor.matmul(pr[0:D, h * D:(h + 1) * D], KQ[:, h * D:(h + 1) * D], V0[:, t % 2, h * D:(h + 1) * D],
                                                   start=True, stop=True)
                    elif n == "O":
                        pe.wait_ge(s.at, t + 1)
                        pe.wait_ge(s.qdt, t + 1)
                        pe.wait_ge(s.s1, t + 1)
                        pe.wait_ge(s.v1, t + 1)
                        for h in range(H):
                            nc.tensor.matmul(pr[0:C, h * D:(h + 1) * D], AT0[:, h, :], V0[:, t % 2, h * D:(h + 1) * D], start=True, stop=True)
                            ins = nc.tensor.matmul(pr[C:P, h * D:(h + 1) * D], LH[:, h, :], RH[:, t % 2, h, :], start=True, stop=True)
                    elif n == "OT":
                        pe.wait_ge(s.oe, t + 1)
                        for j in range(NJ):
                            ins = nc.tensor.transpose(pr[:, j * P:(j + 1) * P], O[:, j * P:(j + 1) * P], E.ident)
                    else:
                        pe.wait_ge(s.ot, t + 1)
                        for j in range(NJ):
                            ins = nc.tensor.matmul(pr[:, 0:P], OT[:, j, :], W.wo[:, j, :], start=j == 0, stop=j == NJ - 1)
                    ins.then_inc(s.pair, 1)

            @block.scalar
            def _(act):
                for g in range(NG):
                    act_layernorm(nc, act, E, s, g)
                for g in range(NG):
                    act.wait_ge(s.xt_ps, g + 1)
                    nc.scalar.copy(E.xt[:, g * GT:(g + 1) * GT], PS[:, g, :]).then_inc(s.xt, 1)
                act.wait_ge(s.zero, 1)
                for n, t in ORDER:
                    p = t % 2
                    if n.isupper():
                        pr = pair((n, t))
                    if n in ("Q", "K"):
                        i = 2 * t + (n == "K")
                        ready(act, (n, t))
                        if i >= 2:
                            act.wait_ge(s.ssq, i - 1)
                        nc.scalar.activation(SQ[:, i % 2], pr, ACT.Square).then_inc(s.sq, 1)
                    elif n == "e":
                        act.wait_ge(s.u, t + 1)
                        nc.scalar.activation(LA[:, p], LA[:, p], ACT.Exp, scale=-1.0).then_inc(s.eg, 1)
                    elif n == "l":
                        act.wait_ge(s.eg, t + 1)
                        nc.scalar.activation(LA[:, p], LA[:, p], ACT.Ln, bias=E.one[:]).then_inc(s.lg, 1)
                        act.wait_ge(s.ssm, t + 1)
                        nc.scalar.activation(SS[:, p], SS[:, p], ACT.Ln, scale=2.0 ** 40).then_inc(s.lss, 1)
                    elif n == "r":
                        act.wait_ge(s.lss, t + 1)
                        if t >= 2:
                            act.wait_ge(s.kn, t - 1)
                        nc.scalar.activation(RN[:, p], SS[:, p], ACT.Exp, scale=-0.5, bias=E.ln2_20[:]).then_inc(s.rn, 1)
                    elif n == "V":
                        ready(act, (n, t))
                        if t >= 2:
                            ready(act, ("O", t - 2))
                        nc.scalar.copy(V0[0:C, p], pr[0:C, :]).then_inc(s.v0, 1)
                        nc.scalar.copy(RH[C:P, p].rearrange("c h e -> c (h e)"), pr[C:P, :]).then_inc(s.v1, 1)
                    elif n == "QT":
                        ready(act, (n, t))
                        if t:
                            ready(act, ("SC", t - 1))
                        for o in range(2):
                            ins = nc.scalar.copy(QB[o * D:(o + 1) * D, :, :, o, :], pr[o * D:(o + 1) * D, :].rearrange("p (j c q) -> p j c q", c=2, q=C))
                        ins.then_inc(s.qt, 1)
                    elif n == "ES":
                        ready(act, (n, t))
                        if t:
                            act.wait_ge(s.kqd, 2 * t)
                        nc.scalar.activation(EX[:], pr, ACT.Exp).then_inc(s.exs, 1)
                    elif n == "DF":
                        ready(act, (n, t))
                        if t:
                            act.wait_ge(s.at, t)
                        nc.scalar.activation(DEC[:].rearrange("p h c -> p (h c)"), pr, ACT.Exp).then_inc(s.dece, 1)
                    elif n == "QD":
                        ready(act, (n, t))
                        if t:
                            ready(act, ("O", t - 1))
                        nc.scalar.copy(LH[0:D].rearrange("p h c -> p (h c)"), pr[0:D, :]).then_inc(s.qdt, 1)
                    elif n == "O":
                        ready(act, (n, t))
                        if t:
                            ready(act, ("OT", t - 1))
                        nc.scalar.copy(O[:], pr).then_inc(s.oe, 1)

            @block.gpsimd
            def _(pool):
                nc.gpsimd.memset(QB[:], 0.0)
                nc.gpsimd.memset(V0[:], 0.0)
                nc.gpsimd.memset(AT0[:], 0.0).then_inc(s.zero, 1)
                for n, t in ORDER:
                    p = t % 2
                    if n == "QT":
                        pool.wait_ge(s.lm, t + 1)
                        if t:
                            ready(pool, ("DF", t - 1))
                        nc.gpsimd.tensor_tensor(RT[:], bc(LM[:, p].unsqueeze(2), [P, H, C]), bc(E.gla_upto.unsqueeze(1), [P, H, C]), ALU.mult).then_inc(s.rt, 1)
                    elif n == "ES":
                        pool.wait_ge(s.exs, t + 1)
                        pool.wait_ge(s.kn, t + 1)
                        if t:
                            ready(pool, ("S1", t - 1))
                        pool.wait_ge(s.rt, t + 1)
                        nc.gpsimd.tensor_tensor(KQ[C:P], QN[C:P, p], EX[C:P], ALU.mult).then_inc(s.kqd, 1)
                        pool.wait_ge(s.kqd, 2 * t + 1)
                        nc.gpsimd.tensor_tensor(KQ[0:C], KN[0:C, p], EX[0:C], ALU.mult).then_inc(s.kqd, 1)
                    elif n == "DF":
                        pool.wait_ge(s.dece, t + 1)
                        nc.gpsimd.tensor_tensor(DEC[:], DEC[:], bc(E.gla_tril.unsqueeze(1), [P, H, C]), ALU.mult).then_inc(s.dec, 1)
                    elif n == "r":
                        pool.wait_ge(s.rn, t + 1)
                        for i, (buf, raw, done) in enumerate(((QN, s.qc, s.qn), (KN, s.kc, s.kn))):
                            pool.wait_ge(raw, t + 1)
                            x = buf[:, p].rearrange("p (h d) -> p h d", d=D)
                            nc.gpsimd.tensor_tensor(x, x, bc(RN[:, p, i, :].unsqueeze(2), [P, H, D]), ALU.mult).then_inc(done, 1)

            @block.vector
            def _(dve):
                for g in range(NG):
                    dve_layernorm(nc, dve, E, s, g, grp(E.x, g), grp(XN, g), W.ln1w, W.ln1b).then_inc(s.xn, 1)
                for n, t in ORDER:
                    p = t % 2
                    if n.isupper():
                        pr = pair((n, t))
                    if n == "G":
                        ready(dve, (n, t))
                        if t >= 2:
                            ready(dve, ("ES", t - 2))
                            dve.wait_ge(s.lm, t - 1)
                        nc.vector.tensor_tensor(LA[:, p], pr, W.bg, ALU.add).then_inc(s.gb, 1)
                        dve.wait_ge(s.gb, t + 1)
                        nc.vector.tensor_scalar(LA[:, p], LA[:, p], -20.0, None, ALU.max).then_inc(s.u, 1)
                    elif n in ("Q", "K"):
                        i = 2 * t + (n == "K")
                        dve.wait_ge(s.sq, i + 1)
                        if t >= 2:
                            ready(dve, ("KT", t - 2))
                            dve.wait_ge(s.kqd, 2 * (t - 1))
                            dve.wait_ge(s.rn, t - 1)
                        nc.vector.tensor_copy((QN if n == "Q" else KN)[:, p], pr).then_inc(s.qc if n == "Q" else s.kc, 1)
                        nc.vector.tensor_reduce(SS[:, p, i % 2, :], SQ[:, i % 2].rearrange("p (h d) -> p h d", d=D), AXX, ALU.add).then_inc(s.ssq, 1)
                        if n == "K":
                            dve.wait_ge(s.ssq, i + 1)
                            nc.vector.tensor_scalar(SS[:, p], SS[:, p], 1e-24, None, ALU.max).then_inc(s.ssm, 1)
                    elif n == "l":
                        dve.wait_ge(s.lg, t + 1)
                        nc.vector.tensor_scalar(LA[:, p], LA[:, p], -1.0, LN_MIN, ALU.mult, ALU.max).then_inc(s.la, 1)
                    elif n == "r":
                        dve.wait_ge(s.la, t + 1)
                        if t >= 2:
                            dve.wait_ge(s.rt, t - 1)
                        nc.vector.tensor_reduce(LM[:, p], LA[:, p].rearrange("p (h d) -> p h d", d=D), AXX, ALU.add).then_inc(s.lm, 1)
                    elif n == "KT":
                        ready(dve, (n, t))
                        if t:
                            ready(dve, ("SC", t - 1))
                        nc.vector.tensor_copy(KNT[:].rearrange("p j q -> p (j q)"), pr).then_inc(s.kt, 1)
                    elif n == "SC":
                        ready(dve, (n, t))
                        dve.wait_ge(s.dec, t + 1)
                        dve.wait_ge(s.zero, 1)
                        if t:
                            ready(dve, ("O", t - 1))
                        prh = pr.rearrange("p (h c) -> p h c", c=C)
                        nc.vector.tensor_tensor(AT0[0:C], prh[0:C], DEC[0:C], ALU.mult)
                        nc.vector.tensor_tensor(LH[C:P], prh[C:P], DEC[C:P], ALU.mult).then_inc(s.at, 1)
                    elif n == "S1":
                        ready(dve, (n, t))
                        if t >= 2:
                            ready(dve, ("O", t - 2))
                        nc.vector.tensor_copy(RH[0:D, p].rearrange("p h e -> p (h e)"), pr[0:D, :]).then_inc(s.s1, 1)
                    elif n == "OT":
                        ready(dve, (n, t))
                        if t:
                            ready(dve, ("OUT", t - 1))
                        nc.vector.tensor_copy(OT[:].rearrange("p j q -> p (j q)"), pr).then_inc(s.ot, 1)
                    elif n == "OUT":
                        ready(dve, (n, t))
                        nc.vector.tensor_tensor(E.r[:, t, :], pr[:, 0:P], E.x[:, t, :], ALU.add).then_inc(s.res, 1)


def ffn(nc, E, post_norm=False):
    W, PS = E.w, E.ps
    NH = 4
    with sublayer(nc, "xn xt_ps xt h_ps hid y_ps xr res po pr" + LN) as (s, ctx):
        sb = E.scratch(ctx)
        XN = sb("XN", [P, NB, P]); HT = sb("HT", [P, NG, NH, GT]); R = sb("R", [P, NB, P])
        with nc.Block() as block:
            @block.tensor
            def _(pe):
                for g in range(NG):
                    pe.wait_ge(s.xn, g + 1)
                    pe_transpose4(nc, [XN[:, g * GB + b, :] for b in range(GB)], PS[:, 6 + g, :], E.ident).then_inc(s.xt_ps, 1)
                for g in range(NG):
                    pe.wait_ge(s.xt, g + 1)
                    for j in range(NH):
                        k = g * NH + j
                        if k >= 4:
                            pe.wait_ge(s.hid, k - 3)
                        nc.tensor.matmul(PS[:, k % 4, :], W.fw1[:, j * P:(j + 1) * P], E.xt[:, g * GT:(g + 1) * GT], start=True, stop=True).then_inc(s.h_ps, 1)
                for g in range(NG):
                    pe.wait_ge(s.hid, (g + 1) * NH)
                    for b in range(GB):
                        o = PS[:, 4 + g, b * P:(b + 1) * P]
                        for j in range(NH):
                            ins = nc.tensor.matmul(o, HT[:, g, j, b * P:(b + 1) * P], W.fw2[:, j, :], start=j == 0, stop=j == NH - 1)
                    ins.then_inc(s.y_ps, 1)

            @block.scalar
            def _(act):
                for g in range(NG):
                    act_layernorm(nc, act, E, s, g)
                for g in range(NG):
                    act.wait_ge(s.xt_ps, g + 1)
                    nc.scalar.copy(E.xt[:, g * GT:(g + 1) * GT], PS[:, 6 + g, :]).then_inc(s.xt, 1)
                for k in range(NG * NH):
                    act.wait_ge(s.h_ps, k + 1)
                    nc.scalar.activation(HT[:, k // NH, k % NH, :], PS[:, k % 4, :], ACT.Gelu, bias=W.fb1[:, k % NH:k % NH + 1]).then_inc(s.hid, 1)
                for k in range(NG * (2 if post_norm else 1)):
                    act_layernorm(nc, act, E, s, NG + k)

            @block.gpsimd
            def _(pool):
                nc.gpsimd.tensor_tensor(R[:], E.r[:], bc(W.fb2.unsqueeze(1), [P, NB, P]), ALU.add).then_inc(s.xr, 1)
                if not post_norm:
                    pool.wait_ge(s.xr, 1)
                    nc.gpsimd.tensor_tensor(R[:], R[:], E.x[:], ALU.add).then_inc(s.xr, 1)

            @block.vector
            def _(dve):
                for g in range(NG):
                    dve_layernorm(nc, dve, E, s, g, grp(E.r, g), grp(XN, g), W.ln2w, W.ln2b).then_inc(s.xn, 1)
                dve.wait_ge(s.xr, 1 if post_norm else 2)
                for g in range(NG):
                    dve.wait_ge(s.y_ps, g + 1)
                    nc.vector.tensor_tensor(grp(R, g), grp(R, g), PS[:, 4 + g, :].rearrange("p (b d) -> p b d", b=GB), ALU.add).then_inc(s.res, 1)
                    dve.wait_ge(s.res, g + 1)
                    if post_norm:
                        dve_layernorm(nc, dve, E, s, NG + g, grp(R, g), grp(R, g), W.gout, W.bout).then_inc(s.po, 1)
                    else:
                        dve_layernorm(nc, dve, E, s, NG + g, grp(R, g), grp(E.x, g))
                if post_norm:
                    for g in range(NG):
                        dve.wait_ge(s.po, g + 1)
                        nc.vector.tensor_tensor(grp(R, g), grp(R, g), grp(E.x, g), ALU.add).then_inc(s.pr, 1)
                        dve.wait_ge(s.pr, g + 1)
                        dve_layernorm(nc, dve, E, s, 2 * NG + g, grp(R, g), grp(E.x, g))


MAGIC = 1.5 * 2.0 ** 23
TWO_PI_HI = 6.28125
TWO_PI_LO = 2 * math.pi - TWO_PI_HI


def l2_xattn_in(nc, E, prefetch=(), stores=None, coming=()):
    W, PS = E.w, E.ps
    H, D, TOP = 4, 32, 32
    CG = GB * L
    NRD = TOP // 8
    with sublayer(nc, "xt_ps xt q_ps q k_ps k v_ps v xn tm mb s_ps sc m8 wk sub ex ne nx exn den rden wh aw att at_ps at c_ps ct f_ps f x1 x2 mk bf w_ld st_x c_ld st" + LN) as (s, ctx):
        sb = E.scratch(ctx)
        U = sb("U", [P, NB, P]); FO = sb("FO", [P, NB, 2 * P])
        vmask = sb("vmask", [P, NB, L]); tmask = sb("tmask", [P, NB])
        QT = sb("QT", [P, NG, GT]); KT = sb("KT", [P, NB, L]); V = sb("V", [L, NB, P]); XN = sb("XN", [P, NB, P])
        MB = sb("MB", [P, NB, L]); TM = sb("TM", [P, NB])
        SC = sb("SC", [P, NG, H, GB, L]); WK = sb("WK", [P, H, GB, L]); M8 = sb("M8", [P, NG, NRD, H, GB, 8])
        EX = sb("EX", [P, NG, H, GB, L]); DEN = sb("DEN", [P, NG, H, GB]); WH = sb("WH", [P, NG, H, GB])
        ATT = sb("ATT", [P, NG, GB, L]); ATT_T = sb("ATT_T", [L, NG, GT]); CT = sb("CT", [P, NG, GT])
        F = sb("F", [P, 2, 2 * P]); BF = sb("BF", [P, 4 * P])
        with nc.Block() as block:
            @block.sync
            def _(sp):
                for dst, src in prefetch:
                    sp.dma_start(dst, src).then_inc(s.w_ld, 16)
                sp.dma_start(stores[1], E.x[:]).then_inc(s.st_x, 16)
                if coming:
                    sp.wait_ge(s.st_x, 16)
                    sp.wait_ge(s.xt_ps, NG)
                    sp.wait_ge(s.v_ps, NG)
                    sp.wait_ge(s.mk, 1)
                    sp.wait_ge(s.xn, NG)
                    for dst, part in coming:
                        sp.dma_start(dst, part).then_inc(s.c_ld, 16)
                    sp.wait_ge(s.c_ld, 16 * len(coming))
                for g in range(NG):
                    sp.wait_ge(s.x2, (g + 1) * GB)
                    sp.dma_start(stores[0][g][0], grp(U, g)).then_inc(s.st, 16)
                    sp.dma_start(stores[0][g][1], grp(FO, g)).then_inc(s.st, 16)
                sp.wait_ge(s.w_ld, 16 * len(prefetch))
                sp.wait_ge(s.st_x, 16)
                sp.wait_ge(s.st, 64)

            @block.tensor
            def _(pe):
                for g in range(NG):
                    pe_transpose4(nc, [E.x[:, g * GB + b, :] for b in range(GB)], PS[:, g, :], E.ident).then_inc(s.xt_ps, 1)
                for g in range(NG):
                    nc.tensor.matmul(PS[:, 2 + g, 0:CG], W.wk, E.ctxT[:, g * GB:(g + 1) * GB, :].rearrange("c b l -> c (b l)"),
                                     start=True, stop=True).then_inc(s.k_ps, 1)
                    for b in range(GB):
                        ins = nc.tensor.matmul(PS[0:L, 4 + g, b * P:(b + 1) * P], E.ctxT[:, g * GB + b, :], W.wv, start=True, stop=True)
                    ins.then_inc(s.v_ps, 1)
                for g in range(NG):
                    pe.wait_ge(s.xt, g + 1)
                    nc.tensor.matmul(PS[:, 6 + g, :], W.wq, E.xt[:, g * GT:(g + 1) * GT], start=True, stop=True).then_inc(s.q_ps, 1)
                for g in range(NG):
                    pe.wait_ge(s.q, NG)
                    pe.wait_ge(s.k, NG)
                    pe.wait_ge(s.v, NG)
                    for b in range(GB):
                        for h in range(H):
                            ins = nc.tensor.matmul(PS[:, 4 * g + h, b * L:(b + 1) * L], QT[h * D:(h + 1) * D, g, b * P:(b + 1) * P],
                                                   KT[h * D:(h + 1) * D, g * GB + b, :], start=True, stop=True)
                    ins.then_inc(s.s_ps, 1)
                pe.wait_ge(s.sc, NG)
                for g in range(NG):
                    pe.wait_ge(s.att, g + 1)
                    for b in range(GB):
                        ins = nc.tensor.transpose(PS[0:L, g, b * P:(b + 1) * P], ATT[:, g, b, :], E.ident)
                    ins.then_inc(s.at_ps, 1)
                    pe.wait_ge(s.at, g + 1)
                    for b in range(GB):
                        ins = nc.tensor.matmul(PS[:, 2 + g, b * P:(b + 1) * P], V[:, g * GB + b, :], ATT_T[:, g, b * P:(b + 1) * P],
                                               start=True, stop=True)
                    ins.then_inc(s.c_ps, 1)
                    pe.wait_ge(s.ct, g + 1)
                    for b in range(GB):
                        t = g * GB + b
                        if t >= 4:
                            pe.wait_ge(s.f, t - 3)
                        nc.tensor.matmul(PS[:, 4 + t % 4, :], CT[:, g, b * P:(b + 1) * P], W.wf, start=True, stop=True).then_inc(s.f_ps, 1)

            @block.scalar
            def _(act):
                for g in range(NG):
                    act.wait_ge(s.xt_ps, g + 1)
                    nc.scalar.copy(E.xt[:, g * GT:(g + 1) * GT], PS[:, g, :]).then_inc(s.xt, 1)
                for g in range(NG):
                    act.wait_ge(s.q_ps, g + 1)
                    nc.scalar.copy(QT[:, g, :], PS[:, 6 + g, :]).then_inc(s.q, 1)
                for g in range(NG):
                    act_layernorm(nc, act, E, s, g)
                for g in range(NG):
                    act.wait_ge(s.sub, g + 1)
                    nc.scalar.activation(EX[:, g], EX[:, g], ACT.Exp, scale=float(D) ** -0.5).then_inc(s.ex, 1)
                for g in range(NG):
                    act.wait_ge(s.at_ps, g + 1)
                    nc.scalar.copy(ATT_T[:, g, :], PS[0:L, g, :]).then_inc(s.at, 1)
                    act.wait_ge(s.c_ps, g + 1)
                    nc.scalar.copy(CT[:, g, :], PS[:, 2 + g, :]).then_inc(s.ct, 1)

            @block.gpsimd
            def _(pool):
                nc.gpsimd.tensor_tensor(BF[:], W.bf, bc(W.mg, [P, 4 * P]), ALU.mult).then_inc(s.bf, 1)
                for g in range(NG):
                    pool.wait_ge(s.m8, NRD * g + 1)
                    nc.gpsimd.tensor_tensor(EX[:, g], SC[:, g], bc(M8[:, g, 0, :, :, 0:1], [P, H, GB, L]), ALU.subtract).then_inc(s.sub, 1)
                    pool.wait_ge(s.wh, g + 1)
                    nc.gpsimd.tensor_tensor(EX[:, g], EX[:, g], bc(WH[:, g].unsqueeze(3), [P, H, GB, L]), ALU.mult).then_inc(s.aw, 1)

            @block.vector
            def _(dve):
                for g in range(NG):
                    dve.wait_ge(s.k_ps, g + 1)
                    nc.vector.tensor_copy(KT[:, g * GB:(g + 1) * GB, :].rearrange("p b l -> p (b l)"), PS[:, 2 + g, 0:CG]).then_inc(s.k, 1)
                for g in range(NG):
                    dve.wait_ge(s.v_ps, g + 1)
                    nc.vector.tensor_copy(V[:, g * GB:(g + 1) * GB, :].rearrange("p b d -> p (b d)"), PS[0:L, 4 + g, :]).then_inc(s.v, 1)
                nc.vector.tensor_copy(vmask[:], E.vmask8[:])
                nc.vector.tensor_copy(tmask[:], E.tmask8[:]).then_inc(s.mk, 1)
                dve.wait_ge(s.mk, 1)
                nc.vector.tensor_scalar(MB[:], vmask[:], 1e30, -1e30, ALU.mult, ALU.add).then_inc(s.mb, 1)
                nc.vector.tensor_scalar(TM[:], tmask[:], 1.0 / H, None, ALU.mult).then_inc(s.tm, 1)
                for g in range(NG):
                    dve_layernorm(nc, dve, E, s, g, grp(E.x, g), grp(XN, g), W.gin, W.bin).then_inc(s.xn, 1)
                dve.wait_ge(s.xn, NG)

                def modulate(g):
                    if g == 0:
                        dve.wait_ge(s.bf, 1)
                    for t in range(g * GB, (g + 1) * GB):
                        f = PS[:, 4 + t % 4, :]
                        dve.wait_ge(s.f_ps, t + 1)
                        if t >= 2:
                            dve.wait_ge(s.x2, t - 1)
                        nc.vector.scalar_tensor_tensor(F[:, t % 2, :], f[:, 0:2 * P], W.mg, BF[:, 0:2 * P], ALU.mult, ALU.add)
                        nc.vector.scalar_tensor_tensor(FO[:, t, :], f[:, 2 * P:4 * P], W.mg, BF[:, 2 * P:4 * P], ALU.mult, ALU.add).then_inc(s.f, 1)
                        dve.wait_ge(s.f, t + 1)
                        nc.vector.scalar_tensor_tensor(U[:, t, :], F[:, t % 2, 0:P], 1.0, XN[:, t, :], ALU.add, ALU.mult).then_inc(s.x1, 1)
                        dve.wait_ge(s.x1, t + 1)
                        nc.vector.tensor_tensor(U[:, t, :], U[:, t, :], F[:, t % 2, P:2 * P], ALU.add).then_inc(s.x2, 1)

                dve.wait_ge(s.mb, 1)
                for g in range(NG):
                    dve.wait_ge(s.s_ps, g + 1)
                    nc.vector.tensor_tensor(SC[:, g], PS[:, 4 * g:4 * g + 4, 0:CG].rearrange("p h (b l) -> p h b l", b=GB),
                                            bc(MB[:, g * GB:(g + 1) * GB, :].unsqueeze(1), [P, H, GB, L]), ALU.add).then_inc(s.sc, 1)
                for g in range(NG):
                    dve.wait_ge(s.sc, g + 1)
                    if g:
                        dve.wait_ge(s.ne, g)
                    for r in range(NRD):
                        src = SC[:, g] if r == 0 else WK[:]
                        for h in range(H):
                            for b in range(GB):
                                ins = nc.vector.max(M8[:, g, r, h, b, :], src[:, h, b, :])
                        ins.then_inc(s.m8, 1)
                        dve.wait_ge(s.m8, NRD * g + r + 1)
                        for h in range(H):
                            for b in range(GB):
                                ins = nc.vector.match_replace(WK[:, h, b, :], M8[:, g, r, h, b, :], src[:, h, b, :], -3e38)
                        ins.then_inc(s.wk, 1)
                        dve.wait_ge(s.wk, NRD * g + r + 1)
                    dve.wait_ge(s.sub, g + 1)
                    nc.vector.tensor_tensor(SC[:, g], WK[:], SC[:, g], ALU.not_equal).then_inc(s.ne, 1)
                    dve.wait_ge(s.ne, g + 1)
                    dve.wait_ge(s.ex, g + 1)
                    nc.vector.tensor_tensor(EX[:, g], EX[:, g], SC[:, g], ALU.mult).then_inc(s.nx, 1)
                    dve.wait_ge(s.nx, g + 1)
                    nc.vector.tensor_reduce(DEN[:, g], EX[:, g], AXX, ALU.add).then_inc(s.den, 1)
                    dve.wait_ge(s.den, g + 1)
                    nc.vector.reciprocal(DEN[:, g], DEN[:, g]).then_inc(s.rden, 1)
                    dve.wait_ge(s.rden, g + 1)
                    dve.wait_ge(s.tm, 1)
                    nc.vector.tensor_tensor(WH[:, g], DEN[:, g], bc(TM[:, g * GB:(g + 1) * GB].unsqueeze(1), [P, H, GB]), ALU.mult).then_inc(s.wh, 1)
                    if g == 1:
                        modulate(0)
                    dve.wait_ge(s.aw, g + 1)
                    nc.vector.tensor_reduce(ATT[:, g], EX[:, g].rearrange("p h b l -> p b l h"), AXX, ALU.add).then_inc(s.att, 1)
                modulate(1)


def s4d_kernel(nc, E, k_dram, prefetch=()):
    W = E.w
    N = 64
    LC = 16
    NCH = P // LC
    with sublayer(nc, "dt dta ph era kk kr r1 r2 rc er sh si co1 co num0 num a2 ra prod dcr m1 m2 d1 w k0 k_st z w_ld") as (s, ctx):
        sb = E.scratch(ctx)
        DT = sb("DT", [P, 1]); ARE = sb("ARE", [P, N]); AIM = sb("AIM", [P, N])
        PH = sb("PH", [P, 2, LC, N]); KK = sb("KK", [P, 2, LC, N]); RC = sb("RC", [P, 2, LC, N])
        ER = sb("ER", [P, 2, LC, N]); SH = sb("SH", [P, 2, LC, N]); SI = sb("SI", [P, 2, LC, N])
        NR_ = sb("NR", [P, N]); NI = sb("NI", [P, N]); T = [sb(f"T{i}", [P, N]) for i in range(8)]
        KP = sb("KP", [P, 2 * P])
        DCR = sb("DCR", [P, N]); DCI = sb("DCI", [P, N])
        full = [P, LC, N]
        with nc.Block() as block:
            @block.scalar
            def _(act):
                nc.scalar.activation(DT[:], W.log_dt, ACT.Exp).then_inc(s.dt, 1)
                for c in range(NCH):
                    p = c % 2
                    act.wait_ge(s.era, c + 1)
                    nc.scalar.activation(ER[:, p], ER[:, p], ACT.Exp).then_inc(s.er, 1)
                    act.wait_ge(s.rc, c + 1)
                    if c >= 2:
                        act.wait_ge(s.w, c - 1)
                    nc.scalar.activation(SH[:, p], RC[:, p], ACT.Sin, scale=0.5).then_inc(s.sh, 1)
                    nc.scalar.activation(SI[:, p], RC[:, p], ACT.Sin).then_inc(s.si, 1)
                    act.wait_ge(s.sh, c + 1)
                    nc.scalar.activation(SH[:, p], SH[:, p], ACT.Square).then_inc(s.co1, 1)

            @block.gpsimd
            def _(pool):
                for c in range(NCH):
                    p = c % 2
                    pool.wait_ge(s.dta, 2)
                    lt = bc(E.times[:, c * LC:(c + 1) * LC].unsqueeze(2), full)
                    if c >= 2:
                        pool.wait_ge(s.r2, c - 1)
                    nc.gpsimd.tensor_tensor(PH[:, p], bc(AIM[:].unsqueeze(1), full), lt, ALU.mult).then_inc(s.ph, 1)
                    if c >= 2:
                        pool.wait_ge(s.w, c - 1)
                    nc.gpsimd.tensor_tensor(ER[:, p], bc(ARE[:].unsqueeze(1), full), lt, ALU.mult).then_inc(s.era, 1)

            @block.vector
            def _(dve):
                v = nc.vector
                v.memset(KP[:, 0:P], 0.0)
                dve.wait_ge(s.dt, 1)
                v.tensor_scalar(ARE[:], W.a_re, DT[:], None, ALU.mult).then_inc(s.dta, 1)
                v.tensor_scalar(AIM[:], W.a_im, DT[:], None, ALU.mult).then_inc(s.dta, 1)

                def reduce_angle(c):
                    p = c % 2
                    dve.wait_ge(s.ph, c + 1)
                    v.tensor_scalar(KK[:, p], PH[:, p], 1.0 / (2 * math.pi), MAGIC, ALU.mult, ALU.add).then_inc(s.kk, 1)
                    dve.wait_ge(s.kk, c + 1)
                    v.tensor_scalar(KK[:, p], KK[:, p], MAGIC, None, ALU.subtract).then_inc(s.kr, 1)
                    dve.wait_ge(s.kr, c + 1)
                    v.scalar_tensor_tensor(PH[:, p], KK[:, p], -TWO_PI_HI, PH[:, p], ALU.mult, ALU.add).then_inc(s.r1, 1)
                    dve.wait_ge(s.r1, c + 1)
                    if c >= 2:
                        dve.wait_ge(s.si, c - 1)
                    v.scalar_tensor_tensor(RC[:, p], KK[:, p], -TWO_PI_LO, PH[:, p], ALU.mult, ALU.add).then_inc(s.r2, 1)
                    dve.wait_ge(s.r2, c + 1)
                    v.tensor_scalar(RC[:, p], RC[:, p], 3.1415925, -3.1415925, ALU.min, ALU.max).then_inc(s.rc, 1)

                def coefficients():
                    er, co, si = ER[:, 0, 1, :], SH[:, 0, 1, :], SI[:, 0, 1, :]
                    n = [0]

                    def link(ins):
                        n[0] += 1
                        ins.then_inc(s.prod, 1)
                        dve.wait_ge(s.prod, n[0])
                    link(v.tensor_tensor(NR_[:], er, co, ALU.mult))
                    link(v.tensor_scalar(NR_[:], NR_[:], 1.0, None, ALU.subtract))
                    link(v.tensor_tensor(NI[:], er, si, ALU.mult))
                    link(v.tensor_tensor(T[0][:], W.a_re, W.a_re, ALU.mult))
                    link(v.tensor_tensor(T[1][:], W.a_im, W.a_im, ALU.mult))
                    link(v.tensor_tensor(T[0][:], T[0][:], T[1][:], ALU.add))
                    link(v.reciprocal(T[0][:], T[0][:]))
                    link(v.tensor_tensor(T[1][:], W.c_re, NR_[:], ALU.mult))
                    link(v.tensor_tensor(T[2][:], W.c_im, NI[:], ALU.mult))
                    link(v.tensor_tensor(T[1][:], T[1][:], T[2][:], ALU.subtract))
                    link(v.tensor_tensor(T[2][:], W.c_re, NI[:], ALU.mult))
                    link(v.tensor_tensor(T[3][:], W.c_im, NR_[:], ALU.mult))
                    link(v.tensor_tensor(T[2][:], T[2][:], T[3][:], ALU.add))
                    link(v.tensor_tensor(T[3][:], T[1][:], W.a_re, ALU.mult))
                    link(v.tensor_tensor(T[4][:], T[2][:], W.a_im, ALU.mult))
                    link(v.tensor_tensor(T[3][:], T[3][:], T[4][:], ALU.add))
                    link(v.tensor_tensor(T[5][:], T[2][:], W.a_re, ALU.mult))
                    link(v.tensor_tensor(T[6][:], T[1][:], W.a_im, ALU.mult))
                    link(v.tensor_tensor(T[5][:], T[5][:], T[6][:], ALU.subtract))
                    link(v.tensor_tensor(DCR[:], T[3][:], T[0][:], ALU.mult))
                    link(v.tensor_tensor(DCI[:], T[5][:], T[0][:], ALU.mult))
                    link(v.tensor_scalar(DCR[:], DCR[:], 2.0, None, ALU.mult))
                    link(v.tensor_scalar(DCI[:], DCI[:], 2.0, None, ALU.mult))

                def accumulate(c):
                    p = c % 2
                    dve.wait_ge(s.co1, c + 1)
                    v.tensor_scalar(SH[:, p], SH[:, p], -2.0, 1.0, ALU.mult, ALU.add).then_inc(s.co, 1)
                    dve.wait_ge(s.co, c + 1)
                    dve.wait_ge(s.er, c + 1)
                    dve.wait_ge(s.si, c + 1)
                    if c == 0:
                        coefficients()
                    v.tensor_tensor(SH[:, p], SH[:, p], bc(DCR[:].unsqueeze(1), full), ALU.mult).then_inc(s.m1, 1)
                    v.tensor_tensor(SI[:, p], SI[:, p], bc(DCI[:].unsqueeze(1), full), ALU.mult).then_inc(s.m2, 1)
                    dve.wait_ge(s.m1, c + 1)
                    dve.wait_ge(s.m2, c + 1)
                    v.tensor_tensor(SH[:, p], SH[:, p], SI[:, p], ALU.subtract).then_inc(s.d1, 1)
                    dve.wait_ge(s.d1, c + 1)
                    v.tensor_tensor(SH[:, p], SH[:, p], ER[:, p], ALU.mult).then_inc(s.num, 1)
                    dve.wait_ge(s.num, c + 1)
                    v.tensor_reduce(KP[:, P + c * LC:P + (c + 1) * LC], SH[:, p], AXX, ALU.add).then_inc(s.w, 1)

                reduce_angle(0)
                for c in range(NCH):
                    if c + 1 < NCH:
                        reduce_angle(c + 1)
                    accumulate(c)
                dve.wait_ge(s.w, NCH)
                v.tensor_tensor(KP[:, P:P + 1], KP[:, P:P + 1], W.dskip, ALU.add).then_inc(s.z, 1)

            @block.sync
            def _(sp):
                for dst, src in prefetch:
                    sp.dma_start(dst, src).then_inc(s.w_ld, 16)
                sp.wait_ge(s.w_ld, 16 * len(prefetch))
                sp.wait_ge(s.z, 1)
                sp.dma_start(k_dram, KP[:]).then_inc(s.k_st, 16)
                sp.wait_ge(s.k_st, 16)


def s4d_conv(nc, E, k_dram, u_dram, y_dram, prefetch):
    PS = E.ps
    DCH = 16
    NCH = P // DCH
    with sublayer(nc, "u_ld t_ld0 t_ld1 ur_ps ur y_ps y y_st w_ld") as (s, ctx):
        sb = E.scratch(ctx)
        U = sb("U", [P, B_ALL, P]); Y = sb("Y", [P, B_ALL, P]); T = sb("T", [P, 2, DCH, P]); UR = sb("UR", [P, B_ALL, P])
        t_ld = [s.t_ld0, s.t_ld1]
        with nc.Block() as block:
            @block.sync
            def _(sp):
                sp.dma_start(U[:], u_dram).then_inc(s.u_ld, 16)
                for c in range(NCH):
                    if c >= 2:
                        sp.wait_ge(s.y_ps, c - 1)
                    src = k_dram[c * DCH:(c + 1) * DCH, :]
                    toeplitz = bass.AP(tensor=src.tensor, offset=src.offset + 1, ap=[[1, P], [2 * P, DCH], [1, P]])
                    sp.dma_start(T[:, c % 2], toeplitz).then_inc(t_ld[c % 2], 16)
                sp.wait_ge(s.y, NCH)
                sp.dma_start(y_dram, Y[:]).then_inc(s.y_st, 16)
                sp.wait_ge(s.y_st, 16)

            @block.scalar
            def _(act):
                for dst, src in prefetch:
                    act.dma_start(dst, src).then_inc(s.w_ld, 16)
                act.wait_ge(s.w_ld, 16 * len(prefetch))

            @block.tensor
            def _(pe):
                pe.wait_ge(s.u_ld, 16)
                for c in range(8):
                    nc.tensor.matmul(PS[:, c, :], E.flip, U[:, 4 * c:4 * c + 4, :].rearrange("p b d -> p (b d)"), start=True, stop=True).then_inc(s.ur_ps, 1)
                pe.wait_ge(s.ur, 8)
                for c in range(NCH):
                    pe.wait_ge(t_ld[c % 2], 16 * (c // 2 + 1))
                    for i in range(DCH):
                        ins = nc.tensor.matmul(PS[:, c, i * B_ALL:(i + 1) * B_ALL], T[:, c % 2, i, :], UR[:, :, c * DCH + i], start=True, stop=True)
                    ins.then_inc(s.y_ps, 1)

            @block.vector
            def _(dve):
                for c in range(8):
                    dve.wait_ge(s.ur_ps, c + 1)
                    nc.vector.tensor_copy(UR[:, 4 * c:4 * c + 4, :].rearrange("p b d -> p (b d)"), PS[:, c, :]).then_inc(s.ur, 1)
                for c in range(NCH):
                    dve.wait_ge(s.y_ps, c + 1)
                    nc.vector.tensor_copy(Y[:, :, c * DCH:(c + 1) * DCH], PS[:, c, :].rearrange("p (i b) -> p b i", i=DCH)).then_inc(s.y, 1)


def l2_xattn_out(nc, E):
    with sublayer(nc, "m1 m2 m3 xc") as (s, ctx):
        with nc.Block() as block:
            @block.vector
            def _(dve):
                nc.vector.scalar_tensor_tensor(E.r[:], E.fo[:, :, 0:P], 1.0, E.u[:], ALU.add, ALU.mult).then_inc(s.m1, 1)
                dve.wait_ge(s.m1, 1)
                nc.vector.tensor_tensor(E.r[:], E.r[:], E.fo[:, :, P:2 * P], ALU.add).then_inc(s.m2, 1)
                dve.wait_ge(s.m2, 1)
                nc.vector.tensor_tensor(E.r[:], E.r[:], E.x_next[:], ALU.add).then_inc(s.m3, 1)

            @block.scalar
            def _(act):
                nc.scalar.copy(E.x[:].rearrange("p b d -> p (b d)"), E.x_next[:].rearrange("p b d -> p (b d)")).then_inc(s.xc, 1)
    ffn(nc, E, post_norm=True)


def l3_attn(nc, E):
    W = E.w
    PS = E.ps
    with sublayer(nc, "xt_ps xt qk_ps qk v_ps v s_ps mx sub ex pt_ps pt z_ps rz zn res" + LN) as (s, ctx):
        sb = E.scratch(ctx)
        QT = sb("QT", [P, 2, GT]); KT = sb("KT", [P, 2, GT]); VA = sb("VA", [P, 2, GB, P + 1])
        nmax = sb("nmax", [P, 2, GB]); SM = sb("SM", [P, 2, GB, P]); PT = sb("PT", [P, 2, GB, P])
        rz = sb("rz", [P, 2, GB]); R = sb("R", [P, NB, P])
        with nc.Block() as block:
            @block.tensor
            def _(pe):
                for g in range(NG):
                    pe_transpose4(nc, [E.x[:, g * GB + b, :] for b in range(GB)], PS[:, g, :], E.ident).then_inc(s.xt_ps, 1)
                for g in range(NG):
                    pe.wait_ge(s.xt, g + 1)
                    xt = E.xt[:, g * GT:(g + 1) * GT]
                    nc.tensor.matmul(PS[:, 2 + g, :], W.wq, xt, start=True, stop=True)
                    nc.tensor.matmul(PS[:, 4 + g, :], W.wk, xt, start=True, stop=True).then_inc(s.qk_ps, 1)
                    for b in range(GB):
                        o = PS[:, 6 + g, b * P:(b + 1) * P]
                        ins = nc.tensor.matmul(o, xt[:, b * P:(b + 1) * P], W.wv, start=True, stop=True)
                    ins.then_inc(s.v_ps, 1)
                for g in range(NG):
                    pe.wait_ge(s.qk, 2 * g + 2)
                    for b in range(GB):
                        ins = nc.tensor.matmul(PS[:, g, b * P:(b + 1) * P], QT[:, g, b * P:(b + 1) * P],
                                               KT[:, g, b * P:(b + 1) * P], start=True, stop=True)
                    ins.then_inc(s.s_ps, 1)
                for g in range(NG):
                    pe.wait_ge(s.ex, g + 1)
                    pe_transpose4(nc, [SM[:, g, b, :] for b in range(GB)], PS[:, 2 + g, :], E.ident).then_inc(s.pt_ps, 1)
                for g in range(NG):
                    pe.wait_ge(s.pt, g + 1)
                    pe.wait_ge(s.v, g + 1)
                    for b in range(GB):
                        o = PS[:, (4 if b < 2 else 6) + g, (b % 2) * (P + 1):(b % 2 + 1) * (P + 1)]
                        ins = nc.tensor.matmul(o, PT[:, g, b, :], VA[:, g, b, :], start=True, stop=True)
                    ins.then_inc(s.z_ps, 1)

            @block.scalar
            def _(act):
                for g in range(NG):
                    act.wait_ge(s.xt_ps, g + 1)
                    nc.scalar.copy(E.xt[:, g * GT:(g + 1) * GT], PS[:, g, :]).then_inc(s.xt, 1)
                for g in range(NG):
                    act.wait_ge(s.qk_ps, g + 1)
                    nc.scalar.activation(QT[:, g, :], PS[:, 2 + g, :], ACT.Identity, bias=W.bq).then_inc(s.qk, 1)
                    nc.scalar.activation(KT[:, g, :], PS[:, 4 + g, :], ACT.Identity, bias=W.bk).then_inc(s.qk, 1)
                for g in range(NG):
                    act.wait_ge(s.sub, g + 1)
                    nc.scalar.activation(SM[:, g], SM[:, g], ACT.Exp, scale=float(P) ** -0.5).then_inc(s.ex, 1)
                for g in range(NG):
                    act.wait_ge(s.pt_ps, g + 1)
                    nc.scalar.copy(PT[:, g].rearrange("p b q -> p (b q)"), PS[:, 2 + g, :]).then_inc(s.pt, 1)
                act_table(nc, E, ACT.Sqrt)
                for g in range(NG):
                    act_layernorm(nc, act, E, s, g)

            @block.vector
            def _(dve):
                for g in range(NG):
                    nc.vector.memset(VA[:, g, :, P:P + 1], 1.0)
                    dve.wait_ge(s.v_ps, g + 1)
                    nc.vector.tensor_tensor(VA[:, g, :, 0:P], PS[:, 6 + g, :].rearrange("p (b d) -> p b d", b=GB),
                                            bc(W.bv.unsqueeze(1), [P, GB, P]), ALU.add).then_inc(s.v, 1)
                for g in range(NG):
                    sc = PS[:, g, :].rearrange("p (b k) -> p b k", b=GB)
                    dve.wait_ge(s.s_ps, g + 1)
                    nc.vector.tensor_reduce(nmax[:, g, :], sc, AXX, ALU.max).then_inc(s.mx, 1)
                    dve.wait_ge(s.mx, g + 1)
                    nc.vector.tensor_tensor(SM[:, g], sc, bc(nmax[:, g, :].unsqueeze(2), [P, GB, P]), ALU.subtract).then_inc(s.sub, 1)
                for g in range(NG):
                    dve.wait_ge(s.z_ps, g + 1)
                    for h in range(2):
                        z = PS[:, 4 + 2 * h + g, 0:2 * (P + 1)].rearrange("p (b d) -> p b d", b=2)
                        ins = nc.vector.reciprocal(rz[:, g, 2 * h:2 * h + 2], z[:, :, P])
                    ins.then_inc(s.rz, 1)
                    dve.wait_ge(s.rz, g + 1)
                    for b in range(GB):
                        z = PS[:, 4 + 2 * (b // 2) + g, (b % 2) * (P + 1):(b % 2) * (P + 1) + P]
                        ins = nc.vector.scalar_tensor_tensor(R[:, g * GB + b, :], z, rz[:, g, b:b + 1],
                                                             E.x[:, g * GB + b, :], ALU.mult, ALU.add)
                    ins.then_inc(s.res, 1)
                    dve.wait_ge(s.res, g + 1)
                    dve_layernorm(nc, dve, E, s, g, grp(R, g), grp(E.x, g))


PASSES = B_ALL // NB

LAYER_A = ["l0_xattn", "l0_ffn", "l1_attn", "l1_xattn", "l1_ffn", "l2_mix"]
LAYER_B = ["l2_ffw", "l2_ffn", "l3_attn", "l3_xattn", "l3_ffn"]


def load_weights(nc, ctx, E, dram, layers):
    todo = []
    for layer in layers:
        w = {}
        for key, ap in dram.items():
            if key.startswith(layer + "__"):
                t = ctx.enter_context(nc.sbuf_tensor("sb_" + key, list(ap.shape), F32))
                w[key[len(layer) + 2:]] = t[:]
                todo.append((t[:], ap))
        if layer == "l0_ffn":
            w["b1lin"] = ctx.enter_context(nc.sbuf_tensor("sb_b1lin", [P, 8, 2], F32))[:]
        E.weights[layer] = namedtuple("Weights", w)(**w)
    return todo


def load_block(nc, todo):
    with sublayer(nc, "ld_sp ld_act") as (s, ctx):
        with nc.Block() as block:
            @block.sync
            def _(sp):
                part = todo[0::2]
                for dst, src in part:
                    sp.dma_start(dst, src).then_inc(s.ld_sp, 16)
                if part:
                    sp.wait_ge(s.ld_sp, 16 * len(part))

            @block.scalar
            def _(act):
                part = todo[1::2]
                for dst, src in part:
                    act.dma_start(dst, src).then_inc(s.ld_act, 16)
                if part:
                    act.wait_ge(s.ld_act, 16 * len(part))


def decoder(nc, dram, out):
    with ExitStack() as top:
        E = Environment()
        E.weights = {}
        alloc_common(nc, top, E)
        scratch_dram = lambda n, shape: nc.dram_tensor(n, shape, F32, kind="Internal").ap()
        k_dram = scratch_dram("s4d_k_dram", [P, 2 * P])
        u_dram = scratch_dram("s4d_u_dram", [P, B_ALL, P])
        y_dram = scratch_dram("s4d_y_dram", [P, B_ALL, P])
        x_dram = scratch_dram("x_mid_dram", [P, B_ALL, P])
        fo_dram = scratch_dram("film_dram", [P, B_ALL, 2 * P])

        def consts(ctx, which):
            todo, c = [], {}
            for key, ap in dram.items():
                if key.startswith(which):
                    t = ctx.enter_context(nc.sbuf_tensor("sb_" + key, list(ap.shape), F32))
                    c[key[len(which):]] = t[:]
                    todo.append((t[:], ap))
            return c, todo

        c, common = consts(top, "c_")
        E.ident, E.ones_row, E.eps5, E.eps6, E.one = c["ident"], c["ones_row"], c["eps5"], c["eps6"], c["one"]
        E.ln2_20, E.headmask, E.flip = c["ln2_20"], c["headmask"], c["flip"]

        def run(layer, fn, **kw):
            E.w = E.weights[layer]
            fn(nc, E, **kw)

        with ExitStack() as first:
            c, todo = consts(first, "a_")
            E.blockmask, E.cos, E.sin, E.causal = c["blockmask"], c["cos"], c["sin"], c["causal"]
            E.gla_sum, E.gla_after, E.gla_upto, E.gla_tril = c["gla_sum"], c["gla_after"], c["gla_upto"], c["gla_tril"]
            todo += load_weights(nc, first, E, dram, LAYER_A)
            SHARED = 7812
            shared = first.enter_context(nc.sbuf_tensor("shared_weights", [P, SHARED], F32))
            turns = {}
            for layer in ("l0_attn", "l2_attn"):
                w, at, pairs = {}, 0, []
                for key, ap in dram.items():
                    if key.startswith(layer + "__"):
                        shape = list(ap.shape)
                        n = 1
                        for d in shape[1:]:
                            n *= d
                        t = shared[0:shape[0], at:at + n]
                        if len(shape) == 3:
                            t = t.rearrange("p (a b) -> p a b", a=shape[1])
                        w[key[len(layer) + 2:]] = t
                        pairs.append((t, ap))
                        at += n
                assert at <= SHARED, at
                E.weights[layer], turns[layer] = namedtuple("Weights", w)(**w), pairs
            inputs = lambda at: [(E.x[:], dram["x"][:, at]), (E.ctxT[:], dram["ctxT"][:, at]),
                                 (E.vmask8[:], dram["vmask"][:, at]), (E.tmask8[:], dram["tmask"][:, at])]
            with ExitStack() as pre:
                c, mine = consts(pre, "k_")
                E.times = c["times"]
                load_block(nc, load_weights(nc, pre, E, dram, ["s4d"]) + mine)
                run("s4d", s4d_kernel, k_dram=k_dram, prefetch=inputs(slice(0, NB)) + common + turns["l0_attn"] + todo)
            with nc.Fori(0, PASSES) as i:
                mine = lambda ap: ap[:, bass.ds(i * NB, NB)]
                run("l0_attn", l0_attn)
                run("l0_xattn", l0_xattn, prefetch=turns["l2_attn"])
                run("l0_ffn", l0_ffn)
                run("l1_attn", l1_attn)
                run("l1_xattn", l1_xattn)
                run("l1_ffn", l1_ffn)
                run("l2_attn", l2_attn)
                run("l2_mix", l2_xattn_in, prefetch=turns["l0_attn"],
                    stores=([(u_dram[:, at], fo_dram[:, at]) for at in (bass.ds(i * NB + g * GB, GB) for g in range(NG))], mine(x_dram)),
                    coming=inputs(bass.ds((i * NB + NB) % B_ALL, NB)))

        with ExitStack() as second:
            todo = load_weights(nc, second, E, dram, LAYER_B)
            E.w = None
            s4d_conv(nc, E, k_dram, u_dram, y_dram, todo)
            E.u = second.enter_context(nc.sbuf_tensor("s4d_out", [P, NB, P], F32))
            E.fo = second.enter_context(nc.sbuf_tensor("film_out", [P, NB, 2 * P], F32))
            E.x_next = second.enter_context(nc.sbuf_tensor("x_next", [P, NB, P], F32))
            inputs = lambda at: [(E.x_next[:], x_dram[:, at]), (E.u[:], y_dram[:, at]), (E.fo[:], fo_dram[:, at]), (E.ctxT[:], dram["ctxT"][:, at])]
            load_block(nc, inputs(slice(0, NB)))
            with nc.Fori(0, PASSES) as i:
                run("l2_ffw", l2_xattn_out)
                run("l2_ffn", l2_ffn)
                run("l3_attn", l3_attn)
                run("l3_xattn", l3_xattn)
                run("l3_ffn", l3_ffn, coming=inputs(bass.ds((i * NB + NB) % B_ALL, NB)),
                    store=[out[:, bass.ds(i * NB + g * GB, GB)] for g in range(NG)])


def layout(i):
    import numpy as np

    col = lambda v: v.reshape(-1, 1)
    row = lambda v: v.reshape(1, -1)
    rep = lambda v: np.broadcast_to(v.reshape(1, -1), (P, v.size))
    split = lambda w: w.reshape(w.shape[0] // P, P, w.shape[1]).transpose(1, 0, 2)
    esplit = lambda w: w.reshape(w.shape[0], w.shape[1] // P, P, w.shape[2]).transpose(2, 0, 1, 3)
    d = {}

    def put(layer, **arrays):
        for k, a in arrays.items():
            d[f"{layer}__{k}"] = a

    g = lambda n: i["L0_attn_" + n]
    l0 = {}
    for n in "QK":
        w, b = g("W_" + n).transpose(1, 0, 2), g("b_" + n)
        l0["w" + n.lower()] = w.reshape(P, 1024)
        l0["w" + n.lower() + "f"] = w.reshape(P, 32, 2, 16)[:, :, ::-1].reshape(P, 1024)
        l0["b" + n.lower()] = b.reshape(8, P).T
        l0["b" + n.lower() + "f"] = b.reshape(32, 2, 16)[:, ::-1].reshape(8, P).T
    vv = np.zeros((8, 16, 4, 16, 8), np.float32)
    v = g("virtual_v").reshape(16, 4, 8, 8)
    vk = np.zeros((4, 32, 8, 4, 16), np.float32)
    for h in range(8):
        for r in range(4):
            vv[h, :, r, 8 * (r % 2) + h, :] = v[:, r, h, :]
    for h in range(4):
        vk[h, :, :, h, :] = g("virtual_k").reshape(16, 8, 4, 32)[:, :, h].transpose(2, 1, 0)
    put("l0_attn", **l0, wv=g("W_V")[:, :, 0].T, bv=rep(g("b_V")), wo=split(g("W_O")[:, 0, :]),
        vk=vk.reshape(P, 8, 64), vv=vv.reshape(P, 4, P))
    g = lambda n: i["L0_xattn_" + n]
    put("l0_xattn", wq=g("Wq"), wk=g("Wk"), wv=g("Wv"), wo=split(g("Wo")), bo=rep(g("bo")))
    g = lambda n: i["L0_ffn_" + n]
    put("l0_ffn", scale=rep(g("norm_scale")), gw=g("gate_w"), gb=rep(g("gate_b")),
        w1=g("mlp1_w").reshape(8, P, 256, 2).transpose(1, 0, 3, 2), b1=g("mlp1_b").reshape(8, 2, P, 2).transpose(2, 0, 3, 1),
        w2=esplit(g("mlp2_w")), b2=g("mlp2_b"))
    g = lambda n: i["L1_attn_" + n]
    put("l1_attn", wq=g("Wq").T, wk=g("Wk").T, wv=g("Wv").T, wo=g("Wo").T, bq=col(g("bq")), bk=row(g("bk")), bv=rep(g("bv")), bo=rep(g("bo")))
    g = lambda n: i["L1_xattn_" + n]
    put("l1_xattn", wq=g("w_q"), wk=g("w_k"), wv=g("w_v"), wo=g("w_o"), bq=col(g("b_q")), bk=col(g("b_k")), bv=rep(g("b_v")), bo=rep(g("b_o")))
    g = lambda n: i["L1_ffn_" + n]
    put("l1_ffn", gw=np.concatenate([g("router_w"), g("shared_gate_w")], 1), w1=g("w1").transpose(1, 0, 2), w2=g("w2").transpose(1, 0, 2),
        sgu=g("shared_gate_up"), sd=g("shared_down"))
    g = lambda n: i["L2_attn_" + n]
    put("l2_attn", wq=g("Wq"), wk=g("Wk"), wv=g("Wv"), wg=g("Wg"), bg=rep(g("bg")), wo=split(g("Wo")), ln1w=rep(g("ln1_w")), ln1b=rep(g("ln1_b")),
        ln2w=rep(g("ln2_w")), ln2b=rep(g("ln2_b")), fw1=g("W1"), fb1=g("b1").reshape(4, P).T, fw2=split(g("W2")), fb2=rep(g("b2")))
    g = lambda n: i["L2_xattn_" + n]
    put("l2_mix", wq=g("Wq"), wk=g("Wk"), wv=g("Wv"), wf=np.concatenate([g("W_film_in"), g("W_film_out")], 1),
        bf=rep(np.concatenate([g("b_film_in"), g("b_film_out")])), gin=rep(g("g_norm_in")), bin=rep(g("b_norm_in")),
        mg=np.broadcast_to(g("mod_gate").reshape(1, 1), (P, 1)))
    put("s4d", log_dt=col(g("log_dt")), a_re=g("A_re"), a_im=g("A_im"), c_re=g("C_re"), c_im=g("C_im"), dskip=col(g("D_skip")))
    put("l2_ffw", ln2w=rep(g("g_ffn")), ln2b=rep(g("b_ffn")), gout=rep(g("g_norm_out")), bout=rep(g("b_norm_out")),
        fw1=g("W1"), fb1=g("b1").reshape(4, P).T, fw2=split(g("W2")), fb2=rep(g("b2")))
    g = lambda n: i["L2_ffn_" + n]
    put("l2_ffn", gw=g("Wg"), w1=g("W1").transpose(1, 0, 2), b1=g("b1").reshape(8, 4, P).transpose(2, 0, 1), w2=esplit(g("W2")), b2=g("b2"))
    g = lambda n: i["L3_attn_" + n]
    put("l3_attn", wq=g("Wq").T, wk=g("Wk").T, wv=g("Wv").T, bq=col(g("bq")), bk=col(g("bk")), bv=rep(g("bv")))
    g = lambda n: i["L3_xattn_" + n]
    put("l3_xattn", wq=g("Wq").T, wk=g("Wk").T, wv=g("Wv").T, wo=g("Wo").T, bq=col(g("bq")), bk=col(g("bk")), bv=rep(g("bv")), bo=rep(g("bo")))
    g = lambda n: i["L3_ffn_" + n]
    put("l3_ffn", scale=rep(g("scale")), gw=g("centroids").T, w1=g("up_w").transpose(1, 0, 2), w2=esplit(g("down_w")))
    d["x"] = i["x"].transpose(1, 0, 2)
    d["ctxT"] = i["ctx_768"].transpose(2, 0, 1)
    d["vmask"] = np.broadcast_to(i["mask_BxS2_bf1"].view(np.uint8)[None], (P, B_ALL, L))
    d["tmask"] = i["mask_BxS_bf1"].view(np.uint8).T
    return {k: np.ascontiguousarray(a) for k, a in d.items()} | shape_constants()


def shape_constants():
    import numpy as np

    f = np.float32
    p, q = np.arange(P)[:, None], np.arange(P)[None]
    full = lambda v: np.full((P, 1), v, f)
    c = {"c_ident": np.eye(P, dtype=f), "c_ones_row": np.ones((1, P), f), "c_eps5": full(1e-5), "c_eps6": full(1e-6),
         "c_one": full(1), "c_ln2_20": full(20 * np.log(2)),
         "c_headmask": (p // 8 == np.arange(16)[None]).astype(f), "a_blockmask": (p // 8 == q // 8).astype(f),
         "k_times": np.broadcast_to(np.arange(P, dtype=f), (P, P)).copy()}
    c["c_flip"] = np.eye(P, dtype=f)[::-1].copy()
    freq = f(10000.0) ** (np.arange(16, dtype=f) / f(16))
    angle = np.arange(P, dtype=f)[None] / np.concatenate([freq, freq])[:, None]
    sign = np.where(np.arange(32) < 16, -1, 1)[:, None]
    c["a_cos"] = np.tile(np.cos(angle), (4, 1)).astype(f)
    c["a_sin"] = np.tile(np.sin(angle) * sign, (4, 1)).astype(f)
    c["a_causal"] = np.where(np.arange(P + 16)[None] <= p + 16, 0, -1e30).astype(f)
    same = p // 64 == q // 64
    c["a_gla_sum"] = (same & np.where(q < 64, p > q, p <= q)).astype(f)
    c["a_gla_after"] = (same & (p > q)).astype(f)
    upto = p % 64 <= np.arange(64)[None]
    c["a_gla_upto"] = (upto / 64.0).astype(f)
    c["a_gla_tril"] = upto.astype(f)
    return c


def kernel(**inputs):
    import numpy as _np
    import concourse.bacc as _bacc
    from concourse import mybir as _mybir
    from concourse.bass_utils import run_bass_kernel_spmd as _run

    nc = _bacc.Bacc("TRN2", target_bir_lowering=False, num_devices=1)
    arrays, dram = {}, {}
    for name, a in layout({k: _np.asarray(v) for k, v in inputs.items()}).items():
        arrays[f"in_{name}_dram"] = a
        dram[name] = nc.dram_tensor(f"in_{name}_dram", a.shape, _mybir.dt.from_np(a.dtype), kind="ExternalInput").ap()
    out = nc.dram_tensor("out_0_dram", (P, B_ALL, P), F32, kind="ExternalOutput").ap()
    decoder(nc, dram, out)
    r = _run(nc, [arrays], core_ids=[0])
    return r.results[0]["out_0_dram"].transpose(1, 0, 2)
```
